# Optimizing a Trainium2 kernel written in Bass

```python
import numpy as np
import jax
import jax.numpy as jnp

def _softmax(x, axis=-1):
    return jax.nn.softmax(x, axis=axis)

def _gelu(x):
    return jax.nn.gelu(x, approximate=True)

def _silu(x):
    return jax.nn.silu(x)

def _sigmoid(x):
    return jax.nn.sigmoid(x)

def _layernorm(x, axis=-1, eps=1e-05):
    m = jnp.mean(x, axis=axis, keepdims=True)
    v = jnp.var(x, axis=axis, keepdims=True)
    return (x - m) / jnp.sqrt(v + eps)

def _scatter_add(tgt, idx, src, axis=0):
    return tgt.at[idx].add(src)

def _segment_sum(src, seg, n):
    return jax.ops.segment_sum(src, seg, n)
kernel_name = 'mk_flamingo_gated_d1_seqx_r4_713eea'

def setup_inputs(seed: int=0):
    np.random.seed(seed)
    _w = jnp.asarray

    def _rec_inputs():
        import jax
        import jax.numpy as jnp
        _rk = jax.random.key(seed)
        x = 7.22e-05 + 1 * jax.random.normal(jax.random.fold_in(_rk, 1), (16, 128, 256), jnp.float32)
        _lenS = 128 - jax.random.randint(jax.random.fold_in(_rk, 7), (16,), 0, max(1, 128 // 4) + 1, jnp.int32)
        _lenS2 = 128 - jax.random.randint(jax.random.fold_in(_rk, 8), (16,), 0, max(1, 128 // 4) + 1, jnp.int32)
        _ctx_1024P = jax.random.normal(jax.random.fold_in(_rk, 11), (16, 16, 256), jnp.float32)
        _ctx_1024c = jax.random.dirichlet(jax.random.fold_in(_rk, 511), 0.3 * jnp.ones((16,), jnp.float32), (16, 128))
        _ctx_1024t = jnp.einsum('bsk,bkd->bsd', _ctx_1024c, _ctx_1024P)
        _ctx_1024t = _ctx_1024t * jax.lax.rsqrt(jnp.mean(jnp.square(_ctx_1024t)) + 1e-12) * 0.953939
        ctx_1024 = -1.39393e-06 + 0.999914 * (_ctx_1024t + 0.3 * jax.random.normal(jax.random.fold_in(_rk, 611), (16, 128, 256), jnp.float32))
        _g = jax.random.normal(jax.random.fold_in(_rk, 9001), (2, 1), jnp.float32)
        _g = jnp.sign(_g) * jnp.maximum(jnp.abs(_g), 1.0) + (_g == 0) * 1.0
        g_xattn = _g[0]
        g_ffn = _g[1]
        return (x, ctx_1024, g_xattn, g_ffn)
    x, ctx_1024, g_xattn, g_ffn = _rec_inputs()

    def _L0_xattn_setup():
        import jax, jax.numpy as jnp
        import numpy as np
        DIM = 256
        CTX_DIM = 256
        HEADS = 16
        DIM_HEAD = 64
        INNER = HEADS * DIM_HEAD
        FF_INNER = 4 * DIM
        EPS = 1e-05

        def layer_norm(x, g, b):
            mu = jnp.mean(x, axis=-1, keepdims=True)
            var = jnp.var(x, axis=-1, keepdims=True)
            return (x - mu) * jax.lax.rsqrt(var + EPS) * g + b
        key = jax.random.key(seed)
        ks = jax.random.split(key, 9)
        b, n, j = (4, 512, 256)
        inp = {'x': jax.random.normal(ks[0], (b, n, DIM), dtype=jnp.float32), 'context': jax.random.normal(ks[1], (b, j, CTX_DIM), dtype=jnp.float32), 'ln_g': jnp.ones((DIM,), jnp.float32), 'ln_b': jnp.zeros((DIM,), jnp.float32), 'cln_g': jnp.ones((CTX_DIM,), jnp.float32), 'cln_b': jnp.zeros((CTX_DIM,), jnp.float32), 'Wq': jax.random.normal(ks[2], (DIM, INNER), dtype=jnp.float32) * DIM ** (-0.5), 'Wkv': jax.random.normal(ks[3], (CTX_DIM, 2 * DIM_HEAD), dtype=jnp.float32) * CTX_DIM ** (-0.5), 'Wo': jax.random.normal(ks[4], (INNER, DIM), dtype=jnp.float32) * INNER ** (-0.5), 'Wff1': jax.random.normal(ks[5], (DIM, 2 * FF_INNER), dtype=jnp.float32) * DIM ** (-0.5), 'Wff2': jax.random.normal(ks[6], (FF_INNER, DIM), dtype=jnp.float32) * FF_INNER ** (-0.5)}
        return inp
    _L0_xattn_all = _L0_xattn_setup()
    _L0_xattn_in = {k: v for k, v in _L0_xattn_all.items() if k in ('ln_g', 'ln_b', 'cln_g', 'cln_b', 'Wq', 'Wkv', 'Wo', 'Wff1', 'Wff2')}
    del _L0_xattn_all

    def _L0_ffn_setup():
        import jax, jax.numpy as jnp
        import numpy as np
        D_MODEL = 256
        HIDDEN = 256
        NUM_EXPERTS = 8
        TOP_K = 2
        key = jax.random.key(seed)
        ks = jax.random.split(key, 10)
        s = 0.02
        return {'x': jax.random.normal(ks[0], (2, 512, D_MODEL), dtype=jnp.float32), 'gate_w': jax.random.normal(ks[1], (NUM_EXPERTS, D_MODEL), dtype=jnp.float32) * s, 'up_w': jax.random.normal(ks[2], (NUM_EXPERTS, D_MODEL, HIDDEN), dtype=jnp.float32) * s, 'up_b': jnp.zeros((NUM_EXPERTS, HIDDEN), dtype=jnp.float32), 'down_w': jax.random.normal(ks[3], (NUM_EXPERTS, HIDDEN, D_MODEL), dtype=jnp.float32) * s, 'down_b': jnp.zeros((NUM_EXPERTS, D_MODEL), dtype=jnp.float32), 'sh_up_w': jax.random.normal(ks[4], (D_MODEL, HIDDEN), dtype=jnp.float32) * s, 'sh_up_b': jnp.zeros((HIDDEN,), dtype=jnp.float32), 'sh_down_w': jax.random.normal(ks[5], (HIDDEN, D_MODEL), dtype=jnp.float32) * s, 'sh_down_b': jnp.zeros((D_MODEL,), dtype=jnp.float32)}
    _L0_ffn_all = _L0_ffn_setup()
    _L0_ffn_in = {k: v for k, v in _L0_ffn_all.items() if k in ('gate_w', 'up_w', 'up_b', 'down_w', 'down_b', 'sh_up_w', 'sh_up_b', 'sh_down_w', 'sh_down_b')}
    del _L0_ffn_all
    return {'x': x, 'ctx_1024': ctx_1024, 'g_xattn': g_xattn, 'g_ffn': g_ffn, 'L0_xattn_ln_g': _L0_xattn_in['ln_g'], 'L0_xattn_ln_b': _L0_xattn_in['ln_b'], 'L0_xattn_cln_g': _L0_xattn_in['cln_g'], 'L0_xattn_cln_b': _L0_xattn_in['cln_b'], 'L0_xattn_Wq': _L0_xattn_in['Wq'], 'L0_xattn_Wkv': _L0_xattn_in['Wkv'], 'L0_xattn_Wo': _L0_xattn_in['Wo'], 'L0_xattn_Wff1': _L0_xattn_in['Wff1'], 'L0_xattn_Wff2': _L0_xattn_in['Wff2'], 'L0_ffn_gate_w': _L0_ffn_in['gate_w'], 'L0_ffn_up_w': _L0_ffn_in['up_w'], 'L0_ffn_up_b': _L0_ffn_in['up_b'], 'L0_ffn_down_w': _L0_ffn_in['down_w'], 'L0_ffn_down_b': _L0_ffn_in['down_b'], 'L0_ffn_sh_up_w': _L0_ffn_in['sh_up_w'], 'L0_ffn_sh_up_b': _L0_ffn_in['sh_up_b'], 'L0_ffn_sh_down_w': _L0_ffn_in['sh_down_w'], 'L0_ffn_sh_down_b': _L0_ffn_in['sh_down_b']}

def reference(x, ctx_1024, g_xattn, g_ffn, L0_xattn_ln_g, L0_xattn_ln_b, L0_xattn_cln_g, L0_xattn_cln_b, L0_xattn_Wq, L0_xattn_Wkv, L0_xattn_Wo, L0_xattn_Wff1, L0_xattn_Wff2, L0_ffn_gate_w, L0_ffn_up_w, L0_ffn_up_b, L0_ffn_down_w, L0_ffn_down_b, L0_ffn_sh_up_w, L0_ffn_sh_up_b, L0_ffn_sh_down_w, L0_ffn_sh_down_b):
    import jax
    import jax.numpy as jnp

    def _L0_xattn_ref(x, context, ln_g, ln_b, cln_g, cln_b, Wq, Wkv, Wo, Wff1, Wff2):
        import jax, jax.numpy as jnp
        import numpy as np
        DIM = 256
        CTX_DIM = 256
        HEADS = 16
        DIM_HEAD = 64
        INNER = HEADS * DIM_HEAD
        FF_INNER = 4 * DIM
        EPS = 1e-05

        def layer_norm(x, g, b):
            mu = jnp.mean(x, axis=-1, keepdims=True)
            var = jnp.var(x, axis=-1, keepdims=True)
            return (x - mu) * jax.lax.rsqrt(var + EPS) * g + b
        scale = DIM_HEAD ** (-0.5)
        xn = layer_norm(x, ln_g, ln_b)
        cn = layer_norm(context, cln_g, cln_b)
        b, n, _ = xn.shape
        q = (xn @ Wq).reshape(b, n, HEADS, DIM_HEAD).transpose(0, 2, 1, 3) * scale
        kv = cn @ Wkv
        k, v = (kv[..., :DIM_HEAD], kv[..., DIM_HEAD:])
        sim = jnp.einsum('bhid,bjd->bhij', q, k)
        attn = jax.nn.softmax(sim, axis=-1)
        out = jnp.einsum('bhij,bjd->bhid', attn, v)
        out = out.transpose(0, 2, 1, 3).reshape(b, n, INNER) @ Wo
        ff = xn @ Wff1
        h, gate = (ff[..., :FF_INNER], ff[..., FF_INNER:])
        out = out + jax.nn.silu(gate) * h @ Wff2
        return out

    def _L0_ffn_ref(x, gate_w, up_w, up_b, down_w, down_b, sh_up_w, sh_up_b, sh_down_w, sh_down_b):
        import jax, jax.numpy as jnp
        import numpy as np
        D_MODEL = 256
        HIDDEN = 256
        NUM_EXPERTS = 8
        TOP_K = 2
        b, s, d = x.shape
        xf = x.reshape(-1, d)
        shared = jax.nn.silu(x @ sh_up_w + sh_up_b) @ sh_down_w + sh_down_b
        logits = xf @ gate_w.T
        scores = jax.nn.softmax(logits, axis=-1)
        topk_w, topk_i = jax.lax.top_k(scores, TOP_K)
        topk_w = topk_w / (topk_w.sum(axis=-1, keepdims=True) + 1e-20)
        comb = (jax.nn.one_hot(topk_i, NUM_EXPERTS, dtype=xf.dtype) * topk_w[..., None]).sum(axis=1)
        h = jnp.einsum('nd,edh->neh', xf, up_w) + up_b
        h = jax.nn.silu(h)
        ye = jnp.einsum('neh,ehd->ned', h, down_w) + down_b
        y = jnp.einsum('ned,ne->nd', ye, comb).reshape(b, s, d)
        return y + shared
    x = x + jnp.tanh(g_xattn[0]) * _L0_xattn_ref(_layernorm(x, axis=-1), ctx_1024, L0_xattn_ln_g, L0_xattn_ln_b, L0_xattn_cln_g, L0_xattn_cln_b, L0_xattn_Wq, L0_xattn_Wkv, L0_xattn_Wo, L0_xattn_Wff1, L0_xattn_Wff2)
    x = x + jnp.tanh(g_ffn[0]) * _L0_ffn_ref(_layernorm(x, axis=-1), L0_ffn_gate_w, L0_ffn_up_w, L0_ffn_up_b, L0_ffn_down_w, L0_ffn_down_b, L0_ffn_sh_up_w, L0_ffn_sh_up_b, L0_ffn_sh_down_w, L0_ffn_sh_down_b)
    return x

_drawn_inputs = setup_inputs


def setup_inputs(seed=0):
    import zlib

    import numpy as np

    out = dict(_drawn_inputs(seed))
    spreads = {'L0_xattn_ln_g': (1.0, 0.2),
     'L0_xattn_ln_b': (0.0, 0.1),
     'L0_xattn_cln_g': (1.0, 0.2),
     'L0_xattn_cln_b': (0.0, 0.1),
     'L0_ffn_up_b': (0.0, 0.8),
     'L0_ffn_down_b': (0.0, 0.1),
     'L0_ffn_sh_up_b': (0.0, 0.602),
     'L0_ffn_sh_down_b': (0.0, 0.1)}
    factors = {}
    for name, (base, spread) in spreads.items():
        noise = np.random.default_rng([zlib.crc32(name.encode()), seed]).standard_normal(out[name].shape)
        drawn = base * np.exp(spread * noise) if base else spread * noise
        out[name] = jnp.asarray(drawn.astype(out[name].dtype))
    for name, factor in factors.items():
        out[name] = (out[name] * factor).astype(out[name].dtype)
    return out
```

```python
from contextlib import ExitStack

import numpy as np

import concourse.bass as bass
from concourse import mybir

F32 = mybir.dt.float32
F32R = mybir.dt.float32r
I32 = mybir.dt.int32
ALU = mybir.AluOpType
ACT = mybir.ActivationFunctionType
AX = mybir.AxisListType

P = 128
NB, D = 16, 256
H, DH = 16, 64
FF = 1024
NE, HID = 8, 256
KT = D // P
NG = NB // 2
GT = 2 * P
NU = 8
NFF = FF // P
EPS = 1e-5
NEWTON = 3
LN_STEPS = 5 + 2 + 3 * NEWTON
RSQRT_GUESS = 0x5F3759DF
WO_T = H * DH // P

NEXT = ["K", "V", "QP0", "QP1"]
MIX_PRO = ["TXc", "TXx"] + NEXT
MIX_MID = ["QP2", "FF0", "FF1", "QP3", "FF2", "X1T", "FF3", "GL", "FF4", "FF5", "TXc", "FF6", "FF7",
           "TXx"] + NEXT
MIX_FIRST = [n for n in MIX_MID if n not in ("X1T", "GL")]
MIX_LAST = [n for n in MIX_MID if n not in ["TXc", "TXx"] + NEXT]


def mix_index(name, g, first, last):
    if g is None:
        return MIX_PRO.index(name)
    if first:
        return len(MIX_PRO) + MIX_FIRST.index(name)
    base = len(MIX_PRO) + len(MIX_FIRST) - len(MIX_MID)
    return g * len(MIX_MID) + (base + (MIX_LAST if last else MIX_MID).index(name))


def ln_base(call):
    return call * LN_STEPS


def mix_bank(name, g, first, last):
    if g is None or first:
        return mix_index(name, g, first, last) % 3
    return (len(MIX_PRO) + len(MIX_FIRST) + (MIX_LAST if last else MIX_MID).index(name)) % 3


CHUNKS_A = ["wkv", "wq0", "wq1", "ff1_0", "ff2_0", "wo_0", "ff1_1", "ff1_2", "ff2_1", "wo_1", "ff1_3"]
EARLY = 4
CHUNK_SLOT = {0: [4, 5], 1: [6], 3: [7], 4: [8, 9], 5: [10]}
NCA = len(CHUNKS_A)
NPOS = NE + 1
STEPS = 4
ST = 4 * P
NSTEP = NPOS * STEPS
TPS = ST // P

USE_X1T, USE_GL, USE_LT = 2, 5, 8
USE_CT = 2 * (NSTEP - 1) + 3
USE_BIAS = USE_CT + 4
USE_END = USE_BIAS + NB // 2


def down_use(step):
    if isinstance(step, int):
        return {0: 0, 1: 3, 2: 6, NSTEP - 1: USE_END}.get(step, 2 * step + 3)
    return step * 2 + 3


def program(nc, x, ctx_in, g_xattn, g_ffn, ln_g, ln_b, cln_g, cln_b, Wq, Wkv, Wo, Wff1, Wff2,
            gate_w, up_w, up_b, down_w, down_b, sh_up_w, sh_up_b, sh_down_w, sh_down_b, out):
    stack = ExitStack()
    with stack:
        def sb(name, shape, dt=F32):
            return stack.enter_context(nc.sbuf_tensor(name, shape, dt))

        def sem(name):
            return stack.enter_context(nc.semaphore(name))

        wq_t = sb("wq_t", [P, 4, H * DH], F32R)
        wq = [wq_t[:, 0:2, :], wq_t[:, 2:4, :]]
        wkk = [sb("wkk_h", [P, KT, P], F32R), sb("wkk_l", [P, KT, P], F32R)]
        wv = [sb("wv_h", [P, KT, P], F32R), sb("wv_l", [P, KT, P], F32R)]
        wo = [sb("wo_h", [P, WO_T, D], F32R), sb("wo_l", [P, WO_T, D], F32R)]
        wf1_t = sb("wf1_t", [P, 2, KT, 2 * FF], F32R)
        wf1 = [wf1_t[:, 0], wf1_t[:, 1]]
        wf2 = [sb("wf2_h", [P, NFF, D], F32R), sb("wf2_l", [P, NFF, D], F32R)]
        gw = [sb("gw_h", [P, KT, P], F32R), sb("gw_l", [P, KT, P], F32R)]
        stage = sb("stage", [P, 2, 1024])
        ident = sb("ident", [P, P])
        NROW = 4 + NE + 1 + NE
        all_rows = sb("all_rows", [32 + NE + 1, D])
        rows, dbrow = all_rows[0:NROW, :], all_rows[32:32 + NE + 1, :]
        cols = sb("cols", [P, KT, NROW])
        gates_in = sb("gates_in", [P, 2])
        gates = sb("gates", [P, 2])
        xs = sb("xs", [P, NB, D])
        ct = sb("ct", [P, 2, D])
        xn = sb("xn", [P, 4, D])
        tf = sb("tf", [P, KT, GT])
        xnT = [sb("xnT_h", [P, KT, GT], F32R), sb("xnT_l", [P, KT, GT], F32R)]
        cnT = [sb("cnT_h", [P, KT, GT], F32R), sb("cnT_l", [P, KT, GT], F32R)]
        q_t = sb("q_t", [P, 2, H // 2, GT], F32R)
        q = [q_t[:, 0], q_t[:, 1]]
        kz = [sb("kz_h", [P, 2, 2, P], F32R), sb("kz_l", [P, 2, 2, P], F32R)]
        vv = [sb("vv_h", [P, 2, P], F32R), sb("vv_l", [P, 2, P], F32R)]
        pr = sb("pr", [P, 2, 4, P])
        pT = [sb("pT_h", [P, 4 * P], F32R), sb("pT_l", [P, 4 * P], F32R)]
        oT = [sb("oT_h", [P, 2, P], F32R), sb("oT_l", [P, 2, P], F32R)]
        nmax = sb("nmax", [P, 2, 4])
        den = sb("den", [P, 2, 4])
        rden = sb("rden", [P, 2, 4])
        th = sb("th", [P, GT])
        u1 = sb("u1", [P, GT])
        uf = sb("uf", [P, GT])
        uT = [sb("uT_h", [P, 2, GT], F32R), sb("uT_l", [P, 2, GT], F32R)]
        bn = sb("bn", [P, 2, 6])
        mean = sb("mean", [P, 2])
        var = sb("var", [P, 2])
        rt = sb("rt", [P, 2])
        ry = sb("ry", [P, 2])
        xmT = [sb("xmT_h", [P, KT, NB * P], F32R), sb("xmT_l", [P, KT, NB * P], F32R)]
        lgT = sb("lgT", [NE, NB * P])
        rio = sb("rio", [P, NB, NE])
        bias = sb("bias", [P, KT, 1])
        g1 = sb("g1", [P, NB])
        g2 = sb("g2", [P, NB])
        g3 = sb("g3", [P, NB])
        lg, ga = [t.rearrange("p (t e) -> p t e", t=NB) for t in (th[:, 0:P], th[:, P:2 * P])]
        gb, oh1 = [t.rearrange("p (t e) -> p t e", t=NB) for t in (u1[:, 0:P], u1[:, P:2 * P])]
        comb = uf[:, 0:NPOS * NB].rearrange("p (c t) -> p c t", c=NPOS)
        ring = wq_t.rearrange("p a n -> p (a n)").rearrange("p (s m k n) -> p s m k n", s=2, m=4, k=KT)
        hh = q_t.rearrange("p a m n -> p (a m n)").rearrange("p (s a m n) -> p s a m n", s=2, a=2, m=KT)
        hf = xn.rearrange("p a n -> p (a n)").rearrange("p (m n) -> p m n", m=KT)
        cf = wf1_t.rearrange("p a k n -> p (a k n)")
        cT = [cf[:, 0:2048], cf[:, 2048:4096]]
        db = [cf[:, 4096:4096 + D], cf[:, 4096 + D:4096 + 2 * D]]

        bank = [stack.enter_context(nc.psum_tensor(f"bank{i}", [P, 512], F32)) for i in range(8)]
        sc_ps, t_ps, pv_ps, out_ps, mix_ps = bank[0:2], bank[2], bank[3], bank[4], bank[5:8]
        up_ps, dn_ps = bank[0:4], bank[4:8]

        rows_in = sem("rows_in")
        gates_loaded = sem("gates_loaded")
        dbrow_in = sem("dbrow_in")
        x_in = [sem(f"x_in{g}") for g in range(NG)]
        ctx_loaded = sem("ctx_loaded")
        stage_full = [sem("stage_full0"), sem("stage_full1")]
        stage_hi = sem("stage_hi")
        w_ready = sem("w_ready")
        ident_done = sem("ident_done")
        rio_done = sem("rio_done")
        zeros_done = sem("zeros_done")
        cols_filled = sem("cols_filled")
        cols_done = sem("cols_done")
        gw_done = sem("gw_done")
        gates_done = sem("gates_done")
        mix_filled = sem("mix_filled")
        mix_freed = sem("mix_freed")
        ln_step = sem("ln_step")
        xnorm_done = sem("xnorm_done")
        cnorm_done = sem("cnorm_done")
        x1norm_done = sem("x1norm_done")
        tfh_done = sem("tfh_done")
        cnT_ready = sem("cnT_ready")
        xnT_ready = sem("xnT_ready")
        kh_done = sem("kh_done")
        vh_done = sem("vh_done")
        qh_done = sem("qh_done")
        scores_filled = sem("scores_filled")
        nmax_done = sem("nmax_done")
        exp_done = sem("exp_done")
        rden_done = sem("rden_done")
        probs_ready = sem("probs_ready")
        pT_filled = sem("pT_filled")
        pTh_done = sem("pTh_done")
        pT_ready = sem("pT_ready")
        pv_filled = sem("pv_filled")
        oh_done = sem("oh_done")
        o_ready = sem("o_ready")
        wo_done = sem("wo_done")
        tanh_done = sem("tanh_done")
        u1_done = sem("u1_done")
        uh_done = sem("uh_done")
        u_ready = sem("u_ready")
        ff2_done = sem("ff2_done")
        x1_done = sem("x1_done")
        xmh_done = sem("xmh_done")
        gate_step = sem("gate_step")
        gexp_done = sem("gexp_done")
        bias_done = sem("bias_done")
        comb_done = sem("comb_done")
        db_done = sem("db_done")
        cth_done = sem("cth_done")
        up_filled = sem("up_filled")
        silu_done = sem("silu_done")
        hh_done = sem("hh_done")
        h_ready = sem("h_ready")
        dn_filled = sem("dn_filled")
        dn_freed = sem("dn_freed")
        written = sem("written")

        block = stack.enter_context(nc.Block())

        def chunk_split(n):
            c, src = CHUNKS_A[n], stage[:, n % 2, :]
            i = int(c[-1])
            if c.startswith("wq"):
                return src, wq[0][:, i, :], wq[1][:, i, :]
            if c.startswith("ff1"):
                w = [t.rearrange("p k (h n) -> p (k h) n", h=2)[:, :, 256 * i:256 * i + 256] for t in wf1]
                return src.rearrange("p (k n) -> p k n", k=4), w[0], w[1]
            w = [t[:, 4 * i:4 * i + 4, :] for t in (wf2 if c.startswith("ff2") else wo)]
            return src.rearrange("p (k n) -> p k n", k=4), w[0], w[1]

        def chunk_loads(n):
            s = stage[:, n % 2, :]
            if n >= NCA:
                c = n - NCA
                s = s.rearrange("p (m k n) -> p m k n", m=2, k=KT)
                pair = (sh_up_w, sh_down_w) if c == 0 else (up_w[c - 1], down_w[c - 1])
                return [(s[:, m], w.rearrange("(k p) n -> p k n", p=P)) for m, w in enumerate(pair)]
            name = CHUNKS_A[n]
            if name == "wkv":
                return [(s[:, 0:KT * P].rearrange("p (k n) -> p k n", k=KT), Wkv.rearrange("(k p) n -> p k n", p=P))]
            i = int(name[-1])
            if name.startswith("wq"):
                return [(s, Wq[i * P:(i + 1) * P, :])]
            if name.startswith("ff1"):
                src = Wff1.rearrange("(k p) (h n) -> p k h n", p=P, h=2)[:, :, :, 256 * i:256 * i + 256]
                dst = s.rearrange("p (k h n) -> p k h n", k=KT, h=2)
                return [(dst[:, k], src[:, k]) for k in range(KT)]
            w = Wff2 if name.startswith("ff2") else Wo
            return [(s.rearrange("p (k n) -> p k n", k=4), w.rearrange("(k p) n -> p k n", p=P)[:, 4 * i:4 * i + 4, :])]

        def stage_value(n):
            return 16 * sum(len(chunk_loads(m)) for m in range(n % 2, n + 1, 2))

        def halves(bank_ap, two):
            return bank_ap[:, :].rearrange("p (a n) -> p a n", a=two)

        @block.sync
        def _(sp):
            def load_x(g):
                sp.dma_start(xs[:, 2 * g:2 * g + 2, :], x[2 * g:2 * g + 2].rearrange("b p d -> p b d")
                             ).then_inc(x_in[g], 16)

            def load_ctx(g):
                if g > 0:
                    sp.wait_ge(cnorm_done, g)
                sp.dma_start(ct[:, :, :], ctx_in[2 * g:2 * g + 2].rearrange("b p d -> p b d")
                             ).then_inc(ctx_loaded, 16)

            def load_chunk(n):
                if n >= 2:
                    sp.wait_ge(w_ready, n - 1)
                for dst, src in chunk_loads(n):
                    sp.dma_start(dst, src).then_inc(stage_full[n % 2], 16)

            load_ctx(0)
            load_x(0)
            for n in range(NCA):
                load_chunk(n)
                if n == EARLY:
                    load_x(1)
                    load_ctx(1)
            for g in range(2, NG):
                load_x(g)
            for g in range(2, NG):
                load_ctx(g)
            for c in range(NPOS):
                load_chunk(NCA + c)
            for s in range(STEPS):
                sp.wait_ge(dn_freed, USE_BIAS + 2 * s + 2 if s < STEPS - 1 else USE_END + 2)
                sp.dma_start(out[TPS * s:TPS * (s + 1)].rearrange("b p d -> p b d"), xs[:, TPS * s:TPS * (s + 1), :]
                             ).then_inc(written, 16)
            sp.wait_ge(written, 16 * STEPS)

        @block.gpsimd
        def _(pool):
            pool.memset(ident[:, :], 0.0).then_inc(ident_done, 1)
            pool.wait_ge(ident_done, 1)
            pool.affine_select(out=ident[:, :], in_=ident[:, :], compare_op=ALU.not_equal, fill=1.0, base=0,
                               pattern=[[-1, P]], channel_multiplier=1).then_inc(ident_done, 1)

            def row(dst, v):
                return pool.dma_start(dst, v.rearrange("(a n) -> a n", a=1))

            for i, v in enumerate((ln_g, ln_b, cln_g, cln_b, sh_up_b)):
                row(rows[i:i + 1, :], v).then_inc(rows_in, 16)
            pool.dma_start(rows[5:5 + NE, :], up_b).then_inc(rows_in, 16)
            pool.dma_start(rows[5 + NE:NROW, :], gate_w).then_inc(rows_in, 16)
            for i, v in enumerate((g_xattn, g_ffn)):
                pool.dma_start(gates_in[:, i:i + 1], v.rearrange("(a n) -> a n", a=1).broadcast_to((P, 1))
                               ).then_inc(gates_loaded, 16)
            row(dbrow[0:1, :], sh_down_b).then_inc(dbrow_in, 16)
            pool.dma_start(dbrow[1:NPOS, :], down_b).then_inc(dbrow_in, 16)
            for e in range(NE):
                last = pool.memset(rio[:, :, e:e + 1], float(NE - e))
            last.then_inc(rio_done, 1)

            def split_lo(n):
                src, hi, lo = chunk_split(n)
                pool.wait_ge(stage_hi, n + 1)
                pool.tensor_tensor(lo, src, hi.bitcast(F32), ALU.subtract).then_inc(w_ready, 1)

            def iteration(g, first=False, last=False):
                for s in range(NU):
                    u = g * NU + s
                    pool.wait_ge(rden_done, u + 1)
                    pool.tensor_tensor(pr[:, s % 2], pr[:, s % 2],
                                       rden[:, s % 2, :].unsqueeze(2).broadcast_to((P, 4, P)),
                                       ALU.mult).then_inc(probs_ready, 1)
                    pool.wait_ge(uh_done, u + 1)
                    pool.tensor_tensor(uT[1][:, s % 2, :], uf[:, :], uT[0][:, s % 2, :].bitcast(F32),
                                       ALU.subtract).then_inc(u_ready, 1)
                    if first:
                        for n in CHUNK_SLOT.get(s, []):
                            split_lo(n)

            iteration(0, first=True)
            with pool.Fori(1, NG - 1) as g:
                iteration(g)
            iteration(NG - 1, last=True)

            for c in range(NPOS):
                n = NCA + c
                half = ring[:, c % 2]
                src = stage[:, n % 2, :].rearrange("p (m k n) -> p m k n", m=2, k=KT)
                if c == 0:
                    pool.wait_ge(mix_filled, mix_index("QP3", NG - 1, False, True) + 1)
                if c >= 2:
                    pool.wait_ge(dn_filled, down_use(STEPS * (c - 1) - 1) + 2)
                pool.wait_ge(stage_full[n % 2], stage_value(n))
                for m in range(2):
                    pool.tensor_scalar(half[:, 2 * m], src[:, m], 1.0, None, ALU.mult).then_inc(stage_hi, 1)
                pool.wait_ge(stage_hi, NCA + 2 * c + 2)
                for m in range(2):
                    done = pool.tensor_tensor(half[:, 2 * m + 1], src[:, m], half[:, 2 * m].bitcast(F32), ALU.subtract)
                done.then_inc(w_ready, 1)

        @block.scalar
        def _(act):
            act.wait_ge(gates_loaded, 32)
            act.activation(gates[:, :], gates_in[:, :], ACT.Tanh).then_inc(gates_done, 1)

            def transposed_hi(name, g, first, last, dst, count):
                act.wait_ge(mix_freed, mix_index(name, g, first, last) + 1)
                act.activation(dst[:, :, :], tf[:, :, :], ACT.Copy).then_inc(tfh_done, 1)

            def keys_values_hi(g, first, last):
                b = mix_ps[mix_bank("K", g, first, last)]
                act.wait_ge(mix_filled, mix_index("K", g, first, last) + 1)
                for a in range(2):
                    r = slice(DH * a, DH * a + DH)
                    done = act.activation(kz[0][r, :, a, :], b[r, 0:GT].rearrange("p (b n) -> p b n", b=2),
                                          ACT.Copy, scale=DH ** -0.5)
                done.then_inc(kh_done, 1)
                b = mix_ps[mix_bank("V", g, first, last)]
                act.wait_ge(mix_filled, mix_index("V", g, first, last) + 1)
                act.activation(vv[0][:, :, :], halves(b, 2)[:, :, 0:P], ACT.Copy).then_inc(vh_done, 1)

            def queries_hi(pair, g, first, last):
                b = mix_ps[mix_bank(f"QP{pair}", g, first, last)]
                act.wait_ge(mix_filled, mix_index(f"QP{pair}", g, first, last) + 1)
                act.activation(q[0][:, 2 * pair:2 * pair + 2, :], halves(b, 2), ACT.Copy).then_inc(qh_done, 1)

            def attended_hi(u, very_first):
                act.wait_ge(pv_filled, u + 1)
                if not very_first:
                    act.wait_ge(wo_done, u)
                v = pv_ps[:, :].rearrange("p (m a n) -> p m a n", m=2, a=2)
                for a in range(2):
                    r = slice(DH * a, DH * a + DH)
                    done = act.activation(oT[0][r, :, :], v[r, :, a, :], ACT.Copy)
                done.then_inc(oh_done, 1)

            def probs_hi(u, very_first):
                act.wait_ge(pT_filled, u + 1)
                if not very_first:
                    act.wait_ge(pv_filled, u)
                act.activation(pT[0][:, :], t_ps[:, :], ACT.Copy).then_inc(pTh_done, 1)

            def iteration(g, first=False, last=False):
                for s in range(NU + 2):
                    u = g * NU + s
                    if s >= 2:
                        attended_hi(u - 2, first and s == 2)
                    if s < NU:
                        act.wait_ge(nmax_done, u + 1)
                        if not (first and s < 2):
                            act.wait_ge(pT_filled, u - 1)
                        for h in range(4):
                            done = act.activation(pr[:, s % 2, h, :], sc_ps[s % 2][:, h * P:(h + 1) * P], ACT.Exp,
                                                  bias=nmax[:, s % 2, h:h + 1], accum_out=den[:, s % 2, h:h + 1])
                        done.then_inc(exp_done, 1)
                    if s == 0:
                        queries_hi(2, g, first, last)
                    if s == 2:
                        queries_hi(3, g, first, last)
                    if s == 6 and not last:
                        transposed_hi("TXc", g, first, last, cnT[0], 0)
                    if s < NU:
                        b = mix_ps[mix_bank(f"FF{s}", g, first, last)]
                        act.wait_ge(mix_filled, mix_index(f"FF{s}", g, first, last) + 1)
                        if not (first and s == 0):
                            act.wait_ge(u1_done, u)
                        act.activation(th[:, :], b[:, GT:2 * GT], ACT.Tanh, scale=0.5).then_inc(tanh_done, 1)
                    if 1 <= s <= NU:
                        probs_hi(u - 1, first and s == 1)
                    if s < NU:
                        act.wait_ge(mix_freed, mix_index(f"FF{s}", g, first, last) + 1)
                        if not (first and s < 2):
                            act.wait_ge(ff2_done, u - 1)
                        act.activation(uT[0][:, s % 2, :], uf[:, :], ACT.Copy).then_inc(uh_done, 1)
                    if s == NU and not last:
                        transposed_hi("TXx", g, first, last, xnT[0], 0)
                        keys_values_hi(g, first, last)
                if not last:
                    queries_hi(0, g, first, last)
                    queries_hi(1, g, first, last)

            transposed_hi("TXc", None, False, False, cnT[0], 0)
            transposed_hi("TXx", None, False, False, xnT[0], 0)
            keys_values_hi(None, False, False)
            queries_hi(0, None, False, False)
            queries_hi(1, None, False, False)
            iteration(0, first=True)
            with act.Fori(1, NG - 1) as g:
                iteration(g)
            iteration(NG - 1, last=True)

            def up_bias(pos):
                act.activation(bias[:, :, :], cols[:, :, bass.ds(pos + 4, 1)], ACT.Copy).then_inc(bias_done, 1)

            def hidden_hi(step, parity, pos, early=None):
                act.wait_ge(bias_done, pos + 1)
                for m in range(KT):
                    act.wait_ge(up_filled, KT * step + m + 1)
                    if early != 0:
                        act.wait_ge(h_ready, KT * step + (m - KT + 1))
                    act.activation(hf[:, m, :], up_ps[2 * parity + m][:, :], ACT.Silu,
                                   bias=bias[:, m, :]).then_inc(silu_done, 1)
                    act.wait_ge(silu_done, KT * step + m + 1)
                    if m == 0 and early not in (0, 1):
                        act.wait_ge(dn_filled, (down_use(step - 2) if early else step * 2 - 1) + 2)
                    act.activation(hh[:, parity, 0, m, :], hf[:, m, :], ACT.Copy).then_inc(hh_done, 1)

            act.wait_ge(cols_done, 1)
            up_bias(0)
            hidden_hi(0, 0, 0, 0)
            hidden_hi(1, 1, 0, 1)
            hidden_hi(2, 0, 0, 2)
            hidden_hi(3, 1, 0, 3)
            act.wait_ge(gate_step, GATE_SHIFTED)
            act.activation(ga[:, :, :], gb[:, :, :], ACT.Exp).then_inc(gexp_done, 1)
            with act.Fori(0, NE // 2) as i:
                for j in range(2 * STEPS):
                    if j % STEPS == 0:
                        up_bias(i * 2 + (1 + j // STEPS))
                    hidden_hi(i * (2 * STEPS) + (STEPS + j), j % 2, i * 2 + (1 + j // STEPS))
            for k in range(4):
                act.wait_ge(dn_filled, USE_CT + k + 1)
                act.activation(cT[0][0:NPOS, k * 512:(k + 1) * 512], dn_ps[(USE_CT + k) % 4][0:NPOS, :],
                               ACT.Copy).then_inc(cth_done, 1)

        @block.vector
        def _(dve):
            def normalise(tiles, dst, double, call, done, after=None):
                if after:
                    dve.wait_ge(*after)
                base, k = ln_base(call), 0

                def link(ins):
                    nonlocal k
                    k += 1
                    ins.then_inc(ln_step, 1)
                    dve.wait_ge(ln_step, base + k)

                for i, t in enumerate(tiles):
                    last = dve.bn_stats(bn[:, i, :], t)
                link(last)
                dve.tensor_tensor(mean[:, :], bn[:, :, 1], bn[:, :, 4], ALU.add)
                dve.tensor_tensor(rt[:, :], bn[:, :, 1], bn[:, :, 4], ALU.subtract)
                link(dve.tensor_tensor(var[:, :], bn[:, :, 2], bn[:, :, 5], ALU.add))
                link(dve.tensor_tensor(rt[:, :], rt[:, :], rt[:, :], ALU.mult))
                link(dve.scalar_tensor_tensor(var[:, :], rt[:, :], D / 4.0, var[:, :], ALU.mult, ALU.add))
                a, b = (1.0 + EPS, EPS * EPS) if double else (1.0, EPS)
                dve.tensor_scalar(mean[:, :], mean[:, :], 0.5, None, ALU.mult)
                link(dve.tensor_scalar(var[:, :], var[:, :], a / D, b, ALU.mult, ALU.add))
                link(dve.tensor_scalar(rt[:, :].bitcast(I32), var[:, :].bitcast(I32), 1, None, ALU.logical_shift_right))
                link(dve.tensor_scalar(ry[:, :].bitcast(I32), rt[:, :].bitcast(I32), -1.0, float(RSQRT_GUESS),
                                       ALU.mult, ALU.add))
                for _ in range(NEWTON):
                    link(dve.tensor_tensor(rt[:, :], ry[:, :], ry[:, :], ALU.mult))
                    link(dve.scalar_tensor_tensor(rt[:, :], rt[:, :], -0.5, var[:, :], ALU.mult, ALU.mult))
                    link(dve.scalar_tensor_tensor(ry[:, :], rt[:, :], 1.5, ry[:, :], ALU.add, ALU.mult))
                assert k == LN_STEPS
                for i, t in enumerate(tiles):
                    last = dve.tensor_scalar(dst[:, i, :], t, mean[:, i:i + 1], ry[:, i:i + 1], ALU.subtract, ALU.mult)
                last.then_inc(done, 1)

            def x_tiles(g):
                return [xs[:, bass.ds(g * 2 + i, 1), :].rearrange("p a n -> p (a n)") for i in range(2)]

            def transposed(name, g, first, last, gn):
                isx = name == "TXx"
                dst, col = (xnT, 0) if isx else (cnT, 2)
                b = mix_ps[mix_bank(name, g, first, last)]
                n = mix_index(name, g, first, last)
                dve.wait_ge(mix_filled, n + 1)
                if isx:
                    dve.wait_ge(cnT_ready, gn + 1)
                elif g is not None:
                    dve.wait_ge(xnT_ready, gn)
                for k in range(KT):
                    done = dve.tensor_scalar(tf[:, k, :], b[:, k * GT:(k + 1) * GT], cols[:, k, col:col + 1],
                                             cols[:, k, col + 1:col + 2], ALU.mult, ALU.add)
                done.then_inc(mix_freed, 1)
                dve.wait_ge(tfh_done, gn * 2 + (2 if isx else 1))
                dve.tensor_tensor(dst[1][:, :, :], tf[:, :, :], dst[0][:, :, :].bitcast(F32), ALU.subtract
                                  ).then_inc(xnT_ready if isx else cnT_ready, 1)

            def keys_values_lo(g, first, last, gn):
                b = mix_ps[mix_bank("K", g, first, last)]
                dve.wait_ge(kh_done, gn + 1)
                for a in range(2):
                    r = slice(DH * a, DH * a + DH)
                    done = dve.scalar_tensor_tensor(
                        kz[1][r, :, a, :], b[r, 0:GT].rearrange("p (b n) -> p b n", b=2), DH ** -0.5,
                        kz[0][r, :, a, :].bitcast(F32), ALU.mult, ALU.subtract)
                done.then_inc(mix_freed, 1)
                b = mix_ps[mix_bank("V", g, first, last)]
                dve.wait_ge(vh_done, gn + 1)
                dve.tensor_tensor(vv[1][:, :, :], halves(b, 2)[:, :, 0:P], vv[0][:, :, :].bitcast(F32), ALU.subtract
                                  ).then_inc(mix_freed, 1)

            def queries_lo(pair, g, first, last, gn):
                b = mix_ps[mix_bank(f"QP{pair}", g, first, last)]
                dve.wait_ge(qh_done, gn * 4 + (pair + 1))
                dve.tensor_tensor(q[1][:, 2 * pair:2 * pair + 2, :], halves(b, 2),
                                  q[0][:, 2 * pair:2 * pair + 2, :].bitcast(F32), ALU.subtract).then_inc(mix_freed, 1)

            def split_hi(n):
                src, hi, _ = chunk_split(n)
                dve.wait_ge(stage_full[n % 2], stage_value(n))
                dve.tensor_copy(hi, src).then_inc(stage_hi, 1)

            def early_split(n):
                split_hi(n)
                src, hi, lo = chunk_split(n)
                dve.wait_ge(stage_hi, n + 1)
                dve.tensor_tensor(lo, src, hi.bitcast(F32), ALU.subtract).then_inc(w_ready, 1)

            for t in kz + gw:
                last = dve.memset(t[:].bitcast(F32), 0.0)
            last.then_inc(zeros_done, 1)
            dve.wait_ge(zeros_done, 1)
            dve.wait_ge(ctx_loaded, 16)
            normalise([ct[:, i, :] for i in range(2)], xn[:, 2:4, :], False, 0, cnorm_done)
            dve.wait_ge(x_in[0], 16)
            normalise(x_tiles(0), xn[:, 0:2, :], True, 1, xnorm_done, (cnorm_done, 1))
            dve.wait_ge(cols_filled, 1)
            dve.tensor_copy(cols[:, :, :], bank[0][:, 0:KT * NROW].rearrange("p (k n) -> p k n", k=KT)
                            ).then_inc(cols_done, 1)
            dve.wait_ge(cols_done, 1)
            dve.wait_ge(stage_full[0], stage_value(0))
            kv = stage[:, 0, 0:KT * P].rearrange("p (k a n) -> p k a n", k=KT, a=2)
            both = [(w, a, slice(DH * h, DH * h + DH)) for w, a in ((wkk, 0), (wv, 1)) for h in range(2)]
            for w, a, r in both:
                last = dve.tensor_copy(w[0][:, :, r], kv[:, :, a, :])
            last.then_inc(stage_hi, 1)
            dve.wait_ge(stage_hi, 1)
            for w, a, r in both:
                last = dve.tensor_tensor(w[1][:, :, r], kv[:, :, a, :], w[0][:, :, r].bitcast(F32), ALU.subtract)
            last.then_inc(w_ready, 1)
            transposed("TXc", None, False, False, 0)
            transposed("TXx", None, False, False, 0)
            early_split(1)
            keys_values_lo(None, False, False, 0)
            early_split(2)
            queries_lo(0, None, False, False, 0)
            queries_lo(1, None, False, False, 0)
            early_split(3)
            gate_cols = cols[:, :, 5 + NE:NROW]
            dve.tensor_copy(gw[0][:, :, 0:NE], gate_cols).then_inc(gw_done, 1)
            dve.wait_ge(gw_done, 1)
            dve.tensor_tensor(gw[1][:, :, 0:NE], gate_cols, gw[0][:, :, 0:NE].bitcast(F32), ALU.subtract
                              ).then_inc(gw_done, 1)

            def attended_lo(u):
                dve.wait_ge(oh_done, u + 1)
                v = pv_ps[:, :].rearrange("p (m a n) -> p m a n", m=2, a=2)
                for a in range(2):
                    r = slice(DH * a, DH * a + DH)
                    done = dve.tensor_tensor(oT[1][r, :, :], v[r, :, a, :], oT[0][r, :, :].bitcast(F32), ALU.subtract)
                done.then_inc(o_ready, 1)

            def x1_split(g, b):
                at = bass.ds(g * GT, GT)
                dve.tensor_scalar(xmT[0][:, :, at], halves(b, KT), 1.0, None, ALU.mult).then_inc(xmh_done, 1)
                dve.wait_ge(xmh_done, g + 1)
                return dve.tensor_tensor(xmT[1][:, :, at], halves(b, KT), xmT[0][:, :, at].bitcast(F32), ALU.subtract)

            def iteration(g, first=False, last=False):
                call = 2 if first else g * 3 + 1
                for s in range(NU + 2):
                    u = g * NU + s
                    if s < NU:
                        dve.wait_ge(scores_filled, u + 1)
                        if not (first and s < 2):
                            dve.wait_ge(exp_done, u - 1)
                        dve.tensor_reduce(nmax[:, s % 2, :], halves(sc_ps[s % 2], 4), AX.X, ALU.max, negate=True
                                          ).then_inc(nmax_done, 1)
                    if s >= 2:
                        attended_lo(u - 2)
                    if first:
                        for n in CHUNK_SLOT.get(s, []):
                            split_hi(n)
                    if s == 0:
                        queries_lo(2, g, first, last, g)
                    if s == 2:
                        queries_lo(3, g, first, last, g)
                    if s < NU:
                        dve.wait_ge(exp_done, u + 1)
                        if not (first and s < 2):
                            dve.wait_ge(probs_ready, u - 1)
                        dve.reciprocal(rden[:, s % 2, :], den[:, s % 2, :]).then_inc(rden_done, 1)
                    if s == 3 and not first:
                        dve.wait_ge(mix_filled, mix_index("X1T", g, first, last) + 1)
                        x1_split(g - 1, mix_ps[mix_bank("X1T", g, first, last)]).then_inc(mix_freed, 1)
                    if s == 4 and not first:
                        b = mix_ps[mix_bank("GL", g, first, last)]
                        dve.wait_ge(mix_filled, mix_index("GL", g, first, last) + 1)
                        dve.tensor_copy(lgT[:, bass.ds(g * GT - GT, GT)], b[0:NE, 0:GT]).then_inc(mix_freed, 1)
                    if s == 6 and not last:
                        transposed("TXc", g, first, last, g + 1)
                    if s < NU:
                        b = mix_ps[mix_bank(f"FF{s}", g, first, last)]
                        dve.wait_ge(tanh_done, u + 1)
                        dve.scalar_tensor_tensor(u1[:, :], th[:, :], 1.0, b[:, GT:2 * GT], ALU.add, ALU.mult
                                                 ).then_inc(u1_done, 1)
                        dve.wait_ge(u1_done, u + 1)
                        if not (first and s == 0):
                            dve.wait_ge(u_ready, u)
                        dve.scalar_tensor_tensor(uf[:, :], b[:, 0:GT], 0.5, u1[:, :], ALU.mult, ALU.mult
                                                 ).then_inc(mix_freed, 1)
                    if 1 <= s <= NU:
                        dve.wait_ge(pTh_done, u)
                        dve.tensor_tensor(pT[1][:, :], t_ps[:, :], pT[0][:, :].bitcast(F32), ALU.subtract
                                          ).then_inc(pT_ready, 1)
                    if s == 1 and not first:
                        dve.wait_ge(x1_done, g)
                        normalise(x_tiles(g - 1), xn[:, 0:2, :], False, call, x1norm_done,
                                  (xnorm_done, g + 1))
                    if s == 3 and not last:
                        dve.wait_ge(ctx_loaded, g * 16 + 32)
                        normalise([ct[:, i, :] for i in range(2)], xn[:, 2:4, :], False,
                                  call + (0 if first else 1), cnorm_done,
                                  (xnorm_done, 1) if first else (x1norm_done, g))
                    if s == 4 and not last:
                        if first:
                            for later in range(1, NG):
                                dve.wait_ge(x_in[later], 16)
                        normalise(x_tiles(g + 1), xn[:, 0:2, :], True, call + (1 if first else 2), xnorm_done,
                                  (cnorm_done, g + 2))
                    if s == NU and not last:
                        transposed("TXx", g, first, last, g + 1)
                        keys_values_lo(g, first, last, g + 1)
                if not last:
                    queries_lo(0, g, first, last, g + 1)
                    queries_lo(1, g, first, last, g + 1)
                dve.wait_ge(wo_done, g * NU + NU)
                at = xs[:, bass.ds(g * 2, 2), :]
                dve.scalar_tensor_tensor(at, halves(out_ps, 2), gates[:, 0:1], at, ALU.mult, ALU.add
                                         ).then_inc(x1_done, 1)

            dve.wait_ge(gates_done, 1)
            iteration(0, first=True)
            with dve.Fori(1, NG - 1) as g:
                iteration(g)
            iteration(NG - 1, last=True)

            dve.wait_ge(x1_done, NG)
            normalise(x_tiles(NG - 1), ct[:, :, :], False, 3 * NG - 1, x1norm_done, (x1norm_done, NG - 1))

            def hidden_lo(step, parity):
                for m in range(KT):
                    dve.wait_ge(hh_done, KT * step + m + 1)
                    dve.tensor_tensor(hh[:, parity, 1, m, :], hf[:, m, :], hh[:, parity, 0, m, :].bitcast(F32),
                                      ALU.subtract).then_inc(h_ready, 1)

            def add_expert(use, j, pos, first_bank):
                for half in range(2):
                    b = dn_ps[(first_bank + half) % 4]
                    dve.wait_ge(dn_filled, use + (half + 1))
                    if not (isinstance(use, int) and use == 0):
                        dve.wait_ge(dn_freed, use + half)
                    for i in range(2):
                        t = TPS * j + 2 * half + i
                        done = dve.scalar_tensor_tensor(
                            xs[:, t, :], b[:, i * D:(i + 1) * D],
                            comb[:, bass.ds(pos, 1), t:t + 1].rearrange("p a n -> p (a n)"), xs[:, t, :],
                            ALU.mult, ALU.add)
                    done.then_inc(dn_freed, 1)

            k = 0

            def link(ins):
                nonlocal k
                k += 1
                ins.then_inc(gate_step, 1)
                dve.wait_ge(gate_step, k)

            link(dve.memset(comb[:, 0, :], 1.0))
            link(dve.tensor_scalar(comb[:, 0, :], comb[:, 0, :], gates[:, 1:2], None, ALU.mult))
            hidden_lo(0, 0)
            hidden_lo(1, 1)
            add_expert(down_use(0), 0, 0, down_use(0))
            dve.wait_ge(dn_filled, USE_X1T + 1)
            x1_split(NG - 1, dn_ps[USE_X1T % 4]).then_inc(dn_freed, 1)
            hidden_lo(2, 0)
            add_expert(down_use(1), 1, 0, down_use(1))
            dve.wait_ge(dn_filled, USE_GL + 1)
            dve.tensor_copy(lgT[:, (NG - 1) * GT:NG * GT], dn_ps[USE_GL % 4][0:NE, 0:GT]).then_inc(dn_freed, 1)
            hidden_lo(3, 1)
            add_expert(down_use(2), 2, 0, down_use(2))
            def per_tile(v):
                return v[:, :].unsqueeze(2).broadcast_to((P, NB, NE))

            dve.wait_ge(dn_filled, USE_LT + 1)
            dve.wait_ge(rio_done, 1)
            dve.tensor_copy(lg[:, :, :], dn_ps[USE_LT % 4][:, 0:NB * NE].rearrange("p (t e) -> p t e", t=NB)
                            ).then_inc(dn_freed, 1)
            dve.wait_ge(dn_freed, USE_LT + 1)
            link(dve.tensor_reduce(g1[:, :], lg[:, :, :], AX.X, ALU.max))
            link(dve.tensor_tensor(gb[:, :, :], lg[:, :, :], per_tile(g1), ALU.subtract))
            assert k == GATE_SHIFTED
            dve.wait_ge(gexp_done, 1)
            link(dve.tensor_reduce(g2[:, :], ga[:, :, :], AX.X, ALU.add))
            link(dve.reciprocal(g3[:, :], g2[:, :]))
            link(dve.tensor_tensor(ga[:, :, :], ga[:, :, :], per_tile(g3), ALU.mult))
            link(dve.tensor_reduce(g1[:, :], ga[:, :, :], AX.X, ALU.max))
            link(dve.tensor_tensor(gb[:, :, :], ga[:, :, :], per_tile(g1), ALU.is_equal))
            link(dve.tensor_tensor(gb[:, :, :], gb[:, :, :], rio[:, :, :], ALU.mult))
            link(dve.tensor_reduce(g3[:, :], gb[:, :, :], AX.X, ALU.max))
            link(dve.tensor_tensor(oh1[:, :, :], rio[:, :, :], per_tile(g3), ALU.is_equal))
            link(dve.scalar_tensor_tensor(lg[:, :, :], oh1[:, :, :], -2.0, ga[:, :, :], ALU.mult, ALU.add))
            link(dve.tensor_reduce(g2[:, :], lg[:, :, :], AX.X, ALU.max))
            link(dve.tensor_tensor(gb[:, :, :], lg[:, :, :], per_tile(g2), ALU.is_equal))
            link(dve.tensor_tensor(gb[:, :, :], gb[:, :, :], rio[:, :, :], ALU.mult))
            link(dve.tensor_reduce(g3[:, :], gb[:, :, :], AX.X, ALU.max))
            link(dve.tensor_tensor(lg[:, :, :], rio[:, :, :], per_tile(g3), ALU.is_equal))
            link(dve.scalar_tensor_tensor(g3[:, :], g1[:, :], 1e-20, g2[:, :], ALU.add, ALU.add))
            link(dve.reciprocal(g3[:, :], g3[:, :]))
            link(dve.tensor_scalar(g3[:, :], g3[:, :], gates[:, 1:2], None, ALU.mult))
            link(dve.tensor_tensor(g1[:, :], g1[:, :], g3[:, :], ALU.mult))
            link(dve.tensor_tensor(g2[:, :], g2[:, :], g3[:, :], ALU.mult))
            link(dve.tensor_tensor(oh1[:, :, :], oh1[:, :, :], per_tile(g1), ALU.mult))
            link(dve.tensor_tensor(lg[:, :, :], lg[:, :, :], per_tile(g2), ALU.mult))
            dve.tensor_tensor(comb[:, 1:NPOS, :].rearrange("p e t -> p t e"), oh1[:, :, :], lg[:, :, :], ALU.add
                              ).then_inc(comb_done, 1)
            dve.wait_ge(comb_done, 1)
            dve.wait_ge(dbrow_in, 32)
            dve.tensor_copy(db[0][0:NPOS, :], dbrow[:, :]).then_inc(db_done, 1)
            dve.wait_ge(db_done, 1)
            dve.tensor_tensor(db[1][0:NPOS, :], dbrow[:, :], db[0][0:NPOS, :].bitcast(F32), ALU.subtract
                              ).then_inc(db_done, 1)
            with dve.Fori(0, NE // 2) as i:
                for j in range(2 * STEPS):
                    hidden_lo(i * (2 * STEPS) + (STEPS + j), j % 2)
                    before = STEPS + j - 1
                    add_expert(i * (4 * STEPS) + down_use(before), before % STEPS, i * 2 + before // STEPS,
                               down_use(before))
            for n in range(4):
                dve.wait_ge(cth_done, n + 1)
                dve.tensor_tensor(cT[1][0:NPOS, n * 512:(n + 1) * 512], dn_ps[(USE_CT + n) % 4][0:NPOS, :],
                                  cT[0][0:NPOS, n * 512:(n + 1) * 512].bitcast(F32), ALU.subtract).then_inc(dn_freed, 1)
            for n in range(NB // 2):
                use = USE_BIAS + n
                dve.wait_ge(dn_filled, use + 1)
                dve.wait_ge(dn_freed, use)
                dve.tensor_tensor(xs[:, 2 * n:2 * n + 2, :], halves(dn_ps[use % 4], 2), xs[:, 2 * n:2 * n + 2, :], ALU.add
                                  ).then_inc(dn_freed, 1)
            add_expert(USE_END, STEPS - 1, NE, USE_END)

        @block.tensor
        def _(pe):
            def matmul3(ps, wts, mov, first, last):
                pe.matmul(ps, wts[1], mov[0], start=first, stop=False, skip_group_check=True)
                pe.matmul(ps, wts[0], mov[0], start=False, stop=False, skip_group_check=True)
                return pe.matmul(ps, wts[0], mov[1], start=False, stop=last, skip_group_check=True)

            def mix(name, g, first, last):
                n = mix_index(name, g, first, last)
                if not (isinstance(n, int) and n < 3):
                    pe.wait_ge(mix_freed, n - 2)
                return mix_ps[mix_bank(name, g, first, last)]

            def transposes(b, tiles):
                for i in range(2):
                    for k in range(KT):
                        done = pe.transpose(b[:, k * GT + i * P:k * GT + (i + 1) * P], tiles[:, i, k * P:(k + 1) * P],
                                            ident[:, :])
                return done

            def norm_T(name, g, first, last, gn):
                b = mix(name, g, first, last)
                isx = name == "TXx"
                pe.wait_ge(xnorm_done if isx else cnorm_done, gn + 1)
                transposes(b, xn[:, 0:2] if isx else xn[:, 2:4]).then_inc(mix_filled, 1)

            def keys_values(g, first, last, gn):
                b = mix("K", g, first, last)
                pe.wait_ge(cnT_ready, gn + 1)
                for k in range(KT):
                    done = matmul3(b[:, 0:GT], [w[:, k, :] for w in wkk], [t[:, k, :] for t in cnT], k == 0, k == KT - 1)
                done.then_inc(mix_filled, 1)
                b = mix("V", g, first, last)
                for i in range(2):
                    for k in range(KT):
                        done = matmul3(b[:, i * GT:(i + 1) * GT], [t[:, k, i * P:(i + 1) * P] for t in cnT],
                                       [w[:, k, :].unsqueeze(1).broadcast_to((P, 2, P)) for w in wv],
                                       k == 0, k == KT - 1)
                done.then_inc(mix_filled, 1)

            def queries(pair, g, first, last, gn):
                b = mix(f"QP{pair}", g, first, last)
                pe.wait_ge(xnT_ready, gn + 1)
                for i in range(2):
                    m = 2 * pair + i
                    for k in range(KT):
                        done = matmul3(b[:, i * GT:(i + 1) * GT], [w[:, k, m * P:(m + 1) * P] for w in wq],
                                       [t[:, k, :] for t in xnT], k == 0, k == KT - 1)
                done.then_inc(mix_filled, 1)

            def logits(b, g):
                for k in range(KT):
                    done = matmul3(b[:, 0:GT], [w[:, k, :] for w in gw],
                                   [t[:, k, bass.ds(g * GT, GT)] for t in xmT], k == 0, k == KT - 1)
                return done

            def attend(u, s, very_first):
                pe.wait_ge(pT_ready, u + 1)
                if not very_first:
                    pe.wait_ge(o_ready, u)
                matmul3(pv_ps[:, :], [t[:, s % 2, :] for t in vv], [t[:, :] for t in pT], True, True
                        ).then_inc(pv_filled, 1)

            def project(u, s, last_of_group):
                pe.wait_ge(o_ready, u + 1)
                b = s % 2
                for m in range(2):
                    done = matmul3(out_ps[:, b * D:(b + 1) * D], [t[:, m, :] for t in oT],
                                   [w[:, 2 * (s // 2) + m, :] for w in wo], False, last_of_group)
                done.then_inc(wo_done, 1)

            def iteration(g, first=False, last=False):
                def chunk(n):
                    if first:
                        pe.wait_ge(w_ready, n + 1)

                for s in range(NU + 2):
                    u = g * NU + s
                    if s >= 2 and s != NU + 1:
                        attend(u - 2, s, first and s == 2)
                    if s < NU:
                        if not (first and s < 2):
                            pe.wait_ge(exp_done, u - 1)
                        if s == 0:
                            n = mix_index("QP0", None, False, False) if first else mix_index(
                                "QP0", g - 1, False, False)
                            pe.wait_ge(mix_freed, n + 2)
                        if s in (4, 6):
                            pe.wait_ge(mix_freed, mix_index(f"QP{s // 2}", g, first, last) + 1)
                        for i in range(2):
                            m = 2 * (s // 2) + i
                            done = matmul3(sc_ps[s % 2][:, i * GT:(i + 1) * GT],
                                           [t[:, m, (s % 2) * P:(s % 2 + 1) * P] for t in q],
                                           [t[:, s % 2, :, :] for t in kz], True, True)
                        done.then_inc(scores_filled, 1)
                    if s == 0:
                        queries(2, g, first, last, g)
                    if s == 2:
                        queries(3, g, first, last, g)
                    if s == 3 and not first:
                        b = mix("X1T", g, first, last)
                        pe.wait_ge(x1norm_done, g)
                        transposes(b, xn[:, 0:2]).then_inc(mix_filled, 1)
                    if s == 4 and not first:
                        b = mix("GL", g, first, last)
                        pe.wait_ge(gw_done, 2)
                        pe.wait_ge(mix_freed, mix_index("X1T", g, first, last) + 1)
                        logits(b, g - 1).then_inc(mix_filled, 1)
                    if s == 6 and not last:
                        norm_T("TXc", g, first, last, g + 1)
                    if s < NU:
                        b = mix(f"FF{s}", g, first, last)
                        chunk([3, 6, 7, 10][s // 2])
                        for i in range(2):
                            for k in range(KT):
                                at = slice(i * FF + s * P, i * FF + (s + 1) * P)
                                done = matmul3(b[:, i * GT:(i + 1) * GT], [w[:, k, at] for w in wf1],
                                               [t[:, k, :] for t in xnT], k == 0, k == KT - 1)
                        done.then_inc(mix_filled, 1)
                    if s == NU and not last:
                        norm_T("TXx", g, first, last, g + 1)
                    if 1 <= s <= NU:
                        pe.wait_ge(probs_ready, u)
                        if not (first and s == 1):
                            pe.wait_ge(pT_ready, u - 1)
                        for h in range(4):
                            done = pe.transpose(t_ps[:, h * P:(h + 1) * P], pr[:, (s - 1) % 2, h, :], ident[:, :])
                        done.then_inc(pT_filled, 1)
                        pe.wait_ge(u_ready, u)
                        chunk([4, 8][(s - 1) // 4])
                        if s == 1 and not first:
                            pe.wait_ge(x1_done, g)
                        for b in range(2):
                            done = matmul3(out_ps[:, b * D:(b + 1) * D],
                                           [t[:, (s - 1) % 2, b * P:(b + 1) * P] for t in uT],
                                           [w[:, s - 1, :] for w in wf2], s == 1 and b == 0, False)
                        done.then_inc(ff2_done, 1)
                    if s >= 2 and s < NU + 1:
                        chunk([5, 9][(s - 2) // 4])
                        project(u - 2, s - 2, False)
                    if s == NU:
                        attend(u - 1, NU - 1, False)
                        if not last:
                            keys_values(g, first, last, g + 1)
                if not last:
                    queries(0, g, first, last, g + 1)
                    queries(1, g, first, last, g + 1)
                project(g * NU + (NU - 1), NU - 1, True)

            pe.wait_ge(ident_done, 2)
            pe.wait_ge(rows_in, 16 * 7)
            for k in range(KT):
                done = pe.transpose(bank[0][:, k * NROW:(k + 1) * NROW], rows[:, k * P:(k + 1) * P],
                                    ident[0:NROW, 0:NROW])
            done.then_inc(cols_filled, 1)
            pe.wait_ge(zeros_done, 1)
            norm_T("TXc", None, False, False, 0)
            norm_T("TXx", None, False, False, 0)
            pe.wait_ge(w_ready, 1)
            keys_values(None, False, False, 0)
            pe.wait_ge(w_ready, 3)
            queries(0, None, False, False, 0)
            queries(1, None, False, False, 0)
            iteration(0, first=True)
            with pe.Fori(1, NG - 1) as g:
                iteration(g)
            iteration(NG - 1, last=True)

            def down_bank(use, bank_of):
                if not (isinstance(use, int) and use < 4):
                    pe.wait_ge(dn_freed, use - 3)
                return dn_ps[bank_of % 4]

            def up(step, parity, j, half, early):
                for m in range(KT):
                    if early is None or early >= 2:
                        pe.wait_ge(silu_done, KT * step + (m - 2 * KT + 1))
                    for k in range(KT):
                        done = matmul3(up_ps[2 * parity + m][:, :],
                                       [ring[:, half, a, k, m * P:(m + 1) * P] for a in range(2)],
                                       [t[:, k, j * ST:(j + 1) * ST] for t in xmT], k == 0, k == KT - 1)
                    done.then_inc(up_filled, 1)

            def down(step, parity, half, use, bank_of):
                pe.wait_ge(h_ready, KT * step + KT)
                for pair in range(2):
                    b = down_bank(use + pair, bank_of + pair)
                    for i in range(2):
                        t = 2 * pair + i
                        for k in range(KT):
                            done = matmul3(b[:, i * D:(i + 1) * D],
                                           [hh[:, parity, a, k, t * P:(t + 1) * P] for a in range(2)],
                                           [ring[:, half, 2 + a, k, :] for a in range(2)], k == 0, k == KT - 1)
                    done.then_inc(dn_filled, 1)

            pe.wait_ge(exp_done, NG * NU)
            pe.wait_ge(pT_ready, NG * NU)
            pe.wait_ge(o_ready, NG * NU)
            pe.wait_ge(mix_freed, len(MIX_PRO) + len(MIX_FIRST) + (NG - 2) * len(MIX_MID) + len(MIX_LAST))
            pe.wait_ge(w_ready, NCA + 1)
            up(0, 0, 0, 0, 0)
            up(1, 1, 1, 0, 1)
            pe.wait_ge(x1_done, NG)
            down(0, 0, 0, down_use(0), down_use(0))
            up(2, 0, 2, 0, 2)
            pe.wait_ge(x1norm_done, NG)
            transposes(down_bank(USE_X1T, USE_X1T), ct[:, :, :]).then_inc(dn_filled, 1)
            down(1, 1, 0, down_use(1), down_use(1))
            b = down_bank(USE_GL, USE_GL)
            pe.wait_ge(dn_freed, USE_X1T + 1)
            logits(b, NG - 1).then_inc(dn_filled, 1)
            up(3, 1, 3, 0, 3)
            down(2, 0, 0, down_use(2), down_use(2))
            b = down_bank(USE_LT, USE_LT)
            pe.wait_ge(dn_freed, USE_GL + 1)
            for t in range(NB):
                done = pe.transpose(b[:, t * NE:(t + 1) * NE], lgT[:, t * P:(t + 1) * P], ident[0:NE, 0:NE])
            done.then_inc(dn_filled, 1)
            with pe.Fori(0, NE // 2) as i:
                for j in range(2 * STEPS):
                    step = i * (2 * STEPS) + (STEPS + j)
                    if j % STEPS == 0:
                        pe.wait_ge(w_ready, i * 2 + (NCA + 2 + j // STEPS))
                    up(step, j % 2, j % STEPS, (1 + j // STEPS) % 2, None)
                    before = STEPS + j - 1
                    down(step - 1, (j + 1) % 2, (before // STEPS) % 2, i * (4 * STEPS) + down_use(before),
                         down_use(before))
            pe.wait_ge(comb_done, 1)
            for n in range(4):
                b = down_bank(USE_CT + n, USE_CT + n)
                for i in range(4):
                    t = 4 * n + i
                    done = pe.transpose(b[0:NPOS, i * P:(i + 1) * P], comb[:, :, t], ident[:, :])
                done.then_inc(dn_filled, 1)
            pe.wait_ge(db_done, 2)
            for n in range(NB // 2):
                use = USE_BIAS + n
                b = down_bank(use, use)
                pe.wait_ge(dn_freed, USE_CT + n // 2 + 1)
                for i in range(2):
                    t = 2 * n + i
                    done = matmul3(b[:, i * D:(i + 1) * D], [c[0:NPOS, t * P:(t + 1) * P] for c in cT],
                                   [d[0:NPOS, :] for d in db], True, True)
                done.then_inc(dn_filled, 1)
            down(NSTEP - 1, (NSTEP - 1) % 2, (NPOS - 1) % 2, USE_END, USE_END)


GATE_SHIFTED = 4

_INS = ["x", "ctx_1024", "g_xattn", "g_ffn", "L0_xattn_ln_g", "L0_xattn_ln_b", "L0_xattn_cln_g", "L0_xattn_cln_b",
        "L0_xattn_Wq", "L0_xattn_Wkv", "L0_xattn_Wo", "L0_xattn_Wff1", "L0_xattn_Wff2", "L0_ffn_gate_w",
        "L0_ffn_up_w", "L0_ffn_up_b", "L0_ffn_down_w", "L0_ffn_down_b", "L0_ffn_sh_up_w", "L0_ffn_sh_up_b",
        "L0_ffn_sh_down_w", "L0_ffn_sh_down_b"]


def kernel(**inputs):
    import concourse.bacc as bacc
    from concourse.bass_utils import run_bass_kernel_spmd

    nc = bacc.Bacc("TRN2", target_bir_lowering=False, num_devices=1)
    arrays, args = {}, []
    for name in _INS:
        a = np.ascontiguousarray(inputs[name])
        arrays[f"in_{name}"] = a
        args.append(nc.dram_tensor(f"in_{name}", a.shape, mybir.dt.from_np(a.dtype), kind="ExternalInput").ap())
    args.append(nc.dram_tensor("out_x", (NB, P, D), F32, kind="ExternalOutput").ap())
    program(nc, *args)
    r = run_bass_kernel_spmd(nc, [arrays], core_ids=[0])
    return r.results[0]["out_x"]
```

```python
from contextlib import ExitStack

import numpy as np

import concourse.bass as bass
from concourse import mybir

F32 = mybir.dt.float32
F32R = mybir.dt.float32r
I32 = mybir.dt.int32
ALU = mybir.AluOpType
ACT = mybir.ActivationFunctionType
AX = mybir.AxisListType

P = 128
NB, D = 16, 256
H, DH = 16, 64
FF = 1024
NE, HID = 8, 256
KT = D // P
NG = NB // 2
GT = 2 * P
NU = 8
NFF = FF // P
EPS = 1e-5
NEWTON = 3
LN_STEPS = 9 + 3 * NEWTON
RSQRT_GUESS = 0x5F3759DF
WO_T = H * DH // P

NEXT = ["K", "V", "QP0", "QP1"]
MIX_PRO = ["TXc", "TXx"] + NEXT
MIX_MID = ["QP2", "FF0", "FF1", "QP3", "FF2", "FF3", "FF4", "X1T", "FF5", "TXc", "FF6", "GL", "FF7",
           "TXx"] + NEXT
MIX_FIRST = [n for n in MIX_MID if n not in ("X1T", "GL")]
MIX_LAST = [n for n in MIX_MID if n not in ["TXc", "TXx"] + NEXT]


def mix_index(name, g, first, last):
    if g is None:
        return MIX_PRO.index(name)
    if first:
        return len(MIX_PRO) + MIX_FIRST.index(name)
    base = len(MIX_PRO) + len(MIX_FIRST) - len(MIX_MID)
    return g * len(MIX_MID) + (base + (MIX_LAST if last else MIX_MID).index(name))


def ln_base(call):
    return call * LN_STEPS


def mix_bank(name, g, first, last):
    if g is None or first:
        return mix_index(name, g, first, last) % 3
    return (len(MIX_PRO) + len(MIX_FIRST) + (MIX_LAST if last else MIX_MID).index(name)) % 3


CHUNKS_A = ["wkv", "wq0", "wq1", "ff1_0", "ff2_0", "wo_0", "ff1_1", "ff1_2", "ff2_1", "wo_1", "ff1_3"]
EARLY = 4
CHUNK_SLOT = {0: [4, 5, 6], 1: [7], 2: [8], 3: [9], 4: [10]}
LO_ON_POOL = (2, 4, 5, 6, 7, 8, 9, 10)
NSTAGE = 4
NCA = len(CHUNKS_A)
NPOS = NE + 1
STEPS = 4
ST = 4 * P
TPS = ST // P

NTS = NB - 2
NCH = 2 * NTS
TILES = NCH + NE - 1
WINDOW = 4
NWIN = (TILES + 1) // WINDOW
SHIFT = 3
assert (TILES - 3) % WINDOW == 0
TCOLS = TILES + TILES % 2
WAVE = NTS

USE_LT = 0
USE_DOWN = [1, 4, 6, 9]
USE_RANK = 3
USE_X1T = 8
USE_DENSE = 11


def program(nc, x, ctx_in, g_xattn, g_ffn, ln_g, ln_b, cln_g, cln_b, Wq, Wkv, Wo, Wff1, Wff2,
            gate_w, up_w, up_b, down_w, down_b, sh_up_w, sh_up_b, sh_down_w, sh_down_b, out):
    stack = ExitStack()
    with stack:
        def sb(name, shape, dt=F32):
            return stack.enter_context(nc.sbuf_tensor(name, shape, dt))

        def sem(name):
            return stack.enter_context(nc.semaphore(name))

        weights = sb("weights", [P, 20 * 1024], F32R)
        wq_t = weights[:, 0:4096].rearrange("p (a n) -> p a n", a=4)
        wq = [wq_t[:, 0:2, :], wq_t[:, 2:4, :]]
        wkk = [sb("wkk_h", [P, KT, P], F32R), sb("wkk_l", [P, KT, P], F32R)]
        wv = [sb("wv_h", [P, KT, P], F32R), sb("wv_l", [P, KT, P], F32R)]
        wf1_t = weights[:, 4096:12288].rearrange("p (a k n) -> p a k n", a=2, k=KT)
        wf1 = [wf1_t[:, 0], wf1_t[:, 1]]
        wf2, wo = [[weights[:, at + 2048 * a:at + 2048 * (a + 1)].rearrange("p (k n) -> p k n", n=D) for a in range(2)]
                   for at in (12288, 16384)]
        gw = [sb("gw_h", [P, KT, P], F32R), sb("gw_l", [P, KT, P], F32R)]
        stage = sb("stage", [P, 2, 1024])
        ident = sb("ident", [P, P])
        NROW = 4 + NE + 1 + NE
        all_rows = sb("all_rows", [32 + NE + 1, D])
        rows, dbrow = all_rows[0:NROW, :], all_rows[32:32 + NE + 1, :]
        cols = sb("cols", [P, KT, NROW])
        gates_in = sb("gates_in", [P, 2])
        gates = sb("gates", [P, 2])
        xs = sb("xs", [P, NB, D])
        ct = sb("ct", [P, 2, D])
        xn = sb("xn", [P, 4, D])
        tf = sb("tf", [P, KT, GT])
        acts = sb("acts", [P, 9 * 512], F32R)
        cnT, xnT, uT = [[acts[:, 512 * i:512 * (i + 1)].rearrange("p (k n) -> p k n", k=2) for i in (n, n + 1)]
                        for n in (0, 2, 4)]
        pT = [acts[:, 512 * i:512 * (i + 1)] for i in (6, 7)]
        oT = [acts[:, 4096 + D * i:4096 + D * (i + 1)].rearrange("p (k n) -> p k n", k=2) for i in (0, 1)]
        q_t = sb("q_t", [P, 2, H // 2, GT], F32R)
        q = [q_t[:, 0], q_t[:, 1]]
        kz = [sb("kz_h", [P, 2, 2, P], F32R), sb("kz_l", [P, 2, 2, P], F32R)]
        vv = [sb("vv_h", [P, 2, P], F32R), sb("vv_l", [P, 2, P], F32R)]
        pr = sb("pr", [P, 2, 4, P])
        nmax = sb("nmax", [P, 2, 4])
        den = sb("den", [P, 2, 4])
        rden = sb("rden", [P, 2, 4])
        th = sb("th", [P, GT])
        u1 = sb("u1", [P, GT])
        uf = sb("uf", [P, GT])
        bn = sb("bn", [P, 6, 6])
        mean = sb("mean", [P, 6])
        var = sb("var", [P, 6])
        rt = sb("rt", [P, 6])
        ry = sb("ry", [P, 6])
        xmT_t = sb("xmT_t", [P, 2 * KT, NB * P], F32R)
        xmT = [xmT_t[:, 0:KT], xmT_t[:, KT:2 * KT]]
        spare = sb("spare", [P, NB * P])
        lgT = spare[0:NE, :]
        rio = sb("rio", [P, NB, NE])
        bias = sb("bias", [P, KT, 1])
        g1 = sb("g1", [P, NB])
        g2 = sb("g2", [P, NB])
        g3 = sb("g3", [P, NB])
        lg, ga = [t.rearrange("p (t e) -> p t e", t=NB) for t in (th[:, 0:P], th[:, P:2 * P])]
        gb, oh1 = [t.rearrange("p (t e) -> p t e", t=NB) for t in (u1[:, 0:P], u1[:, P:2 * P])]
        comb = uf[:, 0:NPOS * NB].rearrange("p (c t) -> p c t", c=NPOS)
        shared = weights[:, 0:2048].rearrange("p (m k n) -> p m k n", m=4, k=KT)
        experts = weights[:, 4096:]
        lo_hot = weights[:, 2048:2048 + WAVE * P].rearrange("p (n c) -> p n c", n=WAVE)
        chosen = weights[:, 4096 - (NTS + 1) * NE:4096]
        hi_hot = [t.rearrange("p a b n -> p (a b n)")[:, 0:WAVE * TCOLS].rearrange("p (n c) -> p n c", n=WAVE)
                  for t in kz]
        shared_brow, brow = acts[:, 0:D], acts[:, D:D + 2 * NE * D]
        ones, before = vv[0][:, 0, :], vv[0][:, 1, :]
        consts = tf.rearrange("p k n -> p (k n)")
        iota_lo, iota_tile = consts[:, 0:P], consts[:, P:P + 40]
        token = consts[:, 168:168 + NTS]
        slot_token = consts[:, 192:192 + TILES].bitcast(I32)
        token_slot = consts[:, 240:240 + NCH].bitcast(I32)
        window = consts[0:1, 272:272 + NWIN].bitcast(I32)
        rank = spare[:, 0:NTS * NE].rearrange("p (t e) -> p t e", e=NE)
        slots8 = spare[:, 128:128 + NCH * NE].rearrange("p (t e) -> p t e", e=NE)
        small = spare[:, 384:576]
        tile_cmp = spare[0:1, 576:576 + 40 * NE].rearrange("p (t e) -> p t e", e=NE)
        tile_expert = spare[0:1, 900:940]
        is_tile = ct.rearrange("p a n -> p (a n)")[:, 0:WAVE * TCOLS]
        pack = spare[0:1, 940:940 + NWIN]
        rows_g = spare[:, 0:4 * D].rearrange("p (s n) -> p s n", s=4)
        xg = kz
        hs = ct
        hsT = [wkk, wv]
        ys = stage[:, 0, :].rearrange("p (s n) -> p s n", s=4)
        last_lgT = all_rows[0:NE, :]
        hh = q_t.rearrange("p a m n -> p (a m n)").rearrange("p (s a m n) -> p s a m n", s=2, a=2, m=KT)
        hf = xn.rearrange("p a n -> p (a n)").rearrange("p (m n) -> p m n", m=KT)
        norm_rows = nc.dram_tensor("norm_rows", (NTS * P, D), F32).ap()
        slot_rows = nc.dram_tensor("slot_rows", (TILES * P, D), F32).ap()
        bias_rows = nc.dram_tensor("bias_rows", (2, 2 * NE + 1, D), F32).ap()

        bank = [stack.enter_context(nc.psum_tensor(f"bank{i}", [P, 512], F32)) for i in range(8)]
        sc_ps, t_ps, pv_ps, out_ps, mix_ps = bank[0:2], bank[2], bank[3], bank[4], bank[5:8]
        up_ps, dn_ps = bank[0:4], bank[4:8]

        rows_in = sem("rows_in")
        gates_loaded = sem("gates_loaded")
        dbrow_in = sem("dbrow_in")
        x_in = [sem(f"x_in{g}") for g in range(NG)]
        ctx_loaded = sem("ctx_loaded")
        stage_full = [sem(f"stage_full{i}") for i in range(NSTAGE)]
        kv_hi_done = sem("kv_hi_done")
        chunk_hi_done = sem("chunk_hi_done")
        chunk_split_done = [sem(f"chunk_split_done{n}") for n in range(NCA)]
        ring_hi_done = sem("ring_hi_done")
        ring_ready = sem("ring_ready")
        ident_done = sem("ident_done")
        rio_done = sem("rio_done")
        zeros_done = sem("zeros_done")
        cols_filled = sem("cols_filled")
        cols_done = sem("cols_done")
        gw_done = sem("gw_done")
        gates_done = sem("gates_done")
        mix_filled = sem("mix_filled")
        mix_freed = sem("mix_freed")
        ln_step = sem("ln_step")
        xnorm_done = sem("xnorm_done")
        cnorm_done = sem("cnorm_done")
        x1norm_done = sem("x1norm_done")
        tfh_done = sem("tfh_done")
        cnT_ready = sem("cnT_ready")
        xnT_ready = sem("xnT_ready")
        kh_done = sem("kh_done")
        vh_done = sem("vh_done")
        qh_done = sem("qh_done")
        scores_filled = sem("scores_filled")
        nmax_done = sem("nmax_done")
        exp_done = sem("exp_done")
        rden_done = sem("rden_done")
        probs_ready = sem("probs_ready")
        pT_filled = sem("pT_filled")
        pTh_done = sem("pTh_done")
        pT_ready = sem("pT_ready")
        pv_filled = sem("pv_filled")
        oh_done = sem("oh_done")
        o_ready = sem("o_ready")
        wo_done = sem("wo_done")
        tanh_done = sem("tanh_done")
        u1_done = sem("u1_done")
        uh_done = sem("uh_done")
        u_ready = sem("u_ready")
        ff2_done = sem("ff2_done")
        x1_done = sem("x1_done")
        xmh_done = sem("xmh_done")
        link_done = sem("link_done")
        shifted_done = sem("shifted_done")
        gexp_done = sem("gexp_done")
        bias_done = sem("bias_done")
        comb_done = sem("comb_done")
        bias_split = sem("bias_split")
        bias_stored = sem("bias_stored")
        shared_zeroed = sem("shared_zeroed")
        shared_brow_in = sem("shared_brow_in")
        brow_zeroed = sem("brow_zeroed")
        brow_in = sem("brow_in")
        rows_stored = sem("rows_stored")
        sort_consts = sem("sort_consts")
        chosen_done = sem("chosen_done")
        hot_done = sem("hot_done")
        wave_used = sem("wave_used")
        sorted_done = sem("sorted_done")
        last_logits_filled = sem("last_logits_filled")
        last_logits_copied = sem("last_logits_copied")
        gathered = [sem(f"gathered{i}") for i in range(4)]
        gT_filled = sem("gT_filled")
        xgh_done = sem("xgh_done")
        xg_ready = sem("xg_ready")
        tile_up_filled = sem("tile_up_filled")
        tile_silu_done = sem("tile_silu_done")
        hT_filled = sem("hT_filled")
        hTh_done = sem("hTh_done")
        hT_ready = sem("hT_ready")
        tile_down_filled = sem("tile_down_filled")
        y_copied = sem("y_copied")
        y_stored = [sem(f"y_stored{i}") for i in range(4)]
        back_in = [sem(f"back_in{i}") for i in range(3)]
        back_added = sem("back_added")
        up_filled = sem("up_filled")
        silu_done = sem("silu_done")
        hh_done = sem("hh_done")
        h_ready = sem("h_ready")
        dn_filled = sem("dn_filled")
        dn_freed = sem("dn_freed")
        written = sem("written")

        block = stack.enter_context(nc.Block())

        def buffer(n):
            if n < NCA:
                i = n % NSTAGE
                return (stage[:, i, :] if i < 2 else spare[:, (i - 2) * 1024:(i - 1) * 1024]), i
            i = (n - NCA) % 4
            return (stage[:, i, :] if i < 2 else pr.rearrange("p s h n -> p (s h n)") if i == 2
                    else spare[:, 1024:2048]), i

        def tile_loop(eng, step):
            for t in range(-1, WINDOW + 2):
                step(t, t % 4, None)
            with eng.Fori(1, (TILES - 3) // WINDOW) as i:
                for j in range(WINDOW):
                    step(i * WINDOW + (2 + j), (2 + j) % 4, (i, j))
            for t in range(TILES - 1, TILES + 2):
                step(t, t % 4, None)

        def runs(t):
            return not isinstance(t, int) or 0 <= t < TILES

        def back(n):
            if n < 24:
                return xmT_t[:, n // 6, (n % 6) * D:(n % 6 + 1) * D].bitcast(F32)
            return rows_g[:, n - 24, :]

        def chunk_split(n):
            c, (src, _) = CHUNKS_A[n], buffer(n)
            i = int(c[-1])
            if c.startswith("wq"):
                return src, wq[0][:, i, :], wq[1][:, i, :]
            if c.startswith("ff1"):
                w = [t.rearrange("p k (h n) -> p (k h) n", h=2)[:, :, 256 * i:256 * i + 256] for t in wf1]
                return src.rearrange("p (k n) -> p k n", k=4), w[0], w[1]
            w = [t[:, 4 * i:4 * i + 4, :] for t in (wf2 if c.startswith("ff2") else wo)]
            return src.rearrange("p (k n) -> p k n", k=4), w[0], w[1]

        def expert_split(c):
            dst = shared if c == 0 else experts[:, (c - 1) * 2048:c * 2048].rearrange("p (m k n) -> p m k n", m=4, k=KT)
            return buffer(NCA + c)[0].rearrange("p (m k n) -> p m k n", m=2, k=KT), dst

        def chunk_loads(n):
            s, _ = buffer(n)
            if n >= NCA:
                c = n - NCA
                s = s.rearrange("p (m k n) -> p m k n", m=2, k=KT)
                pair = (sh_up_w, sh_down_w) if c == 0 else (up_w[c - 1], down_w[c - 1])
                return [(s[:, m], w.rearrange("(k p) n -> p k n", p=P)) for m, w in enumerate(pair)]
            name = CHUNKS_A[n]
            if name == "wkv":
                return [(s[:, 0:KT * P].rearrange("p (k n) -> p k n", k=KT), Wkv.rearrange("(k p) n -> p k n", p=P))]
            i = int(name[-1])
            if name.startswith("wq"):
                return [(s, Wq[i * P:(i + 1) * P, :])]
            if name.startswith("ff1"):
                src = Wff1.rearrange("(k p) (h n) -> p k h n", p=P, h=2)[:, :, :, 256 * i:256 * i + 256]
                dst = s.rearrange("p (k h n) -> p k h n", k=KT, h=2)
                return [(dst[:, k], src[:, k]) for k in range(KT)]
            w = Wff2 if name.startswith("ff2") else Wo
            return [(s.rearrange("p (k n) -> p k n", k=4), w.rearrange("(k p) n -> p k n", p=P)[:, 4 * i:4 * i + 4, :])]

        def stage_value(n):
            return 16 * sum(len(chunk_loads(m)) for m in range(n + 1) if buffer(m)[1] == buffer(n)[1])

        def landed(eng, n):
            eng.wait_ge(stage_full[buffer(n)[1]], stage_value(n))

        def split(eng, n):
            eng.wait_ge(chunk_split_done[n] if n < NCA else ring_ready, 1 if n < NCA else n - NCA + 1)

        def halves(bank_ap, two):
            return bank_ap[:, :].rearrange("p (a n) -> p a n", a=two)

        @block.sync
        def _(sp):
            def load_x(g):
                sp.dma_start(xs[:, 2 * g:2 * g + 2, :], x[2 * g:2 * g + 2].rearrange("b p d -> p b d")
                             ).then_inc(x_in[g], 16)

            def load_ctx(g):
                if g > 0:
                    sp.wait_ge(cnorm_done, g)
                sp.dma_start(ct[:, :, :], ctx_in[2 * g:2 * g + 2].rearrange("b p d -> p b d")
                             ).then_inc(ctx_loaded, 16)

            def load_chunk(n):
                buf = buffer(n)[1]
                before = [m for m in range(n) if buffer(m)[1] == buf]
                if before:
                    split(sp, before[-1])
                for dst, src in chunk_loads(n):
                    sp.dma_start(dst, src).then_inc(stage_full[buf], 16)

            load_ctx(0)
            load_x(0)
            for n in range(NCA):
                load_chunk(n)
                if n == EARLY - 1:
                    for g in range(1, NG):
                        load_x(g)
                    load_ctx(1)
            sp.wait_ge(bias_split, 2)
            for a in range(2):
                for at, r in ((0, slice(5, 5 + NE)), (NE, slice(33, 33 + NE)), (2 * NE, slice(32, 33))):
                    sp.dma_start(bias_rows[a, at:at + r.stop - r.start],
                                 xmT[a][r, 0, (NB - 2) * P:NB * P].bitcast(F32)).then_inc(bias_stored, 16)
            load_ctx(2)
            load_chunk(NCA)
            load_chunk(NCA + 1)
            for g in range(NG - 1):
                sp.wait_ge(x1norm_done, g + 1)
                sp.dma_start(norm_rows[g * GT:(g + 1) * GT].rearrange("(b p) d -> p b d", p=P), xn[:, 0:2, :]
                             ).then_inc(rows_stored, 16)
                if g + 3 < NG:
                    load_ctx(g + 3)
            sp.wait_ge(bias_stored, 16 * 6)
            sp.wait_ge(shared_zeroed, 1)
            for a in range(2):
                sp.dma_start(shared_brow[32 * a:32 * a + 1, :].bitcast(F32), bias_rows[a, 2 * NE:2 * NE + 1]
                             ).then_inc(shared_brow_in, 16)
            sp.wait_ge(pT_filled, NG * NU)
            load_chunk(NCA + 2)
            sp.wait_ge(dn_filled, USE_LT + 1)
            load_chunk(NCA + 3)
            load_chunk(NCA + 4)
            sp.wait_ge(brow_zeroed, 1)
            for a in range(2):
                sp.dma_start(brow[32 * a:32 * a + 1, :].bitcast(F32),
                             bias_rows[a, 0:2 * NE].rearrange("(o r) d -> o (r d)", o=1)).then_inc(brow_in, 16)
            for c in range(5, NPOS):
                load_chunk(NCA + c)
            for t in range(TILES):
                sp.wait_ge(y_copied, t + 1)
                sp.dma_start(slot_rows[t * P:(t + 1) * P], ys[:, t % 4, :]).then_inc(y_stored[t % 4], 16)
            for s in range(STEPS):
                sp.wait_ge(back_added, 2 * min(TPS * (s + 1), NTS))
                if s == STEPS - 1:
                    sp.wait_ge(dn_freed, USE_DENSE + NE)
                sp.dma_start(out[TPS * s:TPS * (s + 1)].rearrange("b p d -> p b d"), xs[:, TPS * s:TPS * (s + 1), :]
                             ).then_inc(written, 16)
            sp.wait_ge(written, 16 * STEPS)

        @block.gpsimd
        def _(pool):
            pool.memset(ident[:, :], 0.0).then_inc(ident_done, 1)
            pool.wait_ge(ident_done, 1)
            pool.affine_select(out=ident[:, :], in_=ident[:, :], compare_op=ALU.not_equal, fill=1.0, base=0,
                               pattern=[[-1, P]], channel_multiplier=1).then_inc(ident_done, 1)

            pool.dma_start(dbrow[0:1, :], sh_down_b.rearrange("(a n) -> a n", a=1)).then_inc(dbrow_in, 16)
            pool.dma_start(dbrow[1:NPOS, :], down_b).then_inc(dbrow_in, 16)
            for e in range(NE):
                last = pool.memset(rio[:, :, e:e + 1], float(NE - e))
            last.then_inc(rio_done, 1)

            def split_lo(n):
                src, hi, lo = chunk_split(n)
                pool.wait_ge(chunk_hi_done, n)
                pool.tensor_tensor(lo, src, hi.bitcast(F32), ALU.subtract).then_inc(chunk_split_done[n], 1)

            def transposed_lo(dst, count, ready):
                pool.wait_ge(tfh_done, count)
                pool.tensor_tensor(dst[1][:, :, :], tf[:, :, :], dst[0][:, :, :].bitcast(F32), ALU.subtract
                                   ).then_inc(ready, 1)

            def iteration(g, first=False, last=False):
                for s in range(NU):
                    u = g * NU + s
                    pool.wait_ge(rden_done, u + 1)
                    pool.tensor_tensor(pr[:, s % 2], pr[:, s % 2],
                                       rden[:, s % 2, :].unsqueeze(2).broadcast_to((P, 4, P)),
                                       ALU.mult).then_inc(probs_ready, 1)
                    pool.wait_ge(uh_done, u + 1)
                    pool.tensor_tensor(uT[1][:, s % 2, :], uf[:, :], uT[0][:, s % 2, :].bitcast(F32),
                                       ALU.subtract).then_inc(u_ready, 1)
                    if s == 6 and not last:
                        transposed_lo(cnT, g * 2 + 3, cnT_ready)
                    if first:
                        for n in CHUNK_SLOT.get(s, []):
                            split_lo(n)
                if not last:
                    transposed_lo(xnT, g * 2 + 4, xnT_ready)

            transposed_lo(cnT, 1, cnT_ready)
            transposed_lo(xnT, 2, xnT_ready)
            split_lo(2)
            iteration(0, first=True)
            with pool.Fori(1, NG - 1) as g:
                iteration(g)
            iteration(NG - 1, last=True)

            pool.wait_ge(xnT_ready, NG)
            pool.iota(iota_lo, [[1, P]], base=0, channel_multiplier=0, allow_small_or_imprecise_dtypes=True)
            pool.iota(iota_tile, [[1, 40]], base=0, channel_multiplier=0, allow_small_or_imprecise_dtypes=True)
            pool.iota(token, [[P, NTS]], base=0, channel_multiplier=1, allow_small_or_imprecise_dtypes=True
                      ).then_inc(sort_consts, 1)

            def split_expert(c):
                src, dst = expert_split(c)
                landed(pool, NCA + c)
                if c < 2:
                    for m in range(2):
                        done = pool.tensor_scalar(dst[:, 2 * m], src[:, m], 1.0, None, ALU.mult)
                    done.then_inc(ring_hi_done, 1)
                pool.wait_ge(ring_hi_done, c + 1)
                for m in range(2):
                    done = pool.tensor_tensor(dst[:, 2 * m + 1], src[:, m], dst[:, 2 * m].bitcast(F32), ALU.subtract)
                done.then_inc(ring_ready, 1)

            pool.wait_ge(mix_filled, mix_index("QP3", NG - 1, False, True) + 1)
            pool.memset(shared_brow.bitcast(F32), 0.0).then_inc(shared_zeroed, 1)
            split_expert(0)
            pool.wait_ge(mix_filled, mix_index("FF7", NG - 1, False, True) + 1)
            split_expert(1)
            pool.wait_ge(ff2_done, NG * NU)
            pool.wait_ge(wo_done, NG * NU)
            pool.memset(ones.bitcast(F32), 1.0)
            pool.memset(brow.bitcast(F32), 0.0).then_inc(brow_zeroed, 1)
            pool.memset(before.bitcast(F32), 1.0).then_inc(sort_consts, 1)
            pool.wait_ge(sort_consts, 2)
            pool.affine_select(out=before, in_=before.bitcast(F32), compare_op=ALU.is_gt, fill=0.0,
                               base=0, pattern=[[1, P]], channel_multiplier=-1).then_inc(sort_consts, 1)
            for c in range(2, NPOS):
                split_expert(c)
            pool.wait_ge(rows_stored, 16 * (NG - 1))
            pool.wait_ge(sorted_done, 1)
            for t in range(TILES):
                if t >= 4:
                    pool.wait_ge(gT_filled, t - 3)
                pool.indirect_dma_start(rows_g[:, t % 4, :], None, norm_rows[:, :],
                                        bass.IndirectOffsetOnAxis(ap=slot_token[:, t:t + 1], axis=0)
                                        ).then_inc(gathered[t % 4], 16)
            pool.wait_ge(gT_filled, TILES)
            for i in range(4):
                pool.wait_ge(y_stored[i], 16 * len(range(i, TILES, 4)))
            for t in range(NTS):
                if t >= 3:
                    pool.wait_ge(back_in[t % 3], 32 * (t // 3))
                for c in range(2):
                    pool.indirect_dma_start(back(2 * t + c), None, slot_rows[:, :],
                                            bass.IndirectOffsetOnAxis(ap=token_slot[:, c * NTS + t:c * NTS + t + 1],
                                                                      axis=0)).then_inc(back_in[t % 3], 16)

        @block.scalar
        def _(act):
            for i, v in enumerate((ln_g, ln_b, cln_g, cln_b, sh_up_b)):
                act.dma_start(rows[i:i + 1, :], v.rearrange("(a n) -> a n", a=1)).then_inc(rows_in, 16)
            act.dma_start(rows[5:5 + NE, :], up_b).then_inc(rows_in, 16)
            act.dma_start(rows[5 + NE:NROW, :], gate_w).then_inc(rows_in, 16)
            for i, v in enumerate((g_xattn, g_ffn)):
                act.dma_start(gates_in[:, i:i + 1], v.rearrange("(a n) -> a n", a=1).broadcast_to((P, 1))
                              ).then_inc(gates_loaded, 16)
            act.wait_ge(gates_loaded, 32)
            act.activation(gates[:, :], gates_in[:, :], ACT.Tanh).then_inc(gates_done, 1)

            def transposed_hi(name, g, first, last, dst):
                act.wait_ge(mix_freed, mix_index(name, g, first, last) + 1)
                act.activation(dst[:, :, :], tf[:, :, :], ACT.Copy).then_inc(tfh_done, 1)

            def keys_values_hi(g, first, last):
                b = mix_ps[mix_bank("K", g, first, last)]
                act.wait_ge(mix_filled, mix_index("K", g, first, last) + 1)
                for a in range(2):
                    r = slice(DH * a, DH * a + DH)
                    done = act.activation(kz[0][r, :, a, :], b[r, 0:GT].rearrange("p (b n) -> p b n", b=2),
                                          ACT.Copy, scale=DH ** -0.5)
                done.then_inc(kh_done, 1)
                b = mix_ps[mix_bank("V", g, first, last)]
                act.wait_ge(mix_filled, mix_index("V", g, first, last) + 1)
                act.activation(vv[0][:, :, :], halves(b, 2)[:, :, 0:P], ACT.Copy).then_inc(vh_done, 1)

            def queries_hi(pair, g, first, last):
                b = mix_ps[mix_bank(f"QP{pair}", g, first, last)]
                act.wait_ge(mix_filled, mix_index(f"QP{pair}", g, first, last) + 1)
                act.activation(q[0][:, 2 * pair:2 * pair + 2, :], halves(b, 2), ACT.Copy).then_inc(qh_done, 1)

            def attended_hi(u, very_first):
                act.wait_ge(pv_filled, u + 1)
                if not very_first:
                    act.wait_ge(wo_done, u)
                v = pv_ps[:, :].rearrange("p (m a n) -> p m a n", m=2, a=2)
                for a in range(2):
                    r = slice(DH * a, DH * a + DH)
                    done = act.activation(oT[0][r, :, :], v[r, :, a, :], ACT.Copy)
                done.then_inc(oh_done, 1)

            def probs_hi(u, very_first):
                act.wait_ge(pT_filled, u + 1)
                if not very_first:
                    act.wait_ge(pv_filled, u)
                act.activation(pT[0][:, :], t_ps[:, :], ACT.Copy).then_inc(pTh_done, 1)

            def iteration(g, first=False, last=False):
                for s in range(NU + 2):
                    u = g * NU + s
                    if s >= 2:
                        attended_hi(u - 2, first and s == 2)
                    if 1 <= s <= NU:
                        act.wait_ge(mix_freed, mix_index(f"FF{s - 1}", g, first, last) + 1)
                        if not (first and s < 3):
                            act.wait_ge(ff2_done, u - 2)
                        act.activation(uT[0][:, (s - 1) % 2, :], uf[:, :], ACT.Copy).then_inc(uh_done, 1)
                    if s < NU:
                        act.wait_ge(nmax_done, u + 1)
                        if not (first and s < 2):
                            act.wait_ge(pT_filled, u - 1)
                        for h in range(4):
                            done = act.activation(pr[:, s % 2, h, :], sc_ps[s % 2][:, h * P:(h + 1) * P], ACT.Exp,
                                                  bias=nmax[:, s % 2, h:h + 1], accum_out=den[:, s % 2, h:h + 1])
                        done.then_inc(exp_done, 1)
                    if first:
                        for n in CHUNK_SLOT.get(s, []):
                            split_hi(n)
                    if s == 0:
                        queries_hi(2, g, first, last)
                    if s == 2:
                        queries_hi(3, g, first, last)
                    if 1 <= s <= NU:
                        probs_hi(u - 1, first and s == 1)
                    if s < NU:
                        b = mix_ps[mix_bank(f"FF{s}", g, first, last)]
                        act.wait_ge(mix_filled, mix_index(f"FF{s}", g, first, last) + 1)
                        if not (first and s == 0):
                            act.wait_ge(u1_done, u)
                        act.activation(th[:, :], b[:, GT:2 * GT], ACT.Tanh, scale=0.5).then_inc(tanh_done, 1)
                    if s == 6 and not last:
                        transposed_hi("TXc", g, first, last, cnT[0])
                    if s == NU and not last:
                        transposed_hi("TXx", g, first, last, xnT[0])
                        keys_values_hi(g, first, last)
                if not last:
                    queries_hi(0, g, first, last)
                    queries_hi(1, g, first, last)

            def split_hi(n):
                src, hi, _ = chunk_split(n)
                landed(act, n)
                act.activation(hi, src, ACT.Copy).then_inc(chunk_hi_done, 1)

            split_hi(1)
            split_hi(2)
            transposed_hi("TXc", None, False, False, cnT[0])
            transposed_hi("TXx", None, False, False, xnT[0])
            keys_values_hi(None, False, False)
            split_hi(3)
            queries_hi(0, None, False, False)
            queries_hi(1, None, False, False)
            iteration(0, first=True)
            with act.Fori(1, NG - 1) as g:
                iteration(g)
            iteration(NG - 1, last=True)

            def up_bias(pos):
                act.activation(bias[:, :, :], cols[:, :, bass.ds(pos + 4, 1)], ACT.Copy).then_inc(bias_done, 1)

            def hidden_hi(step, parity, pos, n):
                act.wait_ge(bias_done, pos + 1)
                for m in range(KT):
                    act.wait_ge(up_filled, step * KT + (m + 1))
                    if not (isinstance(step, int) and step == 0):
                        act.wait_ge(h_ready, step * KT + (m - KT + 1))
                    act.activation(hf[:, m, 0:n], up_ps[2 * parity + m][:, 0:n], ACT.Silu,
                                   bias=bias[:, m, :]).then_inc(silu_done, 1)
                    act.wait_ge(silu_done, step * KT + (m + 1))
                    if m == 0:
                        if isinstance(step, int):
                            if step >= 2:
                                act.wait_ge(dn_filled, USE_DOWN[step - 2] + 2 if step < 6 else USE_DENSE + step - 5)
                        else:
                            act.wait_ge(dn_filled, step + (USE_DENSE - 5))
                    act.activation(hh[:, parity, 0, m, 0:n], hf[:, m, 0:n], ACT.Copy).then_inc(hh_done, 1)

            act.wait_ge(cols_done, 1)
            up_bias(0)
            act.wait_ge(shifted_done, 1)
            act.activation(ga[:, 0:NTS, :], gb[:, 0:NTS, :], ACT.Exp).then_inc(gexp_done, 1)
            act.wait_ge(rows_stored, 16 * (NG - 1))

            def expert_hi(c):
                src, dst = expert_split(c)
                landed(act, NCA + c)
                act.activation(dst[:, 0::2], src, ACT.Copy).then_inc(ring_hi_done, 1)

            hidden_hi(0, 0, 0, ST)
            act.wait_ge(wo_done, NG * NU)
            act.wait_ge(ring_hi_done, 2)
            expert_hi(2)
            expert_hi(3)
            hidden_hi(1, 1, 0, ST)
            for c in (4, 5, 6):
                expert_hi(c)
            hidden_hi(2, 0, 0, ST)
            for c in (7, 8):
                expert_hi(c)

            def tile_step(t, c, loop):
                if runs(t + 1):
                    act.wait_ge(gT_filled, t + 2)
                    if not (isinstance(t, int) and t < 1):
                        act.wait_ge(tile_up_filled, t)
                    act.activation(xg[0][:, (c + 1) % 2], halves(bank[(c + 1) % 2], 4)[:, 0:2, :], ACT.Copy
                                   ).then_inc(xgh_done, 1)
                if runs(t):
                    act.wait_ge(tile_up_filled, t + 1)
                    if not (isinstance(t, int) and t < 2):
                        act.wait_ge(hT_filled, t - 1)
                    act.activation(hs[:, c % 2, :], bank[2 + c % 2][:, 0:HID], ACT.Silu).then_inc(tile_silu_done, 1)
                if loop is None and t == 3:
                    act.wait_ge(shifted_done, 2)
                    act.activation(ga[:, NTS:NB, :], gb[:, NTS:NB, :], ACT.Exp).then_inc(gexp_done, 1)
                if runs(t - 1):
                    act.wait_ge(hT_filled, t)
                    if not (isinstance(t, int) and t < 3):
                        act.wait_ge(tile_down_filled, t - 2)
                    act.activation(hsT[0][(c + 1) % 2][:, :, :], halves(bank[4 + (c + 1) % 2], 4)[:, 0:2, :], ACT.Copy
                                   ).then_inc(hTh_done, 1)

            tile_loop(act, tile_step)
            hidden_hi(3, 1, 0, ST)
            up_bias(1)
            hidden_hi(STEPS, 0, 1, GT)
            up_bias(2)
            hidden_hi(STEPS + 1, 1, 2, GT)
            with act.Fori(0, NE // 2 - 1) as i:
                for j in range(2):
                    up_bias(i * 2 + (3 + j))
                    hidden_hi(i * 2 + (STEPS + 2 + j), j, i * 2 + (3 + j), GT)

        @block.vector
        def _(dve):
            def norm_step(call, k, lo, hi, g_ctx, g_x, g_x1, after):
                c = slice(lo, hi)
                if k == 0:
                    if after:
                        dve.wait_ge(*after)
                else:
                    dve.wait_ge(ln_step, ln_base(call) + k)
                if k < 3:
                    tiles = [None if g_ctx is None else [ct[:, i, :] for i in range(2)],
                             None if g_x is None else x_tiles(g_x), None if g_x1 is None else x_tiles(g_x1)][k]
                    if tiles:
                        for i, t in enumerate(tiles):
                            done = dve.bn_stats(bn[:, 2 * k + i, :], t)
                    else:
                        done = dve.memset(rt[:, c], 0.0)
                elif k == 3:
                    dve.tensor_tensor(mean[:, c], bn[:, c, 1], bn[:, c, 4], ALU.add)
                    dve.tensor_tensor(rt[:, c], bn[:, c, 1], bn[:, c, 4], ALU.subtract)
                    done = dve.tensor_tensor(var[:, c], bn[:, c, 2], bn[:, c, 5], ALU.add)
                elif k == 4:
                    done = dve.tensor_tensor(rt[:, c], rt[:, c], rt[:, c], ALU.mult)
                elif k == 5:
                    done = dve.scalar_tensor_tensor(var[:, c], rt[:, c], D / 4.0, var[:, c], ALU.mult, ALU.add)
                elif k == 6:
                    dve.tensor_scalar(mean[:, c], mean[:, c], 0.5, None, ALU.mult)
                    for at, a, b in ((slice(0, 2), 1.0, EPS), (slice(2, 4), 1.0 + EPS, EPS * EPS), (slice(4, 6), 1.0, EPS)):
                        if lo <= at.start < hi:
                            done = dve.tensor_scalar(var[:, at], var[:, at], a / D, b, ALU.mult, ALU.add)
                elif k == 7:
                    done = dve.tensor_scalar(rt[:, c].bitcast(I32), var[:, c].bitcast(I32), 1, None,
                                             ALU.logical_shift_right)
                elif k == 8:
                    done = dve.tensor_scalar(ry[:, c].bitcast(I32), rt[:, c].bitcast(I32), -1.0, float(RSQRT_GUESS),
                                             ALU.mult, ALU.add)
                elif k % 3 == 0:
                    done = dve.tensor_tensor(rt[:, c], ry[:, c], ry[:, c], ALU.mult)
                elif k % 3 == 1:
                    done = dve.scalar_tensor_tensor(rt[:, c], rt[:, c], -0.5, var[:, c], ALU.mult, ALU.mult)
                else:
                    done = dve.scalar_tensor_tensor(ry[:, c], rt[:, c], 1.5, ry[:, c], ALU.add, ALU.mult)
                done.then_inc(ln_step, 1)

            def norm_apply(call, tiles, dst, col, done):
                dve.wait_ge(ln_step, ln_base(call) + LN_STEPS)
                for i, t in enumerate(tiles):
                    last = dve.tensor_scalar(dst[:, i, :], t, mean[:, col + i:col + i + 1], ry[:, col + i:col + i + 1],
                                             ALU.subtract, ALU.mult)
                last.then_inc(done, 1)

            def x_tiles(g):
                return [xs[:, bass.ds(g * 2 + i, 1), :].rearrange("p a n -> p (a n)") for i in range(2)]

            def transposed(name, g, first, last, gn):
                isx = name == "TXx"
                col = 0 if isx else 2
                b = mix_ps[mix_bank(name, g, first, last)]
                n = mix_index(name, g, first, last)
                dve.wait_ge(mix_filled, n + 1)
                if isx:
                    dve.wait_ge(cnT_ready, gn + 1)
                elif g is not None:
                    dve.wait_ge(xnT_ready, gn)
                for k in range(KT):
                    done = dve.tensor_scalar(tf[:, k, :], b[:, k * GT:(k + 1) * GT], cols[:, k, col:col + 1],
                                             cols[:, k, col + 1:col + 2], ALU.mult, ALU.add)
                done.then_inc(mix_freed, 1)

            def keys_values_lo(g, first, last, gn):
                b = mix_ps[mix_bank("K", g, first, last)]
                dve.wait_ge(kh_done, gn + 1)
                for a in range(2):
                    r = slice(DH * a, DH * a + DH)
                    done = dve.scalar_tensor_tensor(
                        kz[1][r, :, a, :], b[r, 0:GT].rearrange("p (b n) -> p b n", b=2), DH ** -0.5,
                        kz[0][r, :, a, :].bitcast(F32), ALU.mult, ALU.subtract)
                done.then_inc(mix_freed, 1)
                b = mix_ps[mix_bank("V", g, first, last)]
                dve.wait_ge(vh_done, gn + 1)
                dve.tensor_tensor(vv[1][:, :, :], halves(b, 2)[:, :, 0:P], vv[0][:, :, :].bitcast(F32), ALU.subtract
                                  ).then_inc(mix_freed, 1)

            def queries_lo(pair, g, first, last, gn):
                b = mix_ps[mix_bank(f"QP{pair}", g, first, last)]
                dve.wait_ge(qh_done, gn * 4 + (pair + 1))
                dve.tensor_tensor(q[1][:, 2 * pair:2 * pair + 2, :], halves(b, 2),
                                  q[0][:, 2 * pair:2 * pair + 2, :].bitcast(F32), ALU.subtract).then_inc(mix_freed, 1)

            def early_lo(n):
                src, hi, lo = chunk_split(n)
                dve.wait_ge(chunk_hi_done, n)
                dve.tensor_tensor(lo, src, hi.bitcast(F32), ALU.subtract).then_inc(chunk_split_done[n], 1)

            for t in kz + gw:
                last = dve.memset(t[:].bitcast(F32), 0.0)
            last.then_inc(zeros_done, 1)
            dve.wait_ge(zeros_done, 1)
            dve.wait_ge(ctx_loaded, 16)
            dve.wait_ge(x_in[0], 16)
            for k in range(LN_STEPS):
                norm_step(0, k, 0, 4, 0, 0, None, None)
            norm_apply(0, [ct[:, i, :] for i in range(2)], xn[:, 2:4, :], 0, cnorm_done)
            norm_apply(0, x_tiles(0), xn[:, 0:2, :], 2, xnorm_done)
            dve.wait_ge(cols_filled, 1)
            dve.tensor_copy(cols[:, :, :], bank[0][:, 0:KT * NROW].rearrange("p (k n) -> p k n", k=KT)
                            ).then_inc(cols_done, 1)
            dve.wait_ge(cols_done, 1)
            landed(dve, 0)
            kv = stage[:, 0, 0:KT * P].rearrange("p (k a n) -> p k a n", k=KT, a=2)
            both = [(w, a, slice(DH * h, DH * h + DH)) for w, a in ((wkk, 0), (wv, 1)) for h in range(2)]
            for w, a, r in both:
                last = dve.tensor_copy(w[0][:, :, r], kv[:, :, a, :])
            last.then_inc(kv_hi_done, 1)
            dve.wait_ge(kv_hi_done, 1)
            for w, a, r in both:
                last = dve.tensor_tensor(w[1][:, :, r], kv[:, :, a, :], w[0][:, :, r].bitcast(F32), ALU.subtract)
            last.then_inc(chunk_split_done[0], 1)
            transposed("TXc", None, False, False, 0)
            transposed("TXx", None, False, False, 0)
            early_lo(1)
            keys_values_lo(None, False, False, 0)
            queries_lo(0, None, False, False, 0)
            queries_lo(1, None, False, False, 0)
            early_lo(3)
            gate_cols = cols[:, :, 5 + NE:NROW]
            dve.tensor_copy(gw[0][:, :, 0:NE], gate_cols).then_inc(gw_done, 1)
            dve.wait_ge(gw_done, 1)
            dve.tensor_tensor(gw[1][:, :, 0:NE], gate_cols, gw[0][:, :, 0:NE].bitcast(F32), ALU.subtract
                              ).then_inc(gw_done, 1)

            dve.wait_ge(dbrow_in, 32)
            place = [t[:, 0, (NB - 2) * P:NB * P] for t in xmT]
            for r in (slice(0, 5 + NE), slice(32, 33 + NE)):
                done = dve.tensor_copy(place[0][r, :], all_rows[r, :])
            done.then_inc(bias_split, 1)
            dve.wait_ge(bias_split, 1)
            for r in (slice(0, 5 + NE), slice(32, 33 + NE)):
                done = dve.tensor_tensor(place[1][r, :], all_rows[r, :], place[0][r, :].bitcast(F32), ALU.subtract)
            done.then_inc(bias_split, 1)

            def attended_lo(u):
                dve.wait_ge(oh_done, u + 1)
                v = pv_ps[:, :].rearrange("p (m a n) -> p m a n", m=2, a=2)
                for a in range(2):
                    r = slice(DH * a, DH * a + DH)
                    done = dve.tensor_tensor(oT[1][r, :, :], v[r, :, a, :], oT[0][r, :, :].bitcast(F32), ALU.subtract)
                done.then_inc(o_ready, 1)

            def x1_split(g, b):
                at = bass.ds(g * GT, GT)
                dve.tensor_scalar(xmT[0][:, :, at], halves(b, KT), 1.0, None, ALU.mult).then_inc(xmh_done, 1)
                dve.wait_ge(xmh_done, g + 1)
                return dve.tensor_tensor(xmT[1][:, :, at], halves(b, KT), xmT[0][:, :, at].bitcast(F32), ALU.subtract)

            def iteration(g, first=False, last=False):
                call = g + 1
                lo, hi = 4 if last else 0, 4 if first else 6
                at_step = 0

                def small_step():
                    nonlocal at_step
                    if at_step < LN_STEPS:
                        norm_step(call, at_step, lo, hi, None if last else g + 1, None if last else g + 1,
                                  None if first else g - 1, (xnorm_done, g + 1))
                    at_step += 1

                for s in range(NU + 2):
                    u = g * NU + s
                    if s < NU:
                        dve.wait_ge(scores_filled, u + 1)
                        if not (first and s < 2):
                            dve.wait_ge(exp_done, u - 1)
                        dve.tensor_reduce(nmax[:, s % 2, :], halves(sc_ps[s % 2], 4), AX.X, ALU.max, negate=True
                                          ).then_inc(nmax_done, 1)
                    if s == 0 and not last:
                        dve.wait_ge(ctx_loaded, g * 16 + 32)
                        if first:
                            dve.wait_ge(x_in[1], 16)
                    if s == 0 and not first:
                        dve.wait_ge(x1_done, g)
                    if s > 0:
                        small_step()
                    if s >= 2:
                        attended_lo(u - 2)
                    if s > 0:
                        small_step()
                    if s == 0:
                        queries_lo(2, g, first, last, g)
                    if s == 2:
                        queries_lo(3, g, first, last, g)
                    if s == 5 and not first:
                        dve.wait_ge(mix_filled, mix_index("X1T", g, first, last) + 1)
                        x1_split(g - 1, mix_ps[mix_bank("X1T", g, first, last)]).then_inc(mix_freed, 1)
                    if s == 6 and not last:
                        transposed("TXc", g, first, last, g + 1)
                    if s == 7 and not first:
                        b = mix_ps[mix_bank("GL", g, first, last)]
                        dve.wait_ge(mix_filled, mix_index("GL", g, first, last) + 1)
                        dve.tensor_copy(lgT[:, bass.ds(g * GT - GT, GT)], b[0:NE, 0:GT]).then_inc(mix_freed, 1)
                    if s < NU:
                        dve.wait_ge(exp_done, u + 1)
                        if not (first and s < 2):
                            dve.wait_ge(probs_ready, u - 1)
                        dve.reciprocal(rden[:, s % 2, :], den[:, s % 2, :]).then_inc(rden_done, 1)
                    small_step()
                    if 1 <= s <= NU:
                        dve.wait_ge(pTh_done, u)
                        dve.tensor_tensor(pT[1][:, :], t_ps[:, :], pT[0][:, :].bitcast(F32), ALU.subtract
                                          ).then_inc(pT_ready, 1)
                    small_step()
                    if s < NU:
                        b = mix_ps[mix_bank(f"FF{s}", g, first, last)]
                        dve.wait_ge(tanh_done, u + 1)
                        dve.scalar_tensor_tensor(u1[:, :], th[:, :], 1.0, b[:, GT:2 * GT], ALU.add, ALU.mult
                                                 ).then_inc(u1_done, 1)
                        dve.wait_ge(u1_done, u + 1)
                        if not (first and s == 0):
                            dve.wait_ge(u_ready, u)
                        dve.scalar_tensor_tensor(uf[:, :], b[:, 0:GT], 0.5, u1[:, :], ALU.mult, ALU.mult
                                                 ).then_inc(mix_freed, 1)
                    if s == 4:
                        if not first:
                            norm_apply(call, x_tiles(g - 1), xn[:, 0:2, :], 4, x1norm_done)
                        if not last:
                            norm_apply(call, [ct[:, i, :] for i in range(2)], xn[:, 2:4, :], 0, cnorm_done)
                    if s == 7 and not last:
                        if not first:
                            dve.wait_ge(rows_stored, g * 16)
                        norm_apply(call, x_tiles(g + 1), xn[:, 0:2, :], 2, xnorm_done)
                    if s == NU and not last:
                        transposed("TXx", g, first, last, g + 1)
                        keys_values_lo(g, first, last, g + 1)
                if not last:
                    queries_lo(0, g, first, last, g + 1)
                    queries_lo(1, g, first, last, g + 1)
                dve.wait_ge(wo_done, g * NU + NU)
                at = xs[:, bass.ds(g * 2, 2), :]
                dve.scalar_tensor_tensor(at, halves(out_ps, 2), gates[:, 0:1], at, ALU.mult, ALU.add
                                         ).then_inc(x1_done, 1)

            dve.wait_ge(gates_done, 1)
            iteration(0, first=True)
            for g in range(2, NG):
                dve.wait_ge(x_in[g], 16)
            with dve.Fori(1, NG - 1) as g:
                iteration(g)
            iteration(NG - 1, last=True)

            links = 0

            def link(ins):
                nonlocal links
                links += 1
                ins.then_inc(link_done, 1)
                dve.wait_ge(link_done, links)

            def hidden_lo(step, parity, n):
                for m in range(KT):
                    dve.wait_ge(hh_done, step * KT + (m + 1))
                    dve.tensor_tensor(hh[:, parity, 1, m, 0:n], hf[:, m, 0:n], hh[:, parity, 0, m, 0:n].bitcast(F32),
                                      ALU.subtract).then_inc(h_ready, 1)

            def add_tiles(use, bank_of, t0, pos):
                dve.wait_ge(dn_filled, use + 1)
                dve.wait_ge(dn_freed, use)
                for i in range(2):
                    t = t0 + i
                    done = dve.scalar_tensor_tensor(
                        xs[:, t, :], dn_ps[bank_of % 4][:, i * D:(i + 1) * D],
                        comb[:, bass.ds(pos, 1), t:t + 1].rearrange("p a n -> p (a n)"), xs[:, t, :],
                        ALU.mult, ALU.add)
                done.then_inc(dn_freed, 1)

            def add_shared(j):
                for half in range(2):
                    add_tiles(USE_DOWN[j] + half, USE_DOWN[j] + half, TPS * j + 2 * half, 0)

            def add_dense(e, parity):
                add_tiles(e + USE_DENSE, USE_DENSE + parity, NTS, e + 1)

            def gate_logits(t0, t1, b, count, filled, copied):
                T, n = slice(t0, t1), t1 - t0
                dve.wait_ge(*filled)
                dve.tensor_copy(lg[:, T, :], b[:, 0:n * NE].rearrange("p (t e) -> p t e", t=n)).then_inc(copied[0], 1)
                dve.wait_ge(*copied)
                link(dve.tensor_reduce(g1[:, T], lg[:, T, :], AX.X, ALU.max))
                dve.tensor_tensor(gb[:, T, :], lg[:, T, :], per_tile(g1, t0, t1), ALU.subtract).then_inc(shifted_done, 1)
                dve.wait_ge(shifted_done, count)

            def per_tile(v, t0, t1):
                return v[:, t0:t1].unsqueeze(2).broadcast_to((P, t1 - t0, NE))

            def gate_first(t0, t1, count):
                T = slice(t0, t1)
                dve.wait_ge(gexp_done, count)
                link(dve.tensor_reduce(g2[:, T], ga[:, T, :], AX.X, ALU.add))
                link(dve.reciprocal(g3[:, T], g2[:, T]))
                link(dve.tensor_tensor(ga[:, T, :], ga[:, T, :], per_tile(g3, t0, t1), ALU.mult))
                link(dve.tensor_reduce(g1[:, T], ga[:, T, :], AX.X, ALU.max))
                link(dve.tensor_tensor(gb[:, T, :], ga[:, T, :], per_tile(g1, t0, t1), ALU.is_equal))
                link(dve.tensor_tensor(gb[:, T, :], gb[:, T, :], rio[:, T, :], ALU.mult))
                link(dve.tensor_reduce(g3[:, T], gb[:, T, :], AX.X, ALU.max))
                link(dve.tensor_tensor(oh1[:, T, :], rio[:, T, :], per_tile(g3, t0, t1), ALU.is_equal))

            def gate_second(t0, t1):
                T = slice(t0, t1)
                link(dve.scalar_tensor_tensor(lg[:, T, :], oh1[:, T, :], -2.0, ga[:, T, :], ALU.mult, ALU.add))
                link(dve.tensor_reduce(g2[:, T], lg[:, T, :], AX.X, ALU.max))
                link(dve.tensor_tensor(gb[:, T, :], lg[:, T, :], per_tile(g2, t0, t1), ALU.is_equal))
                link(dve.tensor_tensor(gb[:, T, :], gb[:, T, :], rio[:, T, :], ALU.mult))
                link(dve.tensor_reduce(g3[:, T], gb[:, T, :], AX.X, ALU.max))
                link(dve.tensor_tensor(lg[:, T, :], rio[:, T, :], per_tile(g3, t0, t1), ALU.is_equal))

            def gate_weights(t0, t1):
                T = slice(t0, t1)
                link(dve.scalar_tensor_tensor(g3[:, T], g1[:, T], 1e-20, g2[:, T], ALU.add, ALU.add))
                link(dve.reciprocal(g3[:, T], g3[:, T]))
                link(dve.tensor_scalar(g3[:, T], g3[:, T], gates[:, 1:2], None, ALU.mult))
                dve.tensor_tensor(g1[:, T], g1[:, T], g3[:, T], ALU.mult)
                link(dve.tensor_tensor(g2[:, T], g2[:, T], g3[:, T], ALU.mult))

            gate_logits(0, NTS, dn_ps[USE_LT], 1, (dn_filled, USE_LT + 1), (dn_freed, USE_LT + 1))
            gate_first(0, NTS, 1)
            hidden_lo(0, 0, ST)
            gate_second(0, NTS)
            dve.memset(chosen[:, NTS * NE:].bitcast(F32), 0.0)
            dve.tensor_tensor(chosen[:, 0:NTS * NE].rearrange("p (t e) -> p t e", e=NE), oh1[:, 0:NTS, :],
                              lg[:, 0:NTS, :], ALU.add).then_inc(chosen_done, 1)
            hidden_lo(1, 1, ST)
            link(dve.memset(comb[:, 0, :], 1.0))
            link(dve.tensor_scalar(comb[:, 0, :], comb[:, 0, :], gates[:, 1:2], None, ALU.mult))
            add_shared(0)

            def last_norm(steps):
                for k in steps:
                    norm_step(NG + 1, k, 4, 6, None, None, NG - 1, (x1norm_done, NG - 1))

            last_norm(range(0, 6))

            dve.wait_ge(dn_filled, USE_RANK + 1)
            dve.wait_ge(sort_consts, 3)
            pos = dn_ps[USE_RANK % 4][:, 0:(NTS + 1) * NE].rearrange("p (t e) -> p t e", e=NE)
            a8, b8, c8 = small[:, 0:NE], small[:, NE:2 * NE], small[:, 2 * NE:3 * NE]
            link(dve.tensor_scalar(a8.bitcast(I32), pos[:, NTS, :], P - 1.0, None, ALU.add))
            link(dve.tensor_scalar(b8.bitcast(I32), a8.bitcast(I32), 7, None, ALU.logical_shift_right))
            link(dve.tensor_copy(c8, b8.bitcast(I32)))
            link(dve.tensor_copy(a8, c8))
            ends, other = a8, b8
            for d in (1, 2, 4):
                dve.tensor_copy(other[:, 0:d], ends[:, 0:d])
                link(dve.tensor_tensor(other[:, d:NE], ends[:, d:NE], ends[:, 0:NE - d], ALU.add))
                ends, other = other, ends
            link(dve.tensor_tensor(other, ends, c8, ALU.subtract))
            dve.scalar_tensor_tensor(rank[:, :, :], other.unsqueeze(1).broadcast_to((P, NTS, NE)), float(P),
                                     pos[:, 0:NTS, :], ALU.mult, ALU.add).then_inc(dn_freed, 1)
            dve.wait_ge(dn_freed, USE_RANK + 1)
            dve.tensor_tensor(slots8[:, 0:NTS, :], rank[:, :, :], oh1[:, 0:NTS, :], ALU.mult)
            link(dve.tensor_tensor(slots8[:, NTS:NCH, :], rank[:, :, :], lg[:, 0:NTS, :], ALU.mult))
            fslot, ilo, ihi, flo, fhi = [small[:, 32 + 32 * i:32 + 32 * i + NCH] for i in range(5)]
            link(dve.tensor_reduce(fslot, slots8, AX.X, ALU.add))
            link(dve.tensor_copy(token_slot, fslot))
            dve.tensor_scalar(ilo.bitcast(I32), token_slot, P - 1, None, ALU.bitwise_and)
            link(dve.tensor_scalar(ihi.bitcast(I32), token_slot, 7, None, ALU.logical_shift_right))
            dve.tensor_copy(flo, ilo.bitcast(I32))
            link(dve.tensor_copy(fhi, ihi.bitcast(I32)))

            def hots(w):
                eq = is_tile.rearrange("p (n c) -> p n c", n=WAVE)
                link(dve.tensor_tensor(eq, fhi[:, w * WAVE:(w + 1) * WAVE].unsqueeze(2).broadcast_to((P, WAVE, TCOLS)),
                                       iota_tile[:, 0:TCOLS].unsqueeze(1).broadcast_to((P, WAVE, TCOLS)), ALU.is_equal))
                dve.tensor_tensor(hi_hot[w], eq, token.unsqueeze(2).broadcast_to((P, WAVE, TCOLS)), ALU.mult)
                dve.tensor_tensor(lo_hot, flo[:, w * WAVE:(w + 1) * WAVE].unsqueeze(2).broadcast_to((P, WAVE, P)),
                                  iota_lo.unsqueeze(1).broadcast_to((P, WAVE, P)), ALU.is_equal).then_inc(hot_done, 1)

            hots(0)
            hidden_lo(2, 0, ST)
            add_shared(1)
            dve.wait_ge(wave_used, 1)
            hots(1)
            add_shared(2)
            gate_weights(0, NTS)
            link(dve.tensor_tensor(tile_cmp, iota_tile[0:1, :].unsqueeze(2).broadcast_to((1, 40, NE)),
                                   ends[0:1, :].unsqueeze(1).broadcast_to((1, 40, NE)), ALU.is_ge))
            link(dve.tensor_reduce(tile_expert, tile_cmp, AX.X, ALU.add))
            link(dve.tensor_scalar(tile_expert, tile_expert, NE - 1.0, None, ALU.min))
            by_window = tile_expert.rearrange("p (w k) -> p w k", k=WINDOW)
            link(dve.tensor_copy(pack, by_window[:, 0:NWIN, 0]))
            for k in range(1, WINDOW + 2):
                link(dve.scalar_tensor_tensor(pack, by_window[:, k // WINDOW:k // WINDOW + NWIN, k % WINDOW],
                                              float(1 << (SHIFT * k)), pack, ALU.mult, ALU.add))
            link(dve.tensor_copy(window, pack))
            dve.wait_ge(wave_used, 2)
            dve.tensor_copy(slot_token, bank[3][:, 0:TILES]).then_inc(sorted_done, 1)
            last_norm(range(6, LN_STEPS))
            norm_apply(NG + 1, x_tiles(NG - 1), ct[:, :, :], 4, x1norm_done)
            dve.wait_ge(dn_filled, USE_X1T + 1)
            dve.wait_ge(bias_stored, 16 * 6)
            x1_split(NG - 1, dn_ps[USE_X1T % 4]).then_inc(dn_freed, 1)

            def last_gate(t):
                if t == 1:
                    dve.wait_ge(last_logits_filled, 1)
                    dve.tensor_copy(last_lgT, bank[6][0:NE, D:2 * D]).then_inc(last_logits_copied, 1)
                if t == 2:
                    gate_logits(NTS, NB, bank[7][:, D:], 2, (last_logits_filled, 2), (last_logits_copied, 2))
                if t == 3:
                    gate_first(NTS, NB, 2)
                if t == 4:
                    gate_second(NTS, NB)
                if t == 5:
                    gate_weights(NTS, NB)
                    dve.tensor_tensor(oh1[:, NTS:NB, :], oh1[:, NTS:NB, :], per_tile(g1, NTS, NB), ALU.mult)
                    link(dve.tensor_tensor(lg[:, NTS:NB, :], lg[:, NTS:NB, :], per_tile(g2, NTS, NB), ALU.mult))
                    link(dve.tensor_tensor(comb[:, 1:NPOS, NTS:NB].rearrange("p e t -> p t e"), oh1[:, NTS:NB, :],
                                           lg[:, NTS:NB, :], ALU.add))

            def tile_step(t, c, loop):
                if runs(t + 1):
                    dve.wait_ge(xgh_done, t + 2)
                    dve.tensor_tensor(xg[1][:, (c + 1) % 2], halves(bank[(c + 1) % 2], 4)[:, 0:2, :],
                                      xg[0][:, (c + 1) % 2].bitcast(F32), ALU.subtract).then_inc(xg_ready, 1)
                if runs(t - 1):
                    dve.wait_ge(hTh_done, t)
                    dve.tensor_tensor(hsT[1][(c + 1) % 2][:, :, :], halves(bank[4 + (c + 1) % 2], 4)[:, 0:2, :],
                                      hsT[0][(c + 1) % 2][:, :, :].bitcast(F32), ALU.subtract).then_inc(hT_ready, 1)
                if runs(t - 2):
                    dve.wait_ge(tile_down_filled, t - 1)
                    b = (c + 2) % 4
                    if isinstance(t, int):
                        if t >= 6:
                            dve.wait_ge(y_stored[b], 16 * ((t - 2) // 4))
                    else:
                        i, j = loop
                        dve.wait_ge(y_stored[b], i * 16)
                    dve.tensor_copy(ys[:, b, :], bank[6 + c % 2][:, 0:D]).then_inc(y_copied, 1)
                if loop is None:
                    last_gate(t)

            tile_loop(dve, tile_step)
            hidden_lo(3, 1, ST)
            hidden_lo(STEPS, 0, GT)
            add_shared(3)

            def add_back(t, i=None):
                n = 2 * t
                for c in range(2):
                    if i is None:
                        dve.wait_ge(back_in[t % 3], 32 * (t // 3 + 1))
                        at, src, w = xs[:, t, :], back(n + c), (g1, g2)[c][:, t:t + 1]
                        dve.wait_ge(back_added, n + c) if n + c else None
                    else:
                        dve.wait_ge(back_in[t], i * 32 + 32)
                        at = xs[:, bass.ds(i * 3 + t, 1), :].rearrange("p a n -> p (a n)")
                        src = xmT_t[:, bass.ds(i, 1), (n + c) * D:(n + c + 1) * D].rearrange("p a n -> p (a n)").bitcast(F32)
                        w = (g1, g2)[c][:, bass.ds(i * 3 + t, 1)]
                        if n + c:
                            dve.wait_ge(back_added, i * 6 + (n + c))
                    dve.scalar_tensor_tensor(at, src, w, at, ALU.mult, ALU.add).then_inc(back_added, 1)

            hidden_lo(STEPS + 1, 1, GT)
            add_dense(0, 0)
            with dve.Fori(0, NE // 2 - 1) as i:
                for j in range(2):
                    hidden_lo(i * 2 + (STEPS + 2 + j), j, GT)
                    add_dense(i * 2 + (1 + j), (1 + j) % 2)
                for t in range(3):
                    add_back(t, i)
            add_dense(NE - 1, 1)
            for t in range(9, NTS):
                add_back(t)

        @block.tensor
        def _(pe):
            def matmul3(ps, wts, mov, first, last):
                pe.matmul(ps, wts[1], mov[0], start=first, stop=False, skip_group_check=True)
                pe.matmul(ps, wts[0], mov[0], start=False, stop=False, skip_group_check=True)
                return pe.matmul(ps, wts[0], mov[1], start=False, stop=last, skip_group_check=True)

            def mix(name, g, first, last):
                n = mix_index(name, g, first, last)
                if not (isinstance(n, int) and n < 3):
                    pe.wait_ge(mix_freed, n - 2)
                return mix_ps[mix_bank(name, g, first, last)]

            def transposes(b, tiles):
                for i in range(2):
                    for k in range(KT):
                        done = pe.transpose(b[:, k * GT + i * P:k * GT + (i + 1) * P], tiles[:, i, k * P:(k + 1) * P],
                                            ident[:, :])
                return done

            def norm_T(name, g, first, last, gn):
                b = mix(name, g, first, last)
                isx = name == "TXx"
                pe.wait_ge(xnorm_done if isx else cnorm_done, gn + 1)
                transposes(b, xn[:, 0:2] if isx else xn[:, 2:4]).then_inc(mix_filled, 1)

            def keys(g, first, last, gn):
                b = mix("K", g, first, last)
                pe.wait_ge(cnT_ready, gn + 1)
                for k in range(KT):
                    done = matmul3(b[:, 0:GT], [w[:, k, :] for w in wkk], [t[:, k, :] for t in cnT], k == 0, k == KT - 1)
                done.then_inc(mix_filled, 1)

            def values(g, first, last, gn):
                b = mix("V", g, first, last)
                for i in range(2):
                    for k in range(KT):
                        done = matmul3(b[:, i * GT:(i + 1) * GT], [t[:, k, i * P:(i + 1) * P] for t in cnT],
                                       [w[:, k, :].unsqueeze(1).broadcast_to((P, 2, P)) for w in wv],
                                       k == 0, k == KT - 1)
                done.then_inc(mix_filled, 1)

            def queries(pair, g, first, last, gn):
                b = mix(f"QP{pair}", g, first, last)
                pe.wait_ge(xnT_ready, gn + 1)
                for i in range(2):
                    m = 2 * pair + i
                    for k in range(KT):
                        done = matmul3(b[:, i * GT:(i + 1) * GT], [w[:, k, m * P:(m + 1) * P] for w in wq],
                                       [t[:, k, :] for t in xnT], k == 0, k == KT - 1)
                done.then_inc(mix_filled, 1)

            def logits(b, g):
                for k in range(KT):
                    done = matmul3(b[:, 0:GT], [w[:, k, :] for w in gw],
                                   [t[:, k, bass.ds(g * GT, GT)] for t in xmT], k == 0, k == KT - 1)
                return done

            def attend(u, s, very_first):
                pe.wait_ge(pT_ready, u + 1)
                if not very_first:
                    pe.wait_ge(o_ready, u)
                matmul3(pv_ps[:, :], [t[:, s % 2, :] for t in vv], [t[:, :] for t in pT], True, True
                        ).then_inc(pv_filled, 1)

            def project(u, s, last_of_group):
                pe.wait_ge(o_ready, u + 1)
                b = s % 2
                for m in range(2):
                    done = matmul3(out_ps[:, b * D:(b + 1) * D], [t[:, m, :] for t in oT],
                                   [w[:, 2 * (s // 2) + m, :] for w in wo], False, last_of_group)
                done.then_inc(wo_done, 1)

            def iteration(g, first=False, last=False):
                def chunk(n):
                    if first:
                        split(pe, n)

                for s in range(NU + 2):
                    u = g * NU + s
                    if s < NU:
                        if not (first and s < 2):
                            pe.wait_ge(exp_done, u - 1)
                        if s in (0, 2):
                            name = f"QP{s // 2}"
                            n = mix_index(name, None, False, False) if first else mix_index(name, g - 1, False, False)
                            pe.wait_ge(mix_freed, n + 1)
                        if s in (4, 6):
                            pe.wait_ge(mix_freed, mix_index(f"QP{s // 2}", g, first, last) + 1)
                        for i in range(2):
                            m = 2 * (s // 2) + i
                            done = matmul3(sc_ps[s % 2][:, i * GT:(i + 1) * GT],
                                           [t[:, m, (s % 2) * P:(s % 2 + 1) * P] for t in q],
                                           [t[:, s % 2, :, :] for t in kz], True, True)
                        done.then_inc(scores_filled, 1)
                    if 2 <= s <= NU:
                        attend(u - 2, s, first and s == 2)
                    if s == 0:
                        queries(2, g, first, last, g)
                    if s == 2:
                        queries(3, g, first, last, g)
                    if s == 5 and not first:
                        b = mix("X1T", g, first, last)
                        pe.wait_ge(x1norm_done, g)
                        transposes(b, xn[:, 0:2]).then_inc(mix_filled, 1)
                    if s == 6 and not last:
                        norm_T("TXc", g, first, last, g + 1)
                    if s == 7 and not first:
                        b = mix("GL", g, first, last)
                        pe.wait_ge(gw_done, 2)
                        pe.wait_ge(mix_freed, mix_index("X1T", g, first, last) + 1)
                        logits(b, g - 1).then_inc(mix_filled, 1)
                    if s < NU:
                        b = mix(f"FF{s}", g, first, last)
                        chunk([3, 6, 7, 10][s // 2])
                        for i in range(2):
                            for k in range(KT):
                                at = slice(i * FF + s * P, i * FF + (s + 1) * P)
                                done = matmul3(b[:, i * GT:(i + 1) * GT], [w[:, k, at] for w in wf1],
                                               [t[:, k, :] for t in xnT], k == 0, k == KT - 1)
                        done.then_inc(mix_filled, 1)
                    if s == NU and not last:
                        norm_T("TXx", g, first, last, g + 1)
                    if 1 <= s <= NU:
                        pe.wait_ge(probs_ready, u)
                        if not (first and s == 1):
                            pe.wait_ge(pT_ready, u - 1)
                        for h in range(4):
                            done = pe.transpose(t_ps[:, h * P:(h + 1) * P], pr[:, (s - 1) % 2, h, :], ident[:, :])
                        done.then_inc(pT_filled, 1)
                    if 2 <= s <= NU:
                        chunk([5, 9][(s - 2) // 4])
                        project(u - 2, s - 2, False)
                    if 1 <= s <= NU:
                        pe.wait_ge(u_ready, u)
                        chunk([4, 8][(s - 1) // 4])
                        if s == 1 and not first:
                            pe.wait_ge(x1_done, g)
                        for b in range(2):
                            done = matmul3(out_ps[:, b * D:(b + 1) * D],
                                           [t[:, (s - 1) % 2, b * P:(b + 1) * P] for t in uT],
                                           [w[:, s - 1, :] for w in wf2], s == 1 and b == 0, False)
                        done.then_inc(ff2_done, 1)
                if not last:
                    keys(g, first, last, g + 1)
                attend(g * NU + (NU - 1), NU - 1, False)
                if not last:
                    values(g, first, last, g + 1)
                    queries(0, g, first, last, g + 1)
                    queries(1, g, first, last, g + 1)
                project(g * NU + (NU - 1), NU - 1, True)

            pe.wait_ge(ident_done, 2)
            pe.wait_ge(rows_in, 16 * 7)
            for k in range(KT):
                done = pe.transpose(bank[0][:, k * NROW:(k + 1) * NROW], rows[:, k * P:(k + 1) * P],
                                    ident[0:NROW, 0:NROW])
            done.then_inc(cols_filled, 1)
            pe.wait_ge(zeros_done, 1)
            norm_T("TXc", None, False, False, 0)
            norm_T("TXx", None, False, False, 0)
            split(pe, 0)
            keys(None, False, False, 0)
            values(None, False, False, 0)
            split(pe, 1)
            split(pe, 2)
            queries(0, None, False, False, 0)
            queries(1, None, False, False, 0)
            iteration(0, first=True)
            with pe.Fori(1, NG - 1) as g:
                iteration(g)
            iteration(NG - 1, last=True)

            def down_bank(use, parity=None):
                if parity is not None:
                    pe.wait_ge(dn_freed, use - 1)
                    return dn_ps[(USE_DENSE + parity) % 4]
                if use >= 4:
                    pe.wait_ge(dn_freed, use - 3)
                return dn_ps[use % 4]

            def add_bias(b, row):
                pe.matmul(b, ones, shared_brow if row is None else brow[:, bass.ds(row, D)], start=True, stop=False,
                          skip_group_check=True)

            def up(step, parity, w, tokens, n):
                for m in range(KT):
                    if not (isinstance(step, int) and step < 2):
                        pe.wait_ge(silu_done, step * KT + (m - 2 * KT + 1))
                    for k in range(KT):
                        done = matmul3(up_ps[2 * parity + m][:, 0:n], [w(a, k, m * P, P) for a in range(2)],
                                       [t[:, k, tokens:tokens + n] for t in xmT], k == 0, k == KT - 1)
                    done.then_inc(up_filled, 1)

            def down(step, parity, w, bias_row, b, pair):
                for i in range(2):
                    t = 2 * pair + i
                    add_bias(b[:, i * D:(i + 1) * D], bias_row)
                    for k in range(KT):
                        done = matmul3(b[:, i * D:(i + 1) * D], [hh[:, parity, a, k, t * P:(t + 1) * P] for a in range(2)],
                                       [w(2 + a, k, 0, D) for a in range(2)], False, k == KT - 1)
                done.then_inc(dn_filled, 1)

            def shared_w(m, k, at, n):
                return shared[:, m, k, at:at + n]

            def expert_w(e):
                def w(m, k, at, n):
                    first = e * 2048 + ((m * KT + k) * HID + at)
                    return experts[:, first:first + n] if isinstance(e, int) else experts[:, bass.ds(first, n)]
                return w

            def shared_up(j):
                up(j, j % 2, shared_w, j * ST, ST)

            def shared_down(j):
                pe.wait_ge(h_ready, KT * j + KT)
                for pair in range(2):
                    down(j, j % 2, shared_w, None, down_bank(USE_DOWN[j] + pair), pair)

            def dense_up(e, parity):
                up(e + STEPS, parity, expert_w(e), NTS * P, GT)

            def dense_down(e, parity):
                pe.wait_ge(h_ready, e * KT + (STEPS * KT + KT))
                down(e + STEPS, parity, expert_w(e), e * D + NE * D, down_bank(e + USE_DENSE, parity), 0)

            pe.wait_ge(exp_done, NG * NU)
            pe.wait_ge(pT_ready, NG * NU)
            pe.wait_ge(o_ready, NG * NU)
            pe.wait_ge(mix_freed, len(MIX_PRO) + len(MIX_FIRST) + (NG - 2) * len(MIX_MID) + len(MIX_LAST))
            pe.wait_ge(x1_done, NG)
            b = down_bank(USE_LT)
            for t in range(NTS):
                done = pe.transpose(b[:, t * NE:(t + 1) * NE], lgT[:, t * P:(t + 1) * P], ident[0:NE, 0:NE])
            done.then_inc(dn_filled, 1)
            split(pe, NCA)
            shared_up(0)
            shared_up(1)
            pe.wait_ge(shared_brow_in, 32)
            pe.wait_ge(sort_consts, 3)
            shared_down(0)
            b = down_bank(USE_RANK)
            n = (NTS + 1) * NE
            pe.wait_ge(sort_consts, 3)
            pe.wait_ge(chosen_done, 1)
            pe.matmul(b[:, 0:n], before, chosen, start=True, stop=False, skip_group_check=True)
            for d in range(1, NTS + 1):
                done = pe.matmul(b[:, d * NE:n], ones, chosen[:, 0:n - d * NE], start=False, stop=d == NTS,
                                 skip_group_check=True)
            done.then_inc(dn_filled, 1)
            shared_up(2)
            shared_down(1)

            def slot_tokens(b, w):
                pe.wait_ge(hot_done, w + 1)
                for n in range(WAVE):
                    done = pe.matmul(b[:, 0:TCOLS], lo_hot[:, n, :], hi_hot[w][:, n, :], start=w + n == 0,
                                     stop=w == 1 and n == WAVE - 1, skip_group_check=True)
                return done

            ids = bank[3]
            pe.wait_ge(silu_done, 2 * KT)
            slot_tokens(ids, 0).then_inc(wave_used, 1)
            shared_down(2)
            slot_tokens(ids, 1).then_inc(wave_used, 1)
            b = down_bank(USE_X1T)
            pe.wait_ge(x1norm_done, NG)
            transposes(b, ct[:, :, :]).then_inc(dn_filled, 1)

            for n in range(NE):
                split(pe, NCA + 1 + n)
            pe.wait_ge(brow_in, 32)
            pe.wait_ge(sorted_done, 1)
            pe.wait_ge(dn_freed, USE_X1T + 1)
            experts_of = None

            def tile_step(t, c, loop):
                nonlocal experts_of
                k = loop[1] if loop else t - 2 if t < WINDOW + 2 else t - 2 - (NWIN - 1) * WINDOW
                if runs(t + 1):
                    g = (c + 1) % 4
                    if loop:
                        pe.wait_ge(gathered[g], loop[0] * 16 + 16 * ((3 + loop[1]) // 4 + 1))
                    else:
                        pe.wait_ge(gathered[g], 16 * ((t + 1) // 4 + 1))
                    b = bank[(c + 1) % 2]
                    for kt in range(KT):
                        done = pe.transpose(b[:, kt * P:(kt + 1) * P], rows_g[:, g, kt * P:(kt + 1) * P], ident[:, :])
                    done.then_inc(gT_filled, 1)
                if (isinstance(t, int) and t in (-1, TILES - 1)) or (loop and loop[1] == 0):
                    w = loop[0] if loop else 0 if t < 0 else NWIN - 1
                    experts_of = pe.value_load(window[0:1, bass.ds(w, 1)], min_val=0, max_val=(1 << (6 * SHIFT)) - 1)
                if runs(t):
                    e = (experts_of >> (SHIFT * (k + 2))) & (NE - 1)
                    b = bank[2 + c % 2][:, 0:HID]
                    pe.wait_ge(xg_ready, t + 1)
                    add_bias(b, e * D)
                    for kt in range(KT):
                        done = matmul3(b, [x[:, c % 2, kt, :] for x in xg], [expert_w(e)(a, kt, 0, HID) for a in range(2)],
                                       False, kt == KT - 1)
                    done.then_inc(tile_up_filled, 1)
                if runs(t - 1):
                    pe.wait_ge(tile_silu_done, t)
                    b = bank[4 + (c + 1) % 2]
                    for kt in range(KT):
                        done = pe.transpose(b[:, kt * P:(kt + 1) * P], hs[:, (c + 1) % 2, kt * P:(kt + 1) * P], ident[:, :])
                    done.then_inc(hT_filled, 1)
                if loop is None and t == 0:
                    logits(bank[6][:, D:], NG - 1).then_inc(last_logits_filled, 1)
                if loop is None and t == 1:
                    pe.wait_ge(last_logits_copied, 1)
                    for i in range(2):
                        done = pe.transpose(bank[7][:, D + i * NE:D + (i + 1) * NE], last_lgT[:, i * P:(i + 1) * P],
                                            ident[0:NE, 0:NE])
                    done.then_inc(last_logits_filled, 1)
                if runs(t - 2):
                    e = (experts_of >> (SHIFT * k)) & (NE - 1)
                    b = bank[6 + c % 2][:, 0:D]
                    pe.wait_ge(hT_ready, t - 1)
                    if loop is None and t in (2, 3):
                        pe.wait_ge(last_logits_copied, t - 1)
                    if not (isinstance(t, int) and t < 4):
                        pe.wait_ge(y_copied, t - 3)
                    add_bias(b, e * D + NE * D)
                    for kt in range(KT):
                        done = matmul3(b, [x[c % 2][:, kt, :] for x in hsT],
                                       [expert_w(e)(2 + a, kt, 0, D) for a in range(2)], False, kt == KT - 1)
                    done.then_inc(tile_down_filled, 1)

            tile_loop(pe, tile_step)
            shared_up(3)
            dense_up(0, 0)
            pe.wait_ge(y_copied, TILES)
            shared_down(3)
            dense_up(1, 1)
            dense_down(0, 0)
            for e in range(2, NE):
                dense_up(e, e % 2)
                dense_down(e - 1, (e - 1) % 2)
            dense_down(NE - 1, 1)


_INS = ["x", "ctx_1024", "g_xattn", "g_ffn", "L0_xattn_ln_g", "L0_xattn_ln_b", "L0_xattn_cln_g", "L0_xattn_cln_b",
        "L0_xattn_Wq", "L0_xattn_Wkv", "L0_xattn_Wo", "L0_xattn_Wff1", "L0_xattn_Wff2", "L0_ffn_gate_w",
        "L0_ffn_up_w", "L0_ffn_up_b", "L0_ffn_down_w", "L0_ffn_down_b", "L0_ffn_sh_up_w", "L0_ffn_sh_up_b",
        "L0_ffn_sh_down_w", "L0_ffn_sh_down_b"]


def kernel(**inputs):
    import concourse.bacc as bacc
    from concourse.bass_utils import run_bass_kernel_spmd

    nc = bacc.Bacc("TRN2", target_bir_lowering=False, num_devices=1)
    arrays, args = {}, []
    for name in _INS:
        a = np.ascontiguousarray(inputs[name])
        arrays[f"in_{name}"] = a
        args.append(nc.dram_tensor(f"in_{name}", a.shape, mybir.dt.from_np(a.dtype), kind="ExternalInput").ap())
    args.append(nc.dram_tensor("out_x", (NB, P, D), F32, kind="ExternalOutput").ap())
    program(nc, *args)
    r = run_bass_kernel_spmd(nc, [arrays], core_ids=[0])
    return r.results[0]["out_x"]
```

```python
from contextlib import ExitStack

import numpy as np

import concourse.bass as bass
from concourse import mybir

F32 = mybir.dt.float32
F32R = mybir.dt.float32r
I32 = mybir.dt.int32
ALU = mybir.AluOpType
ACT = mybir.ActivationFunctionType
AX = mybir.AxisListType

P = 128
NB, D = 16, 256
H, DH = 16, 64
FF = 1024
NE, HID = 8, 256
KT = D // P
NG = NB // 2
GT = 2 * P
NU = 8
NFF = FF // P
EPS = 1e-5
NEWTON = 3
LN_STEPS = 9 + 3 * NEWTON
RSQRT_GUESS = 0x5F3759DF
WO_T = H * DH // P

NEXT = ["K", "V", "QP0", "QP1"]
MIX_PRO = ["TXc", "TXx"] + NEXT
MIX_MID = ["FF0", "QP2", "FF1", "FF2", "QP3", "FF3", "FF4", "FF5", "X1T", "TXc", "FF6", "GL", "FF7",
           "TXx"] + NEXT
MIX_FIRST = [n for n in MIX_MID if n not in ("X1T", "GL")]
MIX_LAST = [n for n in MIX_MID if n not in ["TXc", "TXx"] + NEXT]


def mix_index(name, g, first, last):
    if g is None:
        return MIX_PRO.index(name)
    if first:
        return len(MIX_PRO) + MIX_FIRST.index(name)
    base = len(MIX_PRO) + len(MIX_FIRST) - len(MIX_MID)
    return g * len(MIX_MID) + (base + (MIX_LAST if last else MIX_MID).index(name))


def ln_base(call):
    return call * LN_STEPS


def mix_bank(name, g, first, last):
    if g is None or first:
        return mix_index(name, g, first, last) % 3
    return (len(MIX_PRO) + len(MIX_FIRST) + (MIX_LAST if last else MIX_MID).index(name)) % 3


CHUNKS_A = ["wkv", "wq0", "wq1", "ff1_0", "ff2_0", "wo_0", "ff1_1", "ff1_2", "ff2_1", "wo_1", "ff1_3"]
EARLY = 6
CHUNK_SLOT = {0: [6], 1: [7], 2: [8], 3: [9], 4: [10]}
LO_ON_POOL = (2, 4, 5, 6, 7, 8, 9, 10)
NSTAGE = 4
NCA = len(CHUNKS_A)
NPOS = NE + 1
STEPS = 4
ST = 4 * P
TPS = ST // P

NTS = NB - 2
NCH = 2 * NTS
TILES = NCH + NE - 1
WINDOW = 4
NWIN = (TILES + 1) // WINDOW
SHIFT = 3
assert (TILES - 3) % WINDOW == 0
TCOLS = TILES + TILES % 2
BACK_ORDER = [(3 * i + t, c) for i in range(3) for t, c in ((0, 0), (1, 0), (0, 1), (1, 1), (2, 0), (2, 1))]
BACK_ORDER += [(t, c) for ts in ((9, 10), (11, 12), (13,)) for c in range(2) for t in ts]
WAVE = NTS

USE_LT = 0
USE_DOWN = [1, 4, 6, 8]
USE_RANK = 3
USE_DENSE = 10


def program(nc, x, ctx_in, g_xattn, g_ffn, ln_g, ln_b, cln_g, cln_b, Wq, Wkv, Wo, Wff1, Wff2,
            gate_w, up_w, up_b, down_w, down_b, sh_up_w, sh_up_b, sh_down_w, sh_down_b, out):
    stack = ExitStack()
    with stack:
        def sb(name, shape, dt=F32):
            return stack.enter_context(nc.sbuf_tensor(name, shape, dt))

        def sem(name):
            return stack.enter_context(nc.semaphore(name))

        weights = sb("weights", [P, 20 * 1024], F32R)
        wq_t = weights[:, 0:4096].rearrange("p (a n) -> p a n", a=4)
        wq = [wq_t[:, 0:2, :], wq_t[:, 2:4, :]]
        wkk = [sb("wkk_h", [P, KT, P], F32R), sb("wkk_l", [P, KT, P], F32R)]
        wv = [sb("wv_h", [P, KT, P], F32R), sb("wv_l", [P, KT, P], F32R)]
        wf1_t = weights[:, 4096:12288].rearrange("p (a k n) -> p a k n", a=2, k=KT)
        wf1 = [wf1_t[:, 0], wf1_t[:, 1]]
        wf2, wo = [[weights[:, at + 2048 * a:at + 2048 * (a + 1)].rearrange("p (k n) -> p k n", n=D) for a in range(2)]
                   for at in (12288, 16384)]
        gw = [sb("gw_h", [P, KT, P], F32R), sb("gw_l", [P, KT, P], F32R)]
        stage = sb("stage", [P, 2, 1024])
        ident = sb("ident", [P, P])
        NROW = 4 + NE + 1 + NE
        all_rows = sb("all_rows", [32 + NE + 1, D])
        rows, dbrow = all_rows[0:NROW, :], all_rows[32:32 + NE + 1, :]
        cols = sb("cols", [P, KT, NROW])
        gates_in = sb("gates_in", [P, 2])
        gates = sb("gates", [P, 2])
        xs = sb("xs", [P, NB, D])
        ct = sb("ct", [P, 2, D])
        xn = sb("xn", [P, 4, D])
        tf = sb("tf", [P, KT, GT])
        acts = sb("acts", [P, 9 * 512], F32R)
        cnT, xnT, uT = [[acts[:, 512 * i:512 * (i + 1)].rearrange("p (k n) -> p k n", k=2) for i in (n, n + 1)]
                        for n in (0, 2, 4)]
        pT = [acts[:, 512 * i:512 * (i + 1)] for i in (6, 7)]
        oT = [acts[:, 4096 + D * i:4096 + D * (i + 1)].rearrange("p (k n) -> p k n", k=2) for i in (0, 1)]
        q_t = sb("q_t", [P, 2, H // 2, GT], F32R)
        q = [q_t[:, 0], q_t[:, 1]]
        kz = [sb("kz_h", [P, 2, 2, P], F32R), sb("kz_l", [P, 2, 2, P], F32R)]
        vv = [sb("vv_h", [P, 2, P], F32R), sb("vv_l", [P, 2, P], F32R)]
        pr = sb("pr", [P, 2, 4, P])
        nmax = sb("nmax", [P, 2, 4])
        den = sb("den", [P, 2, 4])
        rden = sb("rden", [P, 2, 4])
        th = sb("th", [P, GT])
        u1 = sb("u1", [P, GT])
        uf = sb("uf", [P, GT])
        bn = sb("bn", [P, 6, 6])
        mean = sb("mean", [P, 6])
        var = sb("var", [P, 6])
        rt = sb("rt", [P, 6])
        ry = sb("ry", [P, 6])
        xmT_t = sb("xmT_t", [P, 2 * KT, NB * P], F32R)
        xmT = [xmT_t[:, 0:KT], xmT_t[:, KT:2 * KT]]
        spare = sb("spare", [P, NB * P])
        lgT = spare[0:NE, :]
        rio = sb("rio", [P, NB, NE])
        bias = sb("bias", [P, KT, 1])
        g1 = sb("g1", [P, NB])
        g2 = sb("g2", [P, NB])
        g3 = sb("g3", [P, NB])
        lg, ga = [t.rearrange("p (t e) -> p t e", t=NB) for t in (th[:, 0:P], th[:, P:2 * P])]
        gb, oh1 = [t.rearrange("p (t e) -> p t e", t=NB) for t in (u1[:, 0:P], u1[:, P:2 * P])]
        comb = uf[:, 0:NPOS * NB].rearrange("p (c t) -> p c t", c=NPOS)
        shared = weights[:, 0:2048].rearrange("p (m k n) -> p m k n", m=4, k=KT)
        experts = weights[:, 4096:]
        lo_hot = [t[:, 2048:2048 + WAVE * P].rearrange("p (n c) -> p n c", n=WAVE)
                  for t in (weights, q_t.rearrange("p a m n -> p (a m n)"))]
        chosen = weights[:, 4096 - (NTS + 1) * NE:4096]
        hi_hot = [t.rearrange("p a b n -> p (a b n)")[:, 0:WAVE * TCOLS].rearrange("p (n c) -> p n c", n=WAVE)
                  for t in kz]
        shared_brow, brow = acts[:, 0:D], acts[:, D:D + 2 * NE * D]
        ones, before = vv[0][:, 0, :], vv[0][:, 1, :]
        consts = tf.rearrange("p k n -> p (k n)")
        iota_lo, iota_tile = consts[:, 0:P], consts[:, P:P + 40]
        token = consts[:, 168:168 + NTS]
        slot_token = consts[:, 192:192 + TILES].bitcast(I32)
        token_slot = consts[:, 240:240 + NCH].bitcast(I32)
        window = consts[0:1, 272:272 + NWIN].bitcast(I32)
        rank = spare[:, 0:NTS * NE].rearrange("p (t e) -> p t e", e=NE)
        slots8 = spare[:, 128:128 + NCH * NE].rearrange("p (t e) -> p t e", e=NE)
        small = spare[:, 384:576]
        flat_ct = ct.rearrange("p a n -> p (a n)")
        tile_cmp = flat_ct[0:1, 0:40 * NE].rearrange("p (t e) -> p t e", e=NE)
        tile_expert = flat_ct[0:1, 320:360]
        pack = flat_ct[0:1, 360:360 + NWIN]
        is_tile = flat_ct[:, 0:WAVE * TCOLS]
        expert_ends = flat_ct[0:1, 2 * D - NE:2 * D]
        rows_g = spare[:, 0:4 * D].rearrange("p (s n) -> p s n", s=4)
        xg = kz
        hs = ct
        hsT = [wkk, wv]
        ys = stage[:, 0, :].rearrange("p (s n) -> p s n", s=4)
        zero = gw[0][:, 0, NE:NE + 1].bitcast(F32)
        last_lgT = all_rows[0:NE, :]
        hh = q_t.rearrange("p a m n -> p (a m n)").rearrange("p (s a m n) -> p s a m n", s=2, a=2, m=KT)
        hf = xn.rearrange("p a n -> p (a n)").rearrange("p (m n) -> p m n", m=KT)
        norm_rows = nc.dram_tensor("norm_rows", (NTS * P, D), F32).ap()
        slot_rows = nc.dram_tensor("slot_rows", (TILES * P, D), F32).ap()
        bias_rows = nc.dram_tensor("bias_rows", (2, 2 * NE + 1, D), F32).ap()

        bank = [stack.enter_context(nc.psum_tensor(f"bank{i}", [P, 512], F32)) for i in range(8)]
        sc_ps, t_ps, pv_ps, out_ps, mix_ps = bank[0:2], bank[2], bank[3], bank[4], bank[5:8]
        up_ps, dn_ps = bank[0:4], [*bank[5:8], bank[4]]

        rows_in = sem("rows_in")
        gates_loaded = sem("gates_loaded")
        dbrow_in = sem("dbrow_in")
        x_in = [sem(f"x_in{g}") for g in range(NG)]
        ctx_loaded = sem("ctx_loaded")
        stage_full = [sem(f"stage_full{i}") for i in range(NSTAGE)]
        kv_hi_done = sem("kv_hi_done")
        chunk_hi_done = sem("chunk_hi_done")
        chunk_split_done = [sem(f"chunk_split_done{n}") for n in range(NCA)]
        expert_hi_done = sem("expert_hi_done")
        expert_ready = sem("expert_ready")
        ident_done = sem("ident_done")
        rio_done = sem("rio_done")
        zeros_done = sem("zeros_done")
        cols_filled = sem("cols_filled")
        cols_done = sem("cols_done")
        gw_done = sem("gw_done")
        gates_done = sem("gates_done")
        mix_filled = sem("mix_filled")
        mix_freed = sem("mix_freed")
        ln_step = sem("ln_step")
        xnorm_done = sem("xnorm_done")
        cnorm_done = sem("cnorm_done")
        x1norm_done = sem("x1norm_done")
        tfh_done = sem("tfh_done")
        cnT_ready = sem("cnT_ready")
        xnT_ready = sem("xnT_ready")
        kh_done = sem("kh_done")
        vh_done = sem("vh_done")
        qh_done = sem("qh_done")
        scores_filled = sem("scores_filled")
        nmax_done = sem("nmax_done")
        exp_done = sem("exp_done")
        rden_done = sem("rden_done")
        probs_ready = sem("probs_ready")
        pT_filled = sem("pT_filled")
        pTh_done = sem("pTh_done")
        pT_ready = sem("pT_ready")
        pv_filled = sem("pv_filled")
        oh_done = sem("oh_done")
        o_ready = sem("o_ready")
        wo_done = sem("wo_done")
        tanh_done = sem("tanh_done")
        u1_done = sem("u1_done")
        uh_done = sem("uh_done")
        u_ready = sem("u_ready")
        ff2_done = sem("ff2_done")
        x1_done = sem("x1_done")
        xmh_done = sem("xmh_done")
        link_done = sem("link_done")
        shifted_done = sem("shifted_done")
        gexp_done = sem("gexp_done")
        bias_done = sem("bias_done")
        bias_split = sem("bias_split")
        bias_stored = sem("bias_stored")
        shared_zeroed = sem("shared_zeroed")
        shared_brow_in = sem("shared_brow_in")
        brow_zeroed = sem("brow_zeroed")
        brow_in = sem("brow_in")
        rows_stored = sem("rows_stored")
        sort_consts = sem("sort_consts")
        chosen_done = sem("chosen_done")
        hot_done = sem("hot_done")
        wave_used = sem("wave_used")
        windows_done = sem("windows_done")
        sorted_done = sem("sorted_done")
        last_filled = sem("last_filled")
        last_read = sem("last_read")
        gathered = [sem(f"gathered{i}") for i in range(4)]
        gT_filled = sem("gT_filled")
        xgh_done = sem("xgh_done")
        xg_ready = sem("xg_ready")
        tile_up_filled = sem("tile_up_filled")
        tile_silu_done = sem("tile_silu_done")
        hT_filled = sem("hT_filled")
        hTh_done = sem("hTh_done")
        hT_ready = sem("hT_ready")
        tile_down_filled = sem("tile_down_filled")
        y_copied = sem("y_copied")
        y_stored = [sem(f"y_stored{i}") for i in range(4)]
        back_in = [sem(f"back_in{i}") for i in range(3)]
        back_added = sem("back_added")
        up_filled = sem("up_filled")
        silu_done = sem("silu_done")
        hh_done = sem("hh_done")
        h_ready = sem("h_ready")
        dn_filled = sem("dn_filled")
        dn_freed = sem("dn_freed")
        written = sem("written")

        block = stack.enter_context(nc.Block())

        def buffer(n):
            if n < NCA:
                i = n % NSTAGE
                return (stage[:, i, :] if i < 2 else spare[:, (i - 2) * 1024:(i - 1) * 1024]), i
            i = (n - NCA) % 4
            return (stage[:, i, :] if i < 2 else pr.rearrange("p s h n -> p (s h n)") if i == 2
                    else spare[:, 1024:2048]), i

        def tile_loop(eng, step):
            for t in range(-2, WINDOW + 2):
                step(t, t % 4, None)
            with eng.Fori(1, (TILES - 3) // WINDOW - 1) as i:
                for j in range(WINDOW):
                    step(i * WINDOW + (2 + j), (2 + j) % 4, (i, j))
            for t in range(TILES - 1 - WINDOW, TILES + 2):
                step(t, t % 4, None)

        def runs(t):
            return not isinstance(t, int) or 0 <= t < TILES

        def back(n):
            if n < 24:
                return xmT_t[:, n // 6, (n % 6) * D:(n % 6 + 1) * D].bitcast(F32)
            return rows_g[:, n - 24, :]

        def chunk_split(n):
            c, (src, _) = CHUNKS_A[n], buffer(n)
            i = int(c[-1])
            if c.startswith("wq"):
                return src, wq[0][:, i, :], wq[1][:, i, :]
            if c.startswith("ff1"):
                w = [t.rearrange("p k (h n) -> p (k h) n", h=2)[:, :, 256 * i:256 * i + 256] for t in wf1]
                return src.rearrange("p (k n) -> p k n", k=4), w[0], w[1]
            w = [t[:, 4 * i:4 * i + 4, :] for t in (wf2 if c.startswith("ff2") else wo)]
            return src.rearrange("p (k n) -> p k n", k=4), w[0], w[1]

        def expert_split(c):
            dst = shared if c == 0 else experts[:, (c - 1) * 2048:c * 2048].rearrange("p (m k n) -> p m k n", m=4, k=KT)
            return buffer(NCA + c)[0].rearrange("p (m k n) -> p m k n", m=2, k=KT), dst

        def chunk_loads(n):
            s, _ = buffer(n)
            if n >= NCA:
                c = n - NCA
                s = s.rearrange("p (m k n) -> p m k n", m=2, k=KT)
                pair = (sh_up_w, sh_down_w) if c == 0 else (up_w[c - 1], down_w[c - 1])
                return [(s[:, m], w.rearrange("(k p) n -> p k n", p=P)) for m, w in enumerate(pair)]
            name = CHUNKS_A[n]
            if name == "wkv":
                return [(s[:, 0:KT * P].rearrange("p (k n) -> p k n", k=KT), Wkv.rearrange("(k p) n -> p k n", p=P))]
            i = int(name[-1])
            if name.startswith("wq"):
                return [(s, Wq[i * P:(i + 1) * P, :])]
            if name.startswith("ff1"):
                src = Wff1.rearrange("(k p) (h n) -> p k h n", p=P, h=2)[:, :, :, 256 * i:256 * i + 256]
                dst = s.rearrange("p (k h n) -> p k h n", k=KT, h=2)
                return [(dst[:, k], src[:, k]) for k in range(KT)]
            w = Wff2 if name.startswith("ff2") else Wo
            return [(s.rearrange("p (k n) -> p k n", k=4), w.rearrange("(k p) n -> p k n", p=P)[:, 4 * i:4 * i + 4, :])]

        def stage_value(n):
            return 16 * sum(len(chunk_loads(m)) for m in range(n + 1) if buffer(m)[1] == buffer(n)[1])

        def landed(eng, n):
            eng.wait_ge(stage_full[buffer(n)[1]], stage_value(n))

        def split(eng, n):
            eng.wait_ge(chunk_split_done[n] if n < NCA else expert_ready, 1 if n < NCA else n - NCA + 1)

        def halves(bank_ap, two):
            return bank_ap[:, :].rearrange("p (a n) -> p a n", a=two)

        @block.sync
        def _(sp):
            def load_x(g):
                sp.dma_start(xs[:, 2 * g:2 * g + 2, :], x[2 * g:2 * g + 2].rearrange("b p d -> p b d")
                             ).then_inc(x_in[g], 16)

            def load_ctx(g):
                if g > 0:
                    sp.wait_ge(cnorm_done, g)
                sp.dma_start(ct[:, :, :], ctx_in[2 * g:2 * g + 2].rearrange("b p d -> p b d")
                             ).then_inc(ctx_loaded, 16)

            def load_chunk(n):
                buf = buffer(n)[1]
                before = [m for m in range(n) if buffer(m)[1] == buf]
                if before:
                    split(sp, before[-1])
                for dst, src in chunk_loads(n):
                    sp.dma_start(dst, src).then_inc(stage_full[buf], 16)

            load_ctx(0)
            load_x(0)
            for n in range(NCA):
                load_chunk(n)
                if n == EARLY - 1:
                    load_ctx(1)
                    load_x(1)
            for g in range(2, NG):
                load_x(g)
            sp.wait_ge(bias_split, 2)
            for a in range(2):
                for at, r in ((0, slice(5, 5 + NE)), (NE, slice(33, 33 + NE)), (2 * NE, slice(32, 33))):
                    sp.dma_start(bias_rows[a, at:at + r.stop - r.start],
                                 xmT[a][r, 0, (NB - 2) * P:NB * P].bitcast(F32)).then_inc(bias_stored, 16)
            load_ctx(2)
            load_chunk(NCA)
            load_chunk(NCA + 1)
            for g in range(NG - 1):
                sp.wait_ge(x1norm_done, g + 1)
                sp.dma_start(norm_rows[g * GT:(g + 1) * GT].rearrange("(b p) d -> p b d", p=P), xn[:, 0:2, :]
                             ).then_inc(rows_stored, 16)
                if g + 3 < NG:
                    load_ctx(g + 3)
            sp.wait_ge(bias_stored, 16 * 6)
            sp.wait_ge(shared_zeroed, 1)
            for a in range(2):
                sp.dma_start(shared_brow[32 * a:32 * a + 1, :].bitcast(F32), bias_rows[a, 2 * NE:2 * NE + 1]
                             ).then_inc(shared_brow_in, 16)
            sp.wait_ge(pT_filled, NG * NU)
            load_chunk(NCA + 2)
            sp.wait_ge(dn_filled, USE_LT + 1)
            for c in range(3, NPOS):
                load_chunk(NCA + c)
            sp.wait_ge(brow_zeroed, 1)
            for a in range(2):
                sp.dma_start(brow[32 * a:32 * a + 1, :].bitcast(F32),
                             bias_rows[a, 0:2 * NE].rearrange("(o r) d -> o (r d)", o=1)).then_inc(brow_in, 16)
            for t in range(TILES):
                sp.wait_ge(y_copied, t + 1)
                sp.dma_start(slot_rows[t * P:(t + 1) * P], ys[:, t % 4, :]).then_inc(y_stored[t % 4], 16)
            for t0, t1 in ((0, 4), (4, 8), (NTS, NB), (8, 12), (12, NTS)):
                if t0 == NTS:
                    sp.wait_ge(dn_freed, USE_DENSE + NE)
                else:
                    sp.wait_ge(back_added, BACK_ORDER.index((t1 - 1, 1)) + 1)
                sp.dma_start(out[t0:t1].rearrange("b p d -> p b d"), xs[:, t0:t1, :]).then_inc(written, 16)
            sp.wait_ge(written, 16 * 5)

        @block.gpsimd
        def _(pool):
            pool.memset(ident[:, :], 0.0).then_inc(ident_done, 1)
            pool.wait_ge(ident_done, 1)
            pool.affine_select(out=ident[:, :], in_=ident[:, :], compare_op=ALU.not_equal, fill=1.0, base=0,
                               pattern=[[-1, P]], channel_multiplier=1).then_inc(ident_done, 1)

            pool.dma_start(dbrow[0:1, :], sh_down_b.rearrange("(a n) -> a n", a=1)).then_inc(dbrow_in, 16)
            pool.dma_start(dbrow[1:NPOS, :], down_b).then_inc(dbrow_in, 16)
            for e in range(NE):
                last = pool.memset(rio[:, :, e:e + 1], float(NE - e))
            last.then_inc(rio_done, 1)

            def split_lo(n):
                src, hi, lo = chunk_split(n)
                pool.wait_ge(chunk_hi_done, n)
                pool.tensor_tensor(lo, src, hi.bitcast(F32), ALU.subtract).then_inc(chunk_split_done[n], 1)

            def transposed_lo(dst, count, ready):
                pool.wait_ge(tfh_done, count)
                pool.tensor_tensor(dst[1][:, :, :], tf[:, :, :], dst[0][:, :, :].bitcast(F32), ALU.subtract
                                   ).then_inc(ready, 1)

            def expert_lo(c):
                src, dst = expert_split(c)
                pool.wait_ge(expert_hi_done, c + 1)
                for m in range(2):
                    done = pool.tensor_tensor(dst[:, 2 * m + 1], src[:, m], dst[:, 2 * m].bitcast(F32), ALU.subtract)
                done.then_inc(expert_ready, 1)

            def iteration(g, first=False, last=False):
                for s in range(NU):
                    u = g * NU + s
                    pool.wait_ge(rden_done, u + 1)
                    pool.tensor_tensor(pr[:, s % 2], pr[:, s % 2],
                                       rden[:, s % 2, :].unsqueeze(2).broadcast_to((P, 4, P)),
                                       ALU.mult).then_inc(probs_ready, 1)
                    pool.wait_ge(uh_done, u + 1)
                    pool.tensor_tensor(uT[1][:, s % 2, :], uf[:, :], uT[0][:, s % 2, :].bitcast(F32),
                                       ALU.subtract).then_inc(u_ready, 1)
                    if s == 6 and not last:
                        transposed_lo(cnT, g * 2 + 3, cnT_ready)
                    if s == 4 and last:
                        pool.memset(shared_brow.bitcast(F32), 0.0).then_inc(shared_zeroed, 1)
                    if s == 6 and last:
                        expert_lo(0)
                    if first:
                        for n in CHUNK_SLOT.get(s, []):
                            split_lo(n)
                if not last:
                    transposed_lo(xnT, g * 2 + 4, xnT_ready)

            split_lo(2)
            split_lo(4)
            split_lo(5)
            iteration(0, first=True)
            with pool.Fori(1, NG - 1) as g:
                iteration(g)
            iteration(NG - 1, last=True)

            pool.wait_ge(xnT_ready, NG)
            pool.iota(iota_lo, [[1, P]], base=0, channel_multiplier=0, allow_small_or_imprecise_dtypes=True)
            pool.iota(iota_tile, [[1, 40]], base=0, channel_multiplier=0, allow_small_or_imprecise_dtypes=True)
            pool.iota(token, [[P, NTS]], base=0, channel_multiplier=1, allow_small_or_imprecise_dtypes=True
                      ).then_inc(sort_consts, 1)

            pool.wait_ge(pv_filled, NG * NU)
            pool.memset(ones.bitcast(F32), 1.0)
            pool.memset(before.bitcast(F32), 1.0).then_inc(sort_consts, 1)
            pool.wait_ge(sort_consts, 2)
            pool.affine_select(out=before, in_=before.bitcast(F32), compare_op=ALU.is_gt, fill=0.0,
                               base=0, pattern=[[1, P]], channel_multiplier=-1).then_inc(sort_consts, 1)
            for c in range(1, 5):
                expert_lo(c)
            for c in range(5, NPOS - 1):
                expert_lo(c)
            pool.wait_ge(rows_stored, 16 * (NG - 1))
            pool.wait_ge(sorted_done, 1)

            def gather(t):
                if t >= 4:
                    pool.wait_ge(gT_filled, t - 3)
                pool.indirect_dma_start(rows_g[:, t % 4, :], None, norm_rows[:, :],
                                        bass.IndirectOffsetOnAxis(ap=slot_token[:, t:t + 1], axis=0)
                                        ).then_inc(gathered[t % 4], 16)

            for t in range(4):
                gather(t)
            expert_lo(NPOS - 1)
            for t in range(4, TILES):
                gather(t)
            pool.wait_ge(gT_filled, TILES)
            for i in range(4):
                pool.wait_ge(y_stored[i], 16 * len(range(i, TILES, 4)))
            for t in range(NTS):
                if t >= 3:
                    pool.wait_ge(back_in[t % 3], 32 * (t // 3))
                for c in range(2):
                    pool.indirect_dma_start(back(2 * t + c), None, slot_rows[:, :],
                                            bass.IndirectOffsetOnAxis(ap=token_slot[:, c * NTS + t:c * NTS + t + 1],
                                                                      axis=0)).then_inc(back_in[t % 3], 16)

        @block.scalar
        def _(act):
            for i, v in enumerate((ln_g, ln_b, cln_g, cln_b, sh_up_b)):
                act.dma_start(rows[i:i + 1, :], v.rearrange("(a n) -> a n", a=1)).then_inc(rows_in, 16)
            act.dma_start(rows[5:5 + NE, :], up_b).then_inc(rows_in, 16)
            act.dma_start(rows[5 + NE:NROW, :], gate_w).then_inc(rows_in, 16)
            for i, v in enumerate((g_xattn, g_ffn)):
                act.dma_start(gates_in[:, i:i + 1], v.rearrange("(a n) -> a n", a=1).broadcast_to((P, 1))
                              ).then_inc(gates_loaded, 16)

            def transposed_hi(name, g, first, last, dst):
                act.wait_ge(mix_freed, mix_index(name, g, first, last) + 1)
                act.activation(dst[:, :, :], tf[:, :, :], ACT.Copy).then_inc(tfh_done, 1)

            def keys_values_hi(g, first, last):
                b = mix_ps[mix_bank("K", g, first, last)]
                act.wait_ge(mix_filled, mix_index("K", g, first, last) + 1)
                for a in range(2):
                    r = slice(DH * a, DH * a + DH)
                    done = act.activation(kz[0][r, :, a, :], b[r, 0:GT].rearrange("p (b n) -> p b n", b=2),
                                          ACT.Copy, scale=DH ** -0.5)
                done.then_inc(kh_done, 1)
                b = mix_ps[mix_bank("V", g, first, last)]
                act.wait_ge(mix_filled, mix_index("V", g, first, last) + 1)
                if g is not None:
                    act.wait_ge(pv_filled, g * NU + NU)
                act.activation(vv[0][:, :, :], halves(b, 2)[:, :, 0:P], ACT.Copy).then_inc(vh_done, 1)

            def queries_hi(pair, g, first, last):
                b = mix_ps[mix_bank(f"QP{pair}", g, first, last)]
                act.wait_ge(mix_filled, mix_index(f"QP{pair}", g, first, last) + 1)
                act.activation(q[0][:, 2 * pair:2 * pair + 2, :], halves(b, 2), ACT.Copy).then_inc(qh_done, 1)

            def attended_hi(u, very_first):
                act.wait_ge(pv_filled, u + 1)
                if not very_first:
                    act.wait_ge(wo_done, u)
                v = pv_ps[:, :].rearrange("p (m a n) -> p m a n", m=2, a=2)
                for a in range(2):
                    r = slice(DH * a, DH * a + DH)
                    done = act.activation(oT[0][r, :, :], v[r, :, a, :], ACT.Copy)
                done.then_inc(oh_done, 1)

            def probs_hi(u, very_first):
                act.wait_ge(pT_filled, u + 1)
                if not very_first:
                    act.wait_ge(pv_filled, u)
                act.activation(pT[0][:, :], t_ps[:, :], ACT.Copy).then_inc(pTh_done, 1)

            def iteration(g, first=False, last=False):
                for s in range(NU + 2):
                    u = g * NU + s
                    if 1 <= s <= NU:
                        act.wait_ge(mix_freed, mix_index(f"FF{s - 1}", g, first, last) + 1)
                        if not (first and s < 3):
                            act.wait_ge(ff2_done, u - 2)
                        act.activation(uT[0][:, (s - 1) % 2, :], uf[:, :], ACT.Copy).then_inc(uh_done, 1)
                    if s >= 2:
                        attended_hi(u - 2, first and s == 2)
                    if s < NU:
                        act.wait_ge(nmax_done, u + 1)
                        if not (first and s < 2):
                            act.wait_ge(pT_filled, u - 1)
                        for h in range(4):
                            done = act.activation(pr[:, s % 2, h, :], sc_ps[s % 2][:, h * P:(h + 1) * P], ACT.Exp,
                                                  bias=nmax[:, s % 2, h:h + 1], accum_out=den[:, s % 2, h:h + 1])
                        done.then_inc(exp_done, 1)
                    if first:
                        for n in CHUNK_SLOT.get(s, []):
                            split_hi(n)
                    if s == NU and not last:
                        transposed_hi("TXx", g, first, last, xnT[0])
                    if 1 <= s <= NU:
                        probs_hi(u - 1, first and s == 1)
                    if s < NU:
                        b = mix_ps[mix_bank(f"FF{s}", g, first, last)]
                        act.wait_ge(mix_filled, mix_index(f"FF{s}", g, first, last) + 1)
                        if not (first and s == 0):
                            act.wait_ge(u1_done, u)
                        act.activation(th[:, :], b[:, GT:2 * GT], ACT.Tanh, scale=0.5).then_inc(tanh_done, 1)
                    if s == 0:
                        queries_hi(2, g, first, last)
                    if s == 2:
                        queries_hi(3, g, first, last)
                    if s == 5 and not first:
                        act.wait_ge(mix_filled, mix_index("X1T", g, first, last) + 1)
                        act.activation(gates_in[:, 0:1], gates[:, 0:1], ACT.Copy)
                        x1_hi(g - 1, mix_ps[mix_bank("X1T", g, first, last)])
                    if s == 5 and last:
                        expert_hi(0)
                    if s == 6 and not last:
                        transposed_hi("TXc", g, first, last, cnT[0])
                    if s == NU and not last:
                        keys_values_hi(g, first, last)
                if not last:
                    queries_hi(0, g, first, last)
                    queries_hi(1, g, first, last)

            def x1_hi(g, b):
                act.activation(xmT[0][:, :, bass.ds(g * GT, GT)], halves(b, KT), ACT.Copy).then_inc(xmh_done, 1)

            def expert_hi(c):
                src, dst = expert_split(c)
                landed(act, NCA + c)
                act.activation(dst[:, 0::2], src, ACT.Copy).then_inc(expert_hi_done, 1)

            def split_hi(n):
                src, hi, _ = chunk_split(n)
                landed(act, n)
                act.activation(hi, src, ACT.Copy).then_inc(chunk_hi_done, 1)

            split_hi(1)
            split_hi(2)
            act.wait_ge(gates_loaded, 32)
            act.activation(gates[:, :], gates_in[:, :], ACT.Tanh).then_inc(gates_done, 1)
            transposed_hi("TXc", None, False, False, cnT[0])
            transposed_hi("TXx", None, False, False, xnT[0])
            keys_values_hi(None, False, False)
            split_hi(3)
            queries_hi(0, None, False, False)
            split_hi(4)
            queries_hi(1, None, False, False)
            split_hi(5)
            iteration(0, first=True)
            with act.Fori(1, NG - 1) as g:
                iteration(g)
            iteration(NG - 1, last=True)

            def up_bias(pos):
                act.activation(bias[:, :, :], cols[:, :, bass.ds(pos + 4, 1)], ACT.Copy).then_inc(bias_done, 1)

            def hidden_hi(step, parity, pos, n):
                act.wait_ge(bias_done, pos + 1)
                for m in range(KT):
                    act.wait_ge(up_filled, step * KT + (m + 1))
                    if not (isinstance(step, int) and step == 0):
                        act.wait_ge(h_ready, step * KT + (m - KT + 1))
                    act.activation(hf[:, m, 0:n], up_ps[2 * parity + m][:, 0:n], ACT.Silu,
                                   bias=bias[:, m, :]).then_inc(silu_done, 1)
                    act.wait_ge(silu_done, step * KT + (m + 1))
                    if m == 0:
                        if isinstance(step, int):
                            if step >= 2:
                                act.wait_ge(dn_filled, USE_DOWN[step - 2] + 2 if step < 6 else USE_DENSE + step - 5)
                        else:
                            act.wait_ge(dn_filled, step + (USE_DENSE - 5))
                    act.activation(hh[:, parity, 0, m, 0:n], hf[:, m, 0:n], ACT.Copy).then_inc(hh_done, 1)

            act.wait_ge(cols_done, 1)
            up_bias(0)
            expert_hi(1)
            expert_hi(2)
            act.wait_ge(shifted_done, 1)
            act.activation(ga[:, 0:NTS, :], gb[:, 0:NTS, :], ACT.Exp).then_inc(gexp_done, 1)
            act.wait_ge(rows_stored, 16 * (NG - 1))
            hidden_hi(0, 0, 0, ST)
            hidden_hi(1, 1, 0, ST)
            expert_hi(3)
            hidden_hi(2, 0, 0, ST)
            act.wait_ge(wo_done, NG * NU)
            expert_hi(4)
            expert_hi(5)
            act.activation(brow, zero.broadcast_to((P, 2 * NE * D)), ACT.Copy).then_inc(brow_zeroed, 1)
            for c in range(6, NPOS):
                expert_hi(c)
            act.wait_ge(last_filled, 1)
            act.wait_ge(bias_stored, 16 * 6)
            x1_hi(NG - 1, bank[2])

            def tile_step(t, c, loop):
                if runs(t):
                    act.wait_ge(tile_up_filled, t + 1)
                    if not (isinstance(t, int) and t < 2):
                        act.wait_ge(hT_filled, t - 1)
                    act.activation(hs[:, c % 2, :], bank[2 + c % 2][:, 0:HID], ACT.Silu).then_inc(tile_silu_done, 1)
                if runs(t + 2):
                    act.wait_ge(gT_filled, t + 3)
                    act.activation(xg[0][:, c % 2], halves(bank[c % 2], 4)[:, 0:2, :], ACT.Copy).then_inc(xgh_done, 1)
                if loop is None and t == TILES - 5:
                    act.wait_ge(shifted_done, 2)
                    act.activation(ga[:, NTS:NB, :], gb[:, NTS:NB, :], ACT.Exp).then_inc(gexp_done, 1)
                if runs(t - 1):
                    act.wait_ge(hT_filled, t)
                    if not (isinstance(t, int) and t < 3):
                        act.wait_ge(tile_down_filled, t - 2)
                    act.activation(hsT[0][(c + 1) % 2][:, :, :], halves(bank[4 + (c + 1) % 2], 4)[:, 0:2, :], ACT.Copy
                                   ).then_inc(hTh_done, 1)

            tile_loop(act, tile_step)
            hidden_hi(3, 1, 0, ST)
            up_bias(1)
            hidden_hi(STEPS, 0, 1, GT)
            up_bias(2)
            hidden_hi(STEPS + 1, 1, 2, GT)
            with act.Fori(0, NE // 2 - 1) as i:
                for j in range(2):
                    up_bias(i * 2 + (3 + j))
                    hidden_hi(i * 2 + (STEPS + 2 + j), j, i * 2 + (3 + j), GT)

        @block.vector
        def _(dve):
            def norm_step(call, k, lo, hi, g_ctx, g_x, g_x1, after):
                c = slice(lo, hi)
                if k == 0:
                    if after:
                        dve.wait_ge(*after)
                else:
                    dve.wait_ge(ln_step, ln_base(call) + k)
                if k < 3:
                    tiles = [None if g_ctx is None else [ct[:, i, :] for i in range(2)],
                             None if g_x is None else x_tiles(g_x), None if g_x1 is None else x_tiles(g_x1)][k]
                    if tiles:
                        dve.memset(rt[:, c], 0.0)
                        for i, t in enumerate(tiles):
                            done = dve.bn_stats(bn[:, 2 * k + i, :], t)
                    else:
                        done = dve.memset(rt[:, c], 0.0)
                elif k == 3:
                    dve.tensor_tensor(mean[:, c], bn[:, c, 1], bn[:, c, 4], ALU.add)
                    dve.tensor_tensor(rt[:, c], bn[:, c, 1], bn[:, c, 4], ALU.subtract)
                    done = dve.tensor_tensor(var[:, c], bn[:, c, 2], bn[:, c, 5], ALU.add)
                elif k == 4:
                    done = dve.tensor_tensor(rt[:, c], rt[:, c], rt[:, c], ALU.mult)
                elif k == 5:
                    done = dve.scalar_tensor_tensor(var[:, c], rt[:, c], D / 4.0, var[:, c], ALU.mult, ALU.add)
                elif k == 6:
                    dve.tensor_scalar(mean[:, c], mean[:, c], 0.5, None, ALU.mult)
                    for at, a, b in ((slice(0, 2), 1.0, EPS), (slice(2, 4), 1.0 + EPS, EPS * EPS), (slice(4, 6), 1.0, EPS)):
                        if lo <= at.start < hi:
                            done = dve.tensor_scalar(var[:, at], var[:, at], a / D, b, ALU.mult, ALU.add)
                elif k == 7:
                    done = dve.tensor_scalar(rt[:, c].bitcast(I32), var[:, c].bitcast(I32), 1, None,
                                             ALU.logical_shift_right)
                elif k == 8:
                    done = dve.tensor_scalar(ry[:, c].bitcast(I32), rt[:, c].bitcast(I32), -1.0, float(RSQRT_GUESS),
                                             ALU.mult, ALU.add)
                elif k % 3 == 0:
                    done = dve.tensor_tensor(rt[:, c], ry[:, c], ry[:, c], ALU.mult)
                elif k % 3 == 1:
                    done = dve.scalar_tensor_tensor(rt[:, c], rt[:, c], -0.5, var[:, c], ALU.mult, ALU.mult)
                else:
                    done = dve.scalar_tensor_tensor(ry[:, c], rt[:, c], 1.5, ry[:, c], ALU.add, ALU.mult)
                done.then_inc(ln_step, 1)

            def norm_apply(call, tiles, dst, col, done):
                dve.wait_ge(ln_step, ln_base(call) + LN_STEPS)
                for i, t in enumerate(tiles):
                    last = dve.tensor_scalar(dst[:, i, :], t, mean[:, col + i:col + i + 1], ry[:, col + i:col + i + 1],
                                             ALU.subtract, ALU.mult)
                last.then_inc(done, 1)

            def x_tiles(g):
                return [xs[:, bass.ds(g * 2 + i, 1), :].rearrange("p a n -> p (a n)") for i in range(2)]

            def transposed(name, g, first, last, gn):
                isx = name == "TXx"
                col = 0 if isx else 2
                b = mix_ps[mix_bank(name, g, first, last)]
                n = mix_index(name, g, first, last)
                dve.wait_ge(mix_filled, n + 1)
                if isx:
                    dve.wait_ge(cnT_ready, gn + 1)
                elif g is not None:
                    dve.wait_ge(xnT_ready, gn)
                for k in range(KT):
                    done = dve.tensor_scalar(tf[:, k, :], b[:, k * GT:(k + 1) * GT], cols[:, k, col:col + 1],
                                             cols[:, k, col + 1:col + 2], ALU.mult, ALU.add)
                done.then_inc(mix_freed, 1)

            def keys_values_lo(g, first, last, gn):
                b = mix_ps[mix_bank("K", g, first, last)]
                dve.wait_ge(kh_done, gn + 1)
                for a in range(2):
                    r = slice(DH * a, DH * a + DH)
                    done = dve.scalar_tensor_tensor(
                        kz[1][r, :, a, :], b[r, 0:GT].rearrange("p (b n) -> p b n", b=2), DH ** -0.5,
                        kz[0][r, :, a, :].bitcast(F32), ALU.mult, ALU.subtract)
                done.then_inc(mix_freed, 1)
                b = mix_ps[mix_bank("V", g, first, last)]
                dve.wait_ge(vh_done, gn + 1)
                dve.tensor_tensor(vv[1][:, :, :], halves(b, 2)[:, :, 0:P], vv[0][:, :, :].bitcast(F32), ALU.subtract
                                  ).then_inc(mix_freed, 1)

            def queries_lo(pair, g, first, last, gn):
                b = mix_ps[mix_bank(f"QP{pair}", g, first, last)]
                dve.wait_ge(qh_done, gn * 4 + (pair + 1))
                dve.tensor_tensor(q[1][:, 2 * pair:2 * pair + 2, :], halves(b, 2),
                                  q[0][:, 2 * pair:2 * pair + 2, :].bitcast(F32), ALU.subtract).then_inc(mix_freed, 1)

            def early_lo(n):
                src, hi, lo = chunk_split(n)
                dve.wait_ge(chunk_hi_done, n)
                dve.tensor_tensor(lo, src, hi.bitcast(F32), ALU.subtract).then_inc(chunk_split_done[n], 1)

            for t in kz + gw:
                last = dve.memset(t[:].bitcast(F32), 0.0)
            last.then_inc(zeros_done, 1)
            dve.wait_ge(zeros_done, 1)
            dve.wait_ge(ctx_loaded, 16)
            dve.wait_ge(x_in[0], 16)
            for k in range(LN_STEPS):
                norm_step(0, k, 0, 4, 0, 0, None, None)
            norm_apply(0, [ct[:, i, :] for i in range(2)], xn[:, 2:4, :], 0, cnorm_done)
            norm_apply(0, x_tiles(0), xn[:, 0:2, :], 2, xnorm_done)
            dve.wait_ge(cols_filled, 1)
            dve.tensor_copy(cols[:, :, :], bank[0][:, 0:KT * NROW].rearrange("p (k n) -> p k n", k=KT)
                            ).then_inc(cols_done, 1)
            dve.wait_ge(cols_done, 1)
            landed(dve, 0)
            kv = stage[:, 0, 0:KT * P].rearrange("p (k a n) -> p k a n", k=KT, a=2)
            both = [(w, a, slice(DH * h, DH * h + DH)) for w, a in ((wkk, 0), (wv, 1)) for h in range(2)]
            for w, a, r in both:
                last = dve.tensor_copy(w[0][:, :, r], kv[:, :, a, :])
            last.then_inc(kv_hi_done, 1)
            dve.wait_ge(kv_hi_done, 1)
            for w, a, r in both:
                last = dve.tensor_tensor(w[1][:, :, r], kv[:, :, a, :], w[0][:, :, r].bitcast(F32), ALU.subtract)
            last.then_inc(chunk_split_done[0], 1)
            for i, (name, dst, ready) in enumerate((("TXc", cnT, cnT_ready), ("TXx", xnT, xnT_ready))):
                transposed(name, None, False, False, 0)
                dve.wait_ge(tfh_done, i + 1)
                dve.tensor_tensor(dst[1], tf[:, :, :], dst[0].bitcast(F32), ALU.subtract).then_inc(ready, 1)
            early_lo(1)
            keys_values_lo(None, False, False, 0)
            queries_lo(0, None, False, False, 0)
            queries_lo(1, None, False, False, 0)
            early_lo(3)
            gate_cols = cols[:, :, 5 + NE:NROW]
            dve.tensor_copy(gw[0][:, :, 0:NE], gate_cols).then_inc(gw_done, 1)
            dve.wait_ge(gw_done, 1)
            dve.tensor_tensor(gw[1][:, :, 0:NE], gate_cols, gw[0][:, :, 0:NE].bitcast(F32), ALU.subtract
                              ).then_inc(gw_done, 1)

            dve.wait_ge(dbrow_in, 32)
            place = [t[:, 0, (NB - 2) * P:NB * P] for t in xmT]
            for r in (slice(0, 5 + NE), slice(32, 33 + NE)):
                done = dve.tensor_copy(place[0][r, :], all_rows[r, :])
            done.then_inc(bias_split, 1)
            dve.wait_ge(bias_split, 1)
            for r in (slice(0, 5 + NE), slice(32, 33 + NE)):
                done = dve.tensor_tensor(place[1][r, :], all_rows[r, :], place[0][r, :].bitcast(F32), ALU.subtract)
            done.then_inc(bias_split, 1)

            def attended_lo(u):
                dve.wait_ge(oh_done, u + 1)
                v = pv_ps[:, :].rearrange("p (m a n) -> p m a n", m=2, a=2)
                for a in range(2):
                    r = slice(DH * a, DH * a + DH)
                    done = dve.tensor_tensor(oT[1][r, :, :], v[r, :, a, :], oT[0][r, :, :].bitcast(F32), ALU.subtract)
                done.then_inc(o_ready, 1)

            def x1_lo(g, b):
                at = bass.ds(g * GT, GT)
                dve.wait_ge(xmh_done, g + 1)
                return dve.tensor_tensor(xmT[1][:, :, at], halves(b, KT), xmT[0][:, :, at].bitcast(F32), ALU.subtract)

            def iteration(g, first=False, last=False):
                call = g + 1
                lo, hi = 4 if last else 0, 4 if first else 6
                at_step = 0

                def small_step():
                    nonlocal at_step
                    if at_step < LN_STEPS:
                        norm_step(call, at_step, lo, hi, None if last else g + 1, None if last else g + 1,
                                  None if first else g - 1, (xnorm_done, g + 1))
                    at_step += 1

                for s in range(NU + 2):
                    u = g * NU + s
                    if s < NU:
                        dve.wait_ge(scores_filled, u + 1)
                        if not (first and s < 2):
                            dve.wait_ge(exp_done, u - 1)
                        dve.tensor_reduce(nmax[:, s % 2, :], halves(sc_ps[s % 2], 4), AX.X, ALU.max, negate=True
                                          ).then_inc(nmax_done, 1)
                    if s == 0 and not first:
                        residual(g - 1)
                        dve.wait_ge(x1_done, g)
                        if not last:
                            dve.wait_ge(ctx_loaded, g * 16 + 32)
                        small_step()
                    if s > 0:
                        small_step()
                    if s >= 2:
                        attended_lo(u - 2)
                        small_step()
                    if s == 5:
                        if not first:
                            norm_apply(call, x_tiles(g - 1), xn[:, 0:2, :], 4, x1norm_done)
                        if not last:
                            norm_apply(call, [ct[:, i, :] for i in range(2)], xn[:, 2:4, :], 0, cnorm_done)
                    if s == 6 and not last:
                        transposed("TXc", g, first, last, g + 1)
                    if s == 7 and not first:
                        b = mix_ps[mix_bank("GL", g, first, last)]
                        dve.wait_ge(mix_filled, mix_index("GL", g, first, last) + 1)
                        dve.tensor_copy(lgT[:, bass.ds(g * GT - GT, GT)], b[0:NE, 0:GT]).then_inc(mix_freed, 1)
                    if s < NU:
                        dve.wait_ge(exp_done, u + 1)
                        if not (first and s < 2):
                            dve.wait_ge(probs_ready, u - 1)
                        dve.reciprocal(rden[:, s % 2, :], den[:, s % 2, :]).then_inc(rden_done, 1)
                    if s > 1:
                        small_step()
                    if 1 <= s <= NU:
                        dve.wait_ge(pTh_done, u)
                        dve.tensor_tensor(pT[1][:, :], t_ps[:, :], pT[0][:, :].bitcast(F32), ALU.subtract
                                          ).then_inc(pT_ready, 1)
                    if s > 0:
                        small_step()
                    if s < NU:
                        b = mix_ps[mix_bank(f"FF{s}", g, first, last)]
                        dve.wait_ge(tanh_done, u + 1)
                        dve.scalar_tensor_tensor(u1[:, :], th[:, :], 1.0, b[:, GT:2 * GT], ALU.add, ALU.mult
                                                 ).then_inc(u1_done, 1)
                        dve.wait_ge(u1_done, u + 1)
                        if not (first and s == 0):
                            dve.wait_ge(u_ready, u)
                        dve.scalar_tensor_tensor(uf[:, :], b[:, 0:GT], 0.5, u1[:, :], ALU.mult, ALU.mult
                                                 ).then_inc(mix_freed, 1)
                    if s == 5 and not first:
                        x1_lo(g - 1, mix_ps[mix_bank("X1T", g, first, last)]).then_inc(mix_freed, 1)
                    if s == 0:
                        queries_lo(2, g, first, last, g)
                    if s == 2:
                        queries_lo(3, g, first, last, g)
                    if s in (1, 2, 3):
                        small_step()
                    if s == 0 and first:
                        dve.wait_ge(ctx_loaded, 32)
                        dve.wait_ge(x_in[1], 16)
                        small_step()
                    if s == 6 and not last:
                        if not first:
                            dve.wait_ge(rows_stored, g * 16)
                        norm_apply(call, x_tiles(g + 1), xn[:, 0:2, :], 2, xnorm_done)
                    if s == NU - 1 and not last:
                        transposed("TXx", g, first, last, g + 1)
                    if s == NU and not last:
                        keys_values_lo(g, first, last, g + 1)
                if not last:
                    queries_lo(0, g, first, last, g + 1)
                    queries_lo(1, g, first, last, g + 1)

            def residual(g):
                dve.wait_ge(wo_done, g * NU + NU)
                at = xs[:, bass.ds(g * 2, 2), :]
                dve.scalar_tensor_tensor(at, halves(out_ps, 2), gates[:, 0:1], at, ALU.mult, ALU.add
                                         ).then_inc(x1_done, 1)

            dve.wait_ge(gates_done, 1)
            iteration(0, first=True)
            for g in range(2, NG):
                dve.wait_ge(x_in[g], 16)
            with dve.Fori(1, NG - 1) as g:
                iteration(g)
            iteration(NG - 1, last=True)

            links = 0

            def link(ins):
                nonlocal links
                links += 1
                ins.then_inc(link_done, 1)
                dve.wait_ge(link_done, links)

            def hidden_lo(step, parity, n):
                for m in range(KT):
                    dve.wait_ge(hh_done, step * KT + (m + 1))
                    dve.tensor_tensor(hh[:, parity, 1, m, 0:n], hf[:, m, 0:n], hh[:, parity, 0, m, 0:n].bitcast(F32),
                                      ALU.subtract).then_inc(h_ready, 1)

            def add_tiles(use, bank_of, t0, pos):
                dve.wait_ge(dn_filled, use + 1)
                dve.wait_ge(dn_freed, use)
                for i in range(2):
                    t = t0 + i
                    done = dve.scalar_tensor_tensor(
                        xs[:, t, :], dn_ps[bank_of % 4][:, i * D:(i + 1) * D],
                        comb[:, bass.ds(pos, 1), t:t + 1].rearrange("p a n -> p (a n)"), xs[:, t, :],
                        ALU.mult, ALU.add)
                done.then_inc(dn_freed, 1)

            def add_shared(j):
                for half in range(2):
                    add_tiles(USE_DOWN[j] + half, USE_DOWN[j] + half, TPS * j + 2 * half, 0)

            def add_dense(e, parity):
                add_tiles(e + USE_DENSE, USE_DENSE + parity, NTS, e + 1)

            def gate_logits(t0, t1, b, count, filled, copied):
                T, n = slice(t0, t1), t1 - t0
                dve.wait_ge(*filled)
                dve.tensor_copy(lg[:, T, :], b[:, 0:n * NE].rearrange("p (t e) -> p t e", t=n)).then_inc(copied[0], 1)
                dve.wait_ge(*copied)
                link(dve.tensor_reduce(g1[:, T], lg[:, T, :], AX.X, ALU.max))
                dve.tensor_tensor(gb[:, T, :], lg[:, T, :], per_tile(g1, t0, t1), ALU.subtract).then_inc(shifted_done, 1)
                dve.wait_ge(shifted_done, count)

            def per_tile(v, t0, t1):
                return v[:, t0:t1].unsqueeze(2).broadcast_to((P, t1 - t0, NE))

            def gate_first(t0, t1, count):
                T = slice(t0, t1)
                dve.wait_ge(gexp_done, count)
                link(dve.tensor_reduce(g2[:, T], ga[:, T, :], AX.X, ALU.add))
                link(dve.reciprocal(g3[:, T], g2[:, T]))
                link(dve.tensor_tensor(ga[:, T, :], ga[:, T, :], per_tile(g3, t0, t1), ALU.mult))
                link(dve.tensor_reduce(g1[:, T], ga[:, T, :], AX.X, ALU.max))
                link(dve.tensor_tensor(gb[:, T, :], ga[:, T, :], per_tile(g1, t0, t1), ALU.is_equal))
                link(dve.tensor_tensor(gb[:, T, :], gb[:, T, :], rio[:, T, :], ALU.mult))
                link(dve.tensor_reduce(g3[:, T], gb[:, T, :], AX.X, ALU.max))
                link(dve.tensor_tensor(oh1[:, T, :], rio[:, T, :], per_tile(g3, t0, t1), ALU.is_equal))

            def gate_second(t0, t1):
                T = slice(t0, t1)
                link(dve.scalar_tensor_tensor(lg[:, T, :], oh1[:, T, :], -2.0, ga[:, T, :], ALU.mult, ALU.add))
                link(dve.tensor_reduce(g2[:, T], lg[:, T, :], AX.X, ALU.max))
                link(dve.tensor_tensor(gb[:, T, :], lg[:, T, :], per_tile(g2, t0, t1), ALU.is_equal))
                link(dve.tensor_tensor(gb[:, T, :], gb[:, T, :], rio[:, T, :], ALU.mult))
                link(dve.tensor_reduce(g3[:, T], gb[:, T, :], AX.X, ALU.max))
                link(dve.tensor_tensor(lg[:, T, :], rio[:, T, :], per_tile(g3, t0, t1), ALU.is_equal))

            def gate_weights(t0, t1):
                T = slice(t0, t1)
                link(dve.scalar_tensor_tensor(g3[:, T], g1[:, T], 1e-20, g2[:, T], ALU.add, ALU.add))
                link(dve.reciprocal(g3[:, T], g3[:, T]))
                link(dve.tensor_scalar(g3[:, T], g3[:, T], gates[:, 1:2], None, ALU.mult))
                dve.tensor_tensor(g1[:, T], g1[:, T], g3[:, T], ALU.mult)
                link(dve.tensor_tensor(g2[:, T], g2[:, T], g3[:, T], ALU.mult))

            gate_logits(0, NTS, dn_ps[USE_LT], 1, (dn_filled, USE_LT + 1), (dn_freed, USE_LT + 1))
            gate_first(0, NTS, 1)
            hidden_lo(0, 0, ST)
            residual(NG - 1)
            gate_second(0, NTS)
            dve.memset(chosen[:, NTS * NE:].bitcast(F32), 0.0)
            dve.tensor_tensor(chosen[:, 0:NTS * NE].rearrange("p (t e) -> p t e", e=NE), oh1[:, 0:NTS, :],
                              lg[:, 0:NTS, :], ALU.add).then_inc(chosen_done, 1)
            hidden_lo(1, 1, ST)
            link(dve.memset(comb[:, 0, :], 1.0))
            link(dve.tensor_scalar(comb[:, 0, :], comb[:, 0, :], gates[:, 1:2], None, ALU.mult))
            def last_norm(steps):
                for k in steps:
                    norm_step(NG + 1, k, 4, 6, None, None, NG - 1, (x1norm_done, NG - 1))

            last_norm(range(0, 6))
            add_shared(0)

            dve.wait_ge(dn_filled, USE_RANK + 1)
            dve.wait_ge(sort_consts, 3)
            pos = dn_ps[USE_RANK % 4][:, 0:(NTS + 1) * NE].rearrange("p (t e) -> p t e", e=NE)
            a8, b8, c8 = small[:, 0:NE], small[:, NE:2 * NE], small[:, 2 * NE:3 * NE]
            link(dve.tensor_scalar(a8.bitcast(I32), pos[:, NTS, :], P - 1.0, None, ALU.add))
            link(dve.tensor_scalar(b8.bitcast(I32), a8.bitcast(I32), 7, None, ALU.logical_shift_right))
            link(dve.tensor_copy(c8, b8.bitcast(I32)))
            link(dve.tensor_copy(a8, c8))
            ends, other = a8, b8
            for d in (1, 2, 4):
                dve.tensor_copy(other[:, 0:d], ends[:, 0:d])
                link(dve.tensor_tensor(other[:, d:NE], ends[:, d:NE], ends[:, 0:NE - d], ALU.add))
                ends, other = other, ends
            dve.tensor_copy(expert_ends, ends[0:1, :])
            link(dve.tensor_tensor(other, ends, c8, ALU.subtract))
            dve.scalar_tensor_tensor(rank[:, :, :], other.unsqueeze(1).broadcast_to((P, NTS, NE)), float(P),
                                     pos[:, 0:NTS, :], ALU.mult, ALU.add).then_inc(dn_freed, 1)
            dve.wait_ge(dn_freed, USE_RANK + 1)
            dve.tensor_tensor(slots8[:, 0:NTS, :], rank[:, :, :], oh1[:, 0:NTS, :], ALU.mult)
            link(dve.tensor_tensor(slots8[:, NTS:NCH, :], rank[:, :, :], lg[:, 0:NTS, :], ALU.mult))
            fslot, ilo, ihi, flo, fhi = [small[:, 32 + 32 * i:32 + 32 * i + NCH] for i in range(5)]
            link(dve.tensor_reduce(fslot, slots8, AX.X, ALU.add))
            link(dve.tensor_copy(token_slot, fslot))
            dve.tensor_scalar(ilo.bitcast(I32), token_slot, P - 1, None, ALU.bitwise_and)
            link(dve.tensor_scalar(ihi.bitcast(I32), token_slot, 7, None, ALU.logical_shift_right))
            dve.tensor_copy(flo, ilo.bitcast(I32))
            link(dve.tensor_copy(fhi, ihi.bitcast(I32)))

            def hots(w):
                eq = is_tile.rearrange("p (n c) -> p n c", n=WAVE)
                link(dve.tensor_tensor(eq, fhi[:, w * WAVE:(w + 1) * WAVE].unsqueeze(2).broadcast_to((P, WAVE, TCOLS)),
                                       iota_tile[:, 0:TCOLS].unsqueeze(1).broadcast_to((P, WAVE, TCOLS)), ALU.is_equal))
                dve.tensor_tensor(hi_hot[w], eq, token.unsqueeze(2).broadcast_to((P, WAVE, TCOLS)), ALU.mult)
                dve.tensor_tensor(lo_hot[w], flo[:, w * WAVE:(w + 1) * WAVE].unsqueeze(2).broadcast_to((P, WAVE, P)),
                                  iota_lo.unsqueeze(1).broadcast_to((P, WAVE, P)), ALU.is_equal).then_inc(hot_done, 1)

            hots(0)
            dve.wait_ge(dn_filled, USE_DOWN[1] + 2)
            dve.wait_ge(hot_done, 1)
            hots(1)
            hidden_lo(2, 0, ST)
            add_shared(1)
            dve.wait_ge(wave_used, 2)
            dve.tensor_copy(slot_token, bank[3][:, 0:TILES]).then_inc(sorted_done, 1)
            last_norm(range(6, LN_STEPS))
            norm_apply(NG + 1, x_tiles(NG - 1), xn[:, 0:2, :], 4, x1norm_done)
            dve.wait_ge(hot_done, 2)
            link(dve.tensor_tensor(tile_cmp, iota_tile[0:1, :].unsqueeze(2).broadcast_to((1, 40, NE)),
                                   expert_ends.unsqueeze(1).broadcast_to((1, 40, NE)), ALU.is_ge))
            link(dve.tensor_reduce(tile_expert, tile_cmp, AX.X, ALU.add))
            link(dve.tensor_scalar(tile_expert, tile_expert, NE - 1.0, None, ALU.min))
            by_window = tile_expert.rearrange("p (w k) -> p w k", k=WINDOW)
            link(dve.tensor_copy(pack, by_window[:, 0:NWIN, 0]))
            for k in range(1, WINDOW + 2):
                link(dve.scalar_tensor_tensor(pack, by_window[:, k // WINDOW:k // WINDOW + NWIN, k % WINDOW],
                                              float(1 << (SHIFT * k)), pack, ALU.mult, ALU.add))
            dve.tensor_copy(window, pack).then_inc(windows_done, 1)
            x1_lo(NG - 1, bank[2]).then_inc(last_read, 1)

            def last_group(t):
                if t == -1:
                    dve.wait_ge(last_filled, 2)
                    dve.tensor_copy(last_lgT, bank[3][0:NE, 0:GT]).then_inc(last_read, 1)
                    add_shared(2)
                if t == 2:
                    gate_logits(NTS, NB, bank[7][:, D:], 2, (last_filled, 3), (last_read, 3))
                if t == TILES - 5:
                    gate_first(NTS, NB, 2)
                if t == TILES - 4:
                    gate_second(NTS, NB)
                if t == TILES - 3:
                    gate_weights(0, NB)
                if t == TILES - 2:
                    dve.tensor_tensor(oh1[:, NTS:NB, :], oh1[:, NTS:NB, :], per_tile(g1, NTS, NB), ALU.mult)
                    link(dve.tensor_tensor(lg[:, NTS:NB, :], lg[:, NTS:NB, :], per_tile(g2, NTS, NB), ALU.mult))
                    link(dve.tensor_tensor(comb[:, 1:NPOS, NTS:NB].rearrange("p e t -> p t e"), oh1[:, NTS:NB, :],
                                           lg[:, NTS:NB, :], ALU.add))

            def tile_step(t, c, loop):
                if runs(t + 2):
                    dve.wait_ge(xgh_done, t + 3)
                    dve.tensor_tensor(xg[1][:, c % 2], halves(bank[c % 2], 4)[:, 0:2, :], xg[0][:, c % 2].bitcast(F32),
                                      ALU.subtract).then_inc(xg_ready, 1)
                if runs(t - 1):
                    dve.wait_ge(hTh_done, t)
                    dve.tensor_tensor(hsT[1][(c + 1) % 2][:, :, :], halves(bank[4 + (c + 1) % 2], 4)[:, 0:2, :],
                                      hsT[0][(c + 1) % 2][:, :, :].bitcast(F32), ALU.subtract).then_inc(hT_ready, 1)
                if runs(t - 2):
                    dve.wait_ge(tile_down_filled, t - 1)
                    b = (c + 2) % 4
                    if isinstance(t, int):
                        if t >= 6:
                            dve.wait_ge(y_stored[b], 16 * ((t - 2) // 4))
                    else:
                        i, j = loop
                        dve.wait_ge(y_stored[b], i * 16)
                    dve.tensor_copy(ys[:, b, :], bank[6 + c % 2][:, 0:D]).then_inc(y_copied, 1)
                if loop is None:
                    last_group(t)

            tile_loop(dve, tile_step)
            hidden_lo(3, 1, ST)
            hidden_lo(STEPS, 0, GT)
            add_shared(3)

            def add_back(t, c, i=None):
                w = (g1, g2)[c]
                if i is None:
                    dve.wait_ge(back_in[t % 3], 32 * (t // 3 + 1))
                    at, src, w = xs[:, t, :], back(2 * t + c), w[:, t:t + 1]
                    before = 0
                else:
                    dve.wait_ge(back_in[t], i * 32 + 32)
                    at = xs[:, bass.ds(i * 3 + t, 1), :].rearrange("p a n -> p (a n)")
                    src = xmT_t[:, bass.ds(i, 1), (2 * t + c) * D:(2 * t + c + 1) * D].rearrange("p a n -> p (a n)")
                    src, w = src.bitcast(F32), w[:, bass.ds(i * 3 + t, 1)]
                    before = i * 6
                if c == 1:
                    dve.wait_ge(back_added, before + (BACK_ORDER.index((t, 0)) + 1))
                dve.scalar_tensor_tensor(at, src, w, at, ALU.mult, ALU.add).then_inc(back_added, 1)

            hidden_lo(STEPS + 1, 1, GT)
            add_dense(0, 0)
            with dve.Fori(0, NE // 2 - 1) as i:
                for j in range(2):
                    hidden_lo(i * 2 + (STEPS + 2 + j), j, GT)
                    first, second = (((0, 0), (1, 0)), ((0, 1), (1, 1))) if j == 0 else (((2, 0),), ((2, 1),))
                    for t, c in first:
                        add_back(t, c, i)
                    add_dense(i * 2 + (1 + j), (1 + j) % 2)
                    for t, c in second:
                        add_back(t, c, i)
            for t, c in BACK_ORDER[18:22]:
                add_back(t, c)
            add_dense(NE - 1, 1)
            for t, c in BACK_ORDER[22:]:
                add_back(t, c)

        @block.tensor
        def _(pe):
            def matmul3(ps, wts, mov, first, last):
                pe.matmul(ps, wts[1], mov[0], start=first, stop=False, skip_group_check=True)
                pe.matmul(ps, wts[0], mov[0], start=False, stop=False, skip_group_check=True)
                return pe.matmul(ps, wts[0], mov[1], start=False, stop=last, skip_group_check=True)

            def mix(name, g, first, last):
                n = mix_index(name, g, first, last)
                if not (isinstance(n, int) and n < 3):
                    pe.wait_ge(mix_freed, n - 2)
                return mix_ps[mix_bank(name, g, first, last)]

            def transposes(b, tiles):
                for i in range(2):
                    for k in range(KT):
                        done = pe.transpose(b[:, k * GT + i * P:k * GT + (i + 1) * P], tiles[:, i, k * P:(k + 1) * P],
                                            ident[:, :])
                return done

            def norm_T(name, g, first, last, gn):
                b = mix(name, g, first, last)
                isx = name == "TXx"
                pe.wait_ge(xnorm_done if isx else cnorm_done, gn + 1)
                transposes(b, xn[:, 0:2] if isx else xn[:, 2:4]).then_inc(mix_filled, 1)

            def keys(g, first, last, gn):
                b = mix("K", g, first, last)
                pe.wait_ge(cnT_ready, gn + 1)
                for k in range(KT):
                    done = matmul3(b[:, 0:GT], [w[:, k, :] for w in wkk], [t[:, k, :] for t in cnT], k == 0, k == KT - 1)
                done.then_inc(mix_filled, 1)

            def values(g, first, last, gn):
                b = mix("V", g, first, last)
                for i in range(2):
                    for k in range(KT):
                        done = matmul3(b[:, i * GT:(i + 1) * GT], [t[:, k, i * P:(i + 1) * P] for t in cnT],
                                       [w[:, k, :].unsqueeze(1).broadcast_to((P, 2, P)) for w in wv],
                                       k == 0, k == KT - 1)
                done.then_inc(mix_filled, 1)

            def queries(pair, g, first, last, gn):
                b = mix(f"QP{pair}", g, first, last)
                pe.wait_ge(xnT_ready, gn + 1)
                for i in range(2):
                    m = 2 * pair + i
                    for k in range(KT):
                        done = matmul3(b[:, i * GT:(i + 1) * GT], [w[:, k, m * P:(m + 1) * P] for w in wq],
                                       [t[:, k, :] for t in xnT], k == 0, k == KT - 1)
                done.then_inc(mix_filled, 1)

            def logits(b, g):
                for k in range(KT):
                    done = matmul3(b[:, 0:GT], [w[:, k, :] for w in gw],
                                   [t[:, k, bass.ds(g * GT, GT)] for t in xmT], k == 0, k == KT - 1)
                return done

            def attend(u, s, very_first):
                pe.wait_ge(pT_ready, u + 1)
                if not very_first:
                    pe.wait_ge(o_ready, u)
                matmul3(pv_ps[:, :], [t[:, s % 2, :] for t in vv], [t[:, :] for t in pT], True, True
                        ).then_inc(pv_filled, 1)

            def project(u, s, last_of_group):
                pe.wait_ge(o_ready, u + 1)
                b = s % 2
                for m in range(2):
                    done = matmul3(out_ps[:, b * D:(b + 1) * D], [t[:, m, :] for t in oT],
                                   [w[:, 2 * (s // 2) + m, :] for w in wo], False, last_of_group)
                done.then_inc(wo_done, 1)

            def iteration(g, first=False, last=False):
                def chunk(n):
                    if first:
                        split(pe, n)

                for s in range(NU + 2):
                    u = g * NU + s
                    if s < NU:
                        if not (first and s < 2):
                            pe.wait_ge(exp_done, u - 1)
                        if s in (0, 2):
                            name = f"QP{s // 2}"
                            n = mix_index(name, None, False, False) if first else mix_index(name, g - 1, False, False)
                            pe.wait_ge(mix_freed, n + 1)
                        if s in (4, 6):
                            pe.wait_ge(mix_freed, mix_index(f"QP{s // 2}", g, first, last) + 1)
                        for i in range(2):
                            m = 2 * (s // 2) + i
                            done = matmul3(sc_ps[s % 2][:, i * GT:(i + 1) * GT],
                                           [t[:, m, (s % 2) * P:(s % 2 + 1) * P] for t in q],
                                           [t[:, s % 2, :, :] for t in kz], True, True)
                        done.then_inc(scores_filled, 1)
                    if s == 6 and not last:
                        norm_T("TXc", g, first, last, g + 1)
                    if s == 7 and not first:
                        b = mix("GL", g, first, last)
                        pe.wait_ge(gw_done, 2)
                        pe.wait_ge(mix_freed, mix_index("X1T", g, first, last) + 1)
                        logits(b, g - 1).then_inc(mix_filled, 1)
                    if s < NU:
                        b = mix(f"FF{s}", g, first, last)
                        chunk([3, 6, 7, 10][s // 2])
                        for i in range(2):
                            if i == 1 and s >= 2:
                                attend(u - 2, s, first and s == 2)
                            for k in range(KT):
                                at = slice(i * FF + s * P, i * FF + (s + 1) * P)
                                done = matmul3(b[:, i * GT:(i + 1) * GT], [w[:, k, at] for w in wf1],
                                               [t[:, k, :] for t in xnT], k == 0, k == KT - 1)
                        done.then_inc(mix_filled, 1)
                    if s == 0:
                        queries(2, g, first, last, g)
                    if s == 2:
                        queries(3, g, first, last, g)
                    if s == NU - 1 and not last:
                        norm_T("TXx", g, first, last, g + 1)
                    if s == NU and not last:
                        keys(g, first, last, g + 1)
                    if s == NU:
                        attend(u - 2, s, False)
                    if 1 <= s <= NU:
                        pe.wait_ge(probs_ready, u)
                        if not (first and s == 1):
                            pe.wait_ge(pT_ready, u - 1)
                        for h in range(4):
                            done = pe.transpose(t_ps[:, h * P:(h + 1) * P], pr[:, (s - 1) % 2, h, :], ident[:, :])
                        done.then_inc(pT_filled, 1)
                    if s == NU and not last:
                        values(g, first, last, g + 1)
                    if 1 <= s <= NU:
                        pe.wait_ge(u_ready, u)
                        chunk([4, 8][(s - 1) // 4])
                        if s == 1 and not first:
                            pe.wait_ge(x1_done, g)
                        for b in range(2):
                            done = matmul3(out_ps[:, b * D:(b + 1) * D],
                                           [t[:, (s - 1) % 2, b * P:(b + 1) * P] for t in uT],
                                           [w[:, s - 1, :] for w in wf2], s == 1 and b == 0, False)
                        done.then_inc(ff2_done, 1)
                    if 2 <= s <= NU:
                        chunk([5, 9][(s - 2) // 4])
                        project(u - 2, s - 2, False)
                    if s == 5 and not first:
                        b = mix("X1T", g, first, last)
                        pe.wait_ge(x1norm_done, g)
                        transposes(b, xn[:, 0:2]).then_inc(mix_filled, 1)
                attend(g * NU + (NU - 1), NU - 1, False)
                if last:
                    return
                queries(0, g, first, last, g + 1)
                queries(1, g, first, last, g + 1)
                project(g * NU + (NU - 1), NU - 1, True)

            pe.wait_ge(ident_done, 2)
            pe.wait_ge(rows_in, 16 * 7)
            for k in range(KT):
                done = pe.transpose(bank[0][:, k * NROW:(k + 1) * NROW], rows[:, k * P:(k + 1) * P],
                                    ident[0:NROW, 0:NROW])
            done.then_inc(cols_filled, 1)
            pe.wait_ge(zeros_done, 1)
            norm_T("TXc", None, False, False, 0)
            norm_T("TXx", None, False, False, 0)
            split(pe, 0)
            keys(None, False, False, 0)
            values(None, False, False, 0)
            split(pe, 1)
            split(pe, 2)
            queries(0, None, False, False, 0)
            queries(1, None, False, False, 0)
            iteration(0, first=True)
            with pe.Fori(1, NG - 1) as g:
                iteration(g)
            iteration(NG - 1, last=True)

            def down_bank(use, parity=None):
                if parity is not None:
                    pe.wait_ge(dn_freed, use - 1)
                    return dn_ps[(USE_DENSE + parity) % 4]
                if use >= 4:
                    pe.wait_ge(dn_freed, use - 3)
                return dn_ps[use % 4]

            def add_bias(b, row):
                pe.matmul(b, ones, shared_brow if row is None else brow[:, bass.ds(row, D)], start=True, stop=False,
                          skip_group_check=True)

            def up(step, parity, w, tokens, n):
                for m in range(KT):
                    if not (isinstance(step, int) and step < 2):
                        pe.wait_ge(silu_done, step * KT + (m - 2 * KT + 1))
                    for k in range(KT):
                        done = matmul3(up_ps[2 * parity + m][:, 0:n], [w(a, k, m * P, P) for a in range(2)],
                                       [t[:, k, tokens:tokens + n] for t in xmT], k == 0, k == KT - 1)
                    done.then_inc(up_filled, 1)

            def down(step, parity, w, bias_row, b, pair):
                for i in range(2):
                    t = 2 * pair + i
                    add_bias(b[:, i * D:(i + 1) * D], bias_row)
                    for k in range(KT):
                        done = matmul3(b[:, i * D:(i + 1) * D], [hh[:, parity, a, k, t * P:(t + 1) * P] for a in range(2)],
                                       [w(2 + a, k, 0, D) for a in range(2)], False, k == KT - 1)
                done.then_inc(dn_filled, 1)

            def shared_w(m, k, at, n):
                return shared[:, m, k, at:at + n]

            def expert_w(e):
                def w(m, k, at, n):
                    first = e * 2048 + ((m * KT + k) * HID + at)
                    return experts[:, first:first + n] if isinstance(e, int) else experts[:, bass.ds(first, n)]
                return w

            def shared_up(j):
                up(j, j % 2, shared_w, j * ST, ST)

            def shared_down(j):
                pe.wait_ge(h_ready, KT * j + KT)
                for pair in range(2):
                    down(j, j % 2, shared_w, None, down_bank(USE_DOWN[j] + pair), pair)

            def dense_up(e, parity):
                up(e + STEPS, parity, expert_w(e), NTS * P, GT)

            def dense_down(e, parity):
                pe.wait_ge(h_ready, e * KT + (STEPS * KT + KT))
                down(e + STEPS, parity, expert_w(e), e * D + NE * D, down_bank(e + USE_DENSE, parity), 0)

            pe.wait_ge(mix_freed, len(MIX_PRO) + len(MIX_FIRST) + (NG - 2) * len(MIX_MID) + len(MIX_LAST))
            b = down_bank(USE_LT)
            for t in range(NTS):
                done = pe.transpose(b[:, t * NE:(t + 1) * NE], lgT[:, t * P:(t + 1) * P], ident[0:NE, 0:NE])
            done.then_inc(dn_filled, 1)
            split(pe, NCA)
            pe.wait_ge(exp_done, NG * NU)
            shared_up(0)
            project(NG * NU - 1, NU - 1, True)
            pe.wait_ge(pT_ready, NG * NU)
            shared_up(1)
            pe.wait_ge(shared_brow_in, 32)
            pe.wait_ge(sort_consts, 3)
            shared_down(0)
            b = down_bank(USE_RANK)
            pe.wait_ge(x1_done, NG)
            n = (NTS + 1) * NE
            pe.wait_ge(sort_consts, 3)
            pe.wait_ge(chosen_done, 1)
            pe.matmul(b[:, 0:n], before, chosen, start=True, stop=False, skip_group_check=True)
            for d in range(1, NTS + 1):
                done = pe.matmul(b[:, d * NE:n], ones, chosen[:, 0:n - d * NE], start=False, stop=d == NTS,
                                 skip_group_check=True)
            done.then_inc(dn_filled, 1)
            shared_up(2)
            shared_down(1)

            def slot_tokens(b, w):
                pe.wait_ge(hot_done, w + 1)
                for n in range(WAVE):
                    done = pe.matmul(b[:, 0:TCOLS], lo_hot[w][:, n, :], hi_hot[w][:, n, :], start=w + n == 0,
                                     stop=w == 1 and n == WAVE - 1, skip_group_check=True)
                return done

            ids = bank[3]
            pe.wait_ge(silu_done, 2 * KT)
            slot_tokens(ids, 0).then_inc(wave_used, 1)
            slot_tokens(ids, 1).then_inc(wave_used, 1)
            shared_down(2)
            pe.wait_ge(x1norm_done, NG)
            transposes(bank[2], xn[:, 0:2]).then_inc(last_filled, 1)

            experts_of = None

            def tile_step(t, c, loop):
                nonlocal experts_of
                k = loop[1] if loop else t - 2 if t < 2 else (t - 2) % WINDOW
                if loop is None and t == 0:
                    for n in range(NE):
                        split(pe, NCA + 1 + n)
                    pe.wait_ge(brow_in, 32)
                    pe.wait_ge(windows_done, 1)
                if t == 0 if loop is None and t < WINDOW else k == 0:
                    w = loop[0] if loop else max(t - 2, 0) // WINDOW
                    experts_of = pe.value_load(window[0:1, bass.ds(w, 1)])
                if runs(t):
                    e = pe.snap((experts_of >> (SHIFT * (k + 2))) & (NE - 1))
                    b = bank[2 + c % 2][:, 0:HID]
                    pe.wait_ge(xg_ready, t + 1)
                    if loop is None and t in (0, 1):
                        pe.wait_ge(last_read, t + 1)
                    add_bias(b, e * D)
                    for kt in range(KT):
                        done = matmul3(b, [x[:, c % 2, kt, :] for x in xg], [expert_w(e)(a, kt, 0, HID) for a in range(2)],
                                       False, kt == KT - 1)
                    done.then_inc(tile_up_filled, 1)
                if runs(t + 2):
                    g = (c + 2) % 4
                    pe.wait_ge(gathered[g], loop[0] * 16 + 32 if loop else 16 * ((t + 2) // 4 + 1))
                    b = bank[c % 2]
                    for kt in range(KT):
                        done = pe.transpose(b[:, kt * P:(kt + 1) * P], rows_g[:, g, kt * P:(kt + 1) * P], ident[:, :])
                    done.then_inc(gT_filled, 1)
                if runs(t - 1):
                    pe.wait_ge(tile_silu_done, t)
                    if loop is None and t == 1:
                        pe.wait_ge(dn_freed, USE_DOWN[2] + 2)
                    b = bank[4 + (c + 1) % 2]
                    for kt in range(KT):
                        done = pe.transpose(b[:, kt * P:(kt + 1) * P], hs[:, (c + 1) % 2, kt * P:(kt + 1) * P], ident[:, :])
                    done.then_inc(hT_filled, 1)
                if loop is None and t == -1:
                    pe.wait_ge(sorted_done, 1)
                    pe.wait_ge(last_read, 1)
                    logits(bank[3], NG - 1).then_inc(last_filled, 1)
                if loop is None and t == 2:
                    for i in range(2):
                        done = pe.transpose(bank[7][:, D + i * NE:D + (i + 1) * NE], last_lgT[:, i * P:(i + 1) * P],
                                            ident[0:NE, 0:NE])
                    done.then_inc(last_filled, 1)
                if runs(t - 2):
                    e = pe.snap((experts_of >> (SHIFT * k)) & (NE - 1))
                    b = bank[6 + c % 2][:, 0:D]
                    pe.wait_ge(hT_ready, t - 1)
                    if loop is None and t == 3:
                        pe.wait_ge(last_read, 3)
                    if not (isinstance(t, int) and t < 4):
                        pe.wait_ge(y_copied, t - 3)
                    add_bias(b, e * D + NE * D)
                    for kt in range(KT):
                        done = matmul3(b, [x[c % 2][:, kt, :] for x in hsT],
                                       [expert_w(e)(2 + a, kt, 0, D) for a in range(2)], False, kt == KT - 1)
                    done.then_inc(tile_down_filled, 1)

            tile_loop(pe, tile_step)
            shared_up(3)
            dense_up(0, 0)
            pe.wait_ge(y_copied, TILES)
            shared_down(3)
            dense_up(1, 1)
            dense_down(0, 0)
            for e in range(2, NE):
                dense_up(e, e % 2)
                dense_down(e - 1, (e - 1) % 2)
            dense_down(NE - 1, 1)


_INS = ["x", "ctx_1024", "g_xattn", "g_ffn", "L0_xattn_ln_g", "L0_xattn_ln_b", "L0_xattn_cln_g", "L0_xattn_cln_b",
        "L0_xattn_Wq", "L0_xattn_Wkv", "L0_xattn_Wo", "L0_xattn_Wff1", "L0_xattn_Wff2", "L0_ffn_gate_w",
        "L0_ffn_up_w", "L0_ffn_up_b", "L0_ffn_down_w", "L0_ffn_down_b", "L0_ffn_sh_up_w", "L0_ffn_sh_up_b",
        "L0_ffn_sh_down_w", "L0_ffn_sh_down_b"]


def kernel(**inputs):
    import concourse.bacc as bacc
    from concourse.bass_utils import run_bass_kernel_spmd

    nc = bacc.Bacc("TRN2", target_bir_lowering=False, num_devices=1)
    arrays, args = {}, []
    for name in _INS:
        a = np.ascontiguousarray(inputs[name])
        arrays[f"in_{name}"] = a
        args.append(nc.dram_tensor(f"in_{name}", a.shape, mybir.dt.from_np(a.dtype), kind="ExternalInput").ap())
    args.append(nc.dram_tensor("out_x", (NB, P, D), F32, kind="ExternalOutput").ap())
    program(nc, *args)
    r = run_bass_kernel_spmd(nc, [arrays], core_ids=[0])
    return r.results[0]["out_x"]
```
